# Optimizing a Trainium2 kernel written in Bass

```python
import numpy as np
import jax
import jax.numpy as jnp

def _softmax(x, axis=-1):
    return jax.nn.softmax(x, axis=axis)

def _gelu(x):
    return jax.nn.gelu(x, approximate=True)

def _silu(x):
    return jax.nn.silu(x)

def _sigmoid(x):
    return jax.nn.sigmoid(x)

def _layernorm(x, axis=-1, eps=1e-05):
    m = jnp.mean(x, axis=axis, keepdims=True)
    v = jnp.var(x, axis=axis, keepdims=True)
    return (x - m) / jnp.sqrt(v + eps)

def _scatter_add(tgt, idx, src, axis=0):
    return tgt.at[idx].add(src)

def _segment_sum(src, seg, n):
    return jax.ops.segment_sum(src, seg, n)
kernel_name = 'mk_seq_preln_d2_jaxref_r8_32ae03'

def setup_inputs(seed: int=0):
    np.random.seed(seed)
    _w = jnp.asarray

    def _L0_attn_setup():
        import jax, jax.numpy as jnp
        import numpy as np
        B, T, FEATS, HEAD = (2, 256, 256, 16)
        DIM_HEAD = FEATS // HEAD
        EPS = float(jnp.finfo(jnp.float32).eps)

        def _rms_norm(u, g):
            return u * jax.lax.rsqrt(jnp.mean(u * u, axis=-1, keepdims=True) + EPS) * g
        key = jax.random.key(seed)
        kx, kw = jax.random.split(key)
        x = jax.random.normal(kx, (B, T, FEATS), dtype=jnp.float32)
        W = jax.random.normal(kw, (FEATS, FEATS), dtype=jnp.float32) / np.sqrt(FEATS)
        g1 = jnp.ones((DIM_HEAD,), dtype=jnp.float32)
        g2 = jnp.ones((DIM_HEAD,), dtype=jnp.float32)
        g3 = jnp.ones((DIM_HEAD,), dtype=jnp.float32)
        return {'x': x, 'W': W, 'g1': g1, 'g2': g2, 'g3': g3}
    _L0_attn_in = _L0_attn_setup()

    def _L0_ffn_setup():
        import jax, jax.numpy as jnp
        import numpy as np
        B, S, D = (2, 512, 256)
        H = 512
        HS = H // 2
        E = 4
        TOPK = 2
        SCALE = 0.02

        def _swiglu(xt, wu, wg, wd):
            return jax.nn.silu(xt @ wu.T) * (xt @ wg.T) @ wd.T
        key = jax.random.key(seed)
        ks = jax.random.split(key, 8)
        return {'x': jax.random.normal(ks[0], (B, S, D), dtype=jnp.float32), 'gate_w': jax.random.normal(ks[1], (E, D), dtype=jnp.float32) * SCALE, 'w1': jax.random.normal(ks[2], (E, H, D), dtype=jnp.float32) * SCALE, 'w3': jax.random.normal(ks[3], (E, H, D), dtype=jnp.float32) * SCALE, 'w2': jax.random.normal(ks[4], (E, D, H), dtype=jnp.float32) * SCALE, 'sw1': jax.random.normal(ks[5], (HS, D), dtype=jnp.float32) * SCALE, 'sw3': jax.random.normal(ks[6], (HS, D), dtype=jnp.float32) * SCALE, 'sw2': jax.random.normal(ks[7], (D, HS), dtype=jnp.float32) * SCALE}
    _L0_ffn_in = _L0_ffn_setup()

    def _L1_attn_setup():
        import jax, jax.numpy as jnp
        import numpy as np
        B, T, D = (4, 512, 256)
        LAYER_ID, N_LAYERS = (0, 12)
        LN_EPS = 1e-05

        def _wkv(w, u, k, v):
            Bb, Tt, Dd = k.shape
            neg_ew = -jnp.exp(w)

            def step(carry, kv):
                aa, bb, pp = carry
                kt, vt = kv
                qt = jnp.maximum(pp, kt + u)
                e1 = jnp.exp(pp - qt)
                e2 = jnp.exp(kt + u - qt)
                out = (e1 * aa + e2 * vt) / (e1 * bb + e2)
                pp_new = jnp.maximum(pp + neg_ew, kt)
                f1 = jnp.exp(pp - pp_new)
                f2 = jnp.exp(kt - pp_new)
                return ((f1 * aa + f2 * vt, f1 * bb + f2, pp_new), out)
            init = (jnp.zeros((Bb, Dd), k.dtype), jnp.zeros((Bb, Dd), k.dtype), jnp.full((Bb, Dd), -1e+38, k.dtype))
            kT = jnp.swapaxes(k, 0, 1)
            vT = jnp.swapaxes(v, 0, 1)
            _, outT = jax.lax.scan(step, init, (kT, vT))
            return jnp.swapaxes(outT, 0, 1)
        key = jax.random.key(seed)
        ks = jax.random.split(key, 9)
        s = 0.02
        x = jax.random.normal(ks[0], (B, T, D), jnp.float32)
        Wk = jax.random.normal(ks[1], (D, D), jnp.float32) * s
        Wv = jax.random.normal(ks[2], (D, D), jnp.float32) * s
        Wr = jax.random.normal(ks[3], (D, D), jnp.float32) * s
        Wo = jax.random.normal(ks[4], (D, D), jnp.float32) * s
        tm_k = jax.random.uniform(ks[5], (1, 1, D), jnp.float32)
        tm_v = jax.random.uniform(ks[6], (1, 1, D), jnp.float32)
        tm_r = jax.random.uniform(ks[7], (1, 1, D), jnp.float32)
        ratio_0_to_1 = LAYER_ID / max(N_LAYERS - 1, 1)
        ratio_1_to_almost_0 = 1.0 - LAYER_ID / N_LAYERS
        i = jnp.arange(D, dtype=jnp.float32)
        time_decay = -5.0 + 8.0 * (i / (D - 1)) ** (0.7 + 1.3 * ratio_0_to_1)
        zigzag = (jnp.arange(D) % 3 - 1).astype(jnp.float32) * ratio_1_to_almost_0
        time_first = jnp.full((D,), jnp.log(jnp.float32(0.3))) + zigzag
        ln_g = jnp.ones((D,), jnp.float32)
        ln_b = jnp.zeros((D,), jnp.float32)
        return {'x': x, 'Wk': Wk, 'Wv': Wv, 'Wr': Wr, 'Wo': Wo, 'tm_k': tm_k, 'tm_v': tm_v, 'tm_r': tm_r, 'time_decay': time_decay, 'time_first': time_first, 'ln_g': ln_g, 'ln_b': ln_b}
    _L1_attn_in = _L1_attn_setup()

    def _L1_ffn_setup():
        import jax, jax.numpy as jnp
        import numpy as np
        NUM_EXPERTS = 8
        TOP_K = 2
        key = jax.random.key(seed)
        ks = jax.random.split(key, 7)
        B, S, H, I, E = (4, 256, 256, 256, NUM_EXPERTS)
        sc = 0.02
        return {'hidden_states': jax.random.normal(ks[0], (B, S, H), dtype=jnp.float32), 'gate_w': jax.random.normal(ks[1], (E, H), dtype=jnp.float32) * sc, 'gate_b': jax.random.normal(ks[2], (E,), dtype=jnp.float32) * sc, 'w1': jax.random.normal(ks[3], (E, 2 * I, H), dtype=jnp.float32) * sc, 'b1': jax.random.normal(ks[4], (E, 2 * I), dtype=jnp.float32) * sc, 'w2': jax.random.normal(ks[5], (E, H, I), dtype=jnp.float32) * sc, 'b2': jax.random.normal(ks[6], (E, H), dtype=jnp.float32) * sc}
    _L1_ffn_in = _L1_ffn_setup()
    _d = {'L0_attn_x': _L0_attn_in['x'], 'L0_attn_W': _L0_attn_in['W'], 'L0_attn_g1': _L0_attn_in['g1'], 'L0_attn_g2': _L0_attn_in['g2'], 'L0_attn_g3': _L0_attn_in['g3'], 'L0_ffn_gate_w': _L0_ffn_in['gate_w'], 'L0_ffn_w1': _L0_ffn_in['w1'], 'L0_ffn_w3': _L0_ffn_in['w3'], 'L0_ffn_w2': _L0_ffn_in['w2'], 'L0_ffn_sw1': _L0_ffn_in['sw1'], 'L0_ffn_sw3': _L0_ffn_in['sw3'], 'L0_ffn_sw2': _L0_ffn_in['sw2'], 'L1_attn_Wk': _L1_attn_in['Wk'], 'L1_attn_Wv': _L1_attn_in['Wv'], 'L1_attn_Wr': _L1_attn_in['Wr'], 'L1_attn_Wo': _L1_attn_in['Wo'], 'L1_attn_tm_k': _L1_attn_in['tm_k'], 'L1_attn_tm_v': _L1_attn_in['tm_v'], 'L1_attn_tm_r': _L1_attn_in['tm_r'], 'L1_attn_time_decay': _L1_attn_in['time_decay'], 'L1_attn_time_first': _L1_attn_in['time_first'], 'L1_attn_ln_g': _L1_attn_in['ln_g'], 'L1_attn_ln_b': _L1_attn_in['ln_b'], 'L1_ffn_gate_w': _L1_ffn_in['gate_w'], 'L1_ffn_gate_b': _L1_ffn_in['gate_b'], 'L1_ffn_w1': _L1_ffn_in['w1'], 'L1_ffn_b1': _L1_ffn_in['b1'], 'L1_ffn_w2': _L1_ffn_in['w2'], 'L1_ffn_b2': _L1_ffn_in['b2']}
    _x0 = _d['L0_attn_x']
    _d['L0_attn_x'] = jax.random.normal(jax.random.fold_in(jax.random.key(seed), 1), (8, 256, 256), dtype=_x0.dtype)
    del _x0
    return _d

def reference(L0_attn_x, L0_attn_W, L0_attn_g1, L0_attn_g2, L0_attn_g3, L0_ffn_gate_w, L0_ffn_w1, L0_ffn_w3, L0_ffn_w2, L0_ffn_sw1, L0_ffn_sw3, L0_ffn_sw2, L1_attn_Wk, L1_attn_Wv, L1_attn_Wr, L1_attn_Wo, L1_attn_tm_k, L1_attn_tm_v, L1_attn_tm_r, L1_attn_time_decay, L1_attn_time_first, L1_attn_ln_g, L1_attn_ln_b, L1_ffn_gate_w, L1_ffn_gate_b, L1_ffn_w1, L1_ffn_b1, L1_ffn_w2, L1_ffn_b2):

    def _L0_attn_ref(x, W, g1, g2, g3):
        import jax, jax.numpy as jnp
        import numpy as np
        B, T, FEATS, HEAD = (2, 256, 256, 16)
        DIM_HEAD = FEATS // HEAD
        EPS = float(jnp.finfo(jnp.float32).eps)

        def _rms_norm(u, g):
            return u * jax.lax.rsqrt(jnp.mean(u * u, axis=-1, keepdims=True) + EPS) * g
        Bb, Tt, C = x.shape
        sqrt_d = jnp.asarray(DIM_HEAD ** 0.5, dtype=x.dtype)
        w = (x @ W.T).reshape(Bb, Tt, HEAD, DIM_HEAD).transpose(0, 2, 1, 3)
        q = _rms_norm(w, g1)
        k = _rms_norm(w, g2)
        v = _rms_norm(w, g3)
        att = jnp.einsum('bhid,bhjd->bhij', q, k) / sqrt_d
        score = jax.nn.softmax(att, axis=-1) + jax.nn.softmax(att, axis=-2)
        y = jnp.einsum('bhij,bhjd->bihd', score, v).reshape(Bb, Tt, C)
        return y @ W

    def _L0_ffn_ref(x, gate_w, w1, w3, w2, sw1, sw3, sw2):
        import jax, jax.numpy as jnp
        import numpy as np
        B, S, D = (2, 512, 256)
        H = 512
        HS = H // 2
        E = 4
        TOPK = 2
        SCALE = 0.02

        def _swiglu(xt, wu, wg, wd):
            return jax.nn.silu(xt @ wu.T) * (xt @ wg.T) @ wd.T
        orig_shape = x.shape
        xt = x.reshape(-1, orig_shape[-1])
        T = xt.shape[0]
        logits = xt @ gate_w.T
        probs = jax.nn.softmax(logits, axis=-1)
        topk_weight, topk_idx = jax.lax.top_k(probs, TOPK)
        rows = jnp.arange(T)[:, None]
        combine = jnp.zeros((T, E), dtype=x.dtype).at[rows, topk_idx].add(topk_weight)
        y = jnp.zeros_like(xt)
        for e in range(E):
            y = y + combine[:, e:e + 1] * _swiglu(xt, w1[e], w3[e], w2[e])
        y = y + _swiglu(xt, sw1, sw3, sw2)
        return y.reshape(orig_shape)

    def _L1_attn_ref(x, Wk, Wv, Wr, Wo, tm_k, tm_v, tm_r, time_decay, time_first, ln_g, ln_b):
        import jax, jax.numpy as jnp
        import numpy as np
        B, T, D = (4, 512, 256)
        LAYER_ID, N_LAYERS = (0, 12)
        LN_EPS = 1e-05

        def _wkv(w, u, k, v):
            Bb, Tt, Dd = k.shape
            neg_ew = -jnp.exp(w)

            def step(carry, kv):
                aa, bb, pp = carry
                kt, vt = kv
                qt = jnp.maximum(pp, kt + u)
                e1 = jnp.exp(pp - qt)
                e2 = jnp.exp(kt + u - qt)
                out = (e1 * aa + e2 * vt) / (e1 * bb + e2)
                pp_new = jnp.maximum(pp + neg_ew, kt)
                f1 = jnp.exp(pp - pp_new)
                f2 = jnp.exp(kt - pp_new)
                return ((f1 * aa + f2 * vt, f1 * bb + f2, pp_new), out)
            init = (jnp.zeros((Bb, Dd), k.dtype), jnp.zeros((Bb, Dd), k.dtype), jnp.full((Bb, Dd), -1e+38, k.dtype))
            kT = jnp.swapaxes(k, 0, 1)
            vT = jnp.swapaxes(v, 0, 1)
            _, outT = jax.lax.scan(step, init, (kT, vT))
            return jnp.swapaxes(outT, 0, 1)
        xs = jnp.pad(x, ((0, 0), (1, 0), (0, 0)))[:, :-1, :]
        xk = x * tm_k + xs * (1.0 - tm_k)
        xv = x * tm_v + xs * (1.0 - tm_v)
        xr = x * tm_r + xs * (1.0 - tm_r)
        k = jnp.einsum('btd,ed->bte', xk, Wk)
        v = jnp.einsum('btd,ed->bte', xv, Wv)
        r = jax.nn.sigmoid(jnp.einsum('btd,ed->bte', xr, Wr))
        wkv = _wkv(time_decay, time_first, k, v)
        mu = jnp.mean(wkv, axis=-1, keepdims=True)
        var = jnp.mean(jnp.square(wkv - mu), axis=-1, keepdims=True)
        ln = (wkv - mu) * jax.lax.rsqrt(var + LN_EPS) * ln_g + ln_b
        rwkv = r * ln
        return jnp.einsum('btd,ed->bte', rwkv, Wo)

    def _L1_ffn_ref(hidden_states, gate_w, gate_b, w1, b1, w2, b2):
        import jax, jax.numpy as jnp
        import numpy as np
        NUM_EXPERTS = 8
        TOP_K = 2
        B, S, H = hidden_states.shape
        x = hidden_states.reshape(-1, H)
        logits = x @ gate_w.T + gate_b
        top_vals, top_idx = jax.lax.top_k(logits, TOP_K)
        routing = jax.nn.softmax(top_vals.astype(jnp.float32), axis=-1).astype(x.dtype)
        out = jnp.zeros_like(x)
        E = w1.shape[0]
        for e in range(E):
            h = x @ w1[e].T + b1[e]
            x_glu = h[:, 0::2]
            x_lin = h[:, 1::2]
            y = x_glu * jax.nn.sigmoid(1.702 * x_glu) * (x_lin + 1.0)
            ye = y @ w2[e].T + b2[e]
            we = jnp.sum(routing * (top_idx == e), axis=-1)
            out = out + ye * we[:, None]
        return out.reshape(B, S, H)
    x = L0_attn_x
    x = x + _L0_attn_ref(_layernorm(x, axis=-1), L0_attn_W, L0_attn_g1, L0_attn_g2, L0_attn_g3)
    x = x + _L0_ffn_ref(_layernorm(x, axis=-1), L0_ffn_gate_w, L0_ffn_w1, L0_ffn_w3, L0_ffn_w2, L0_ffn_sw1, L0_ffn_sw3, L0_ffn_sw2)
    x = x + _L1_attn_ref(_layernorm(x, axis=-1), L1_attn_Wk, L1_attn_Wv, L1_attn_Wr, L1_attn_Wo, L1_attn_tm_k, L1_attn_tm_v, L1_attn_tm_r, L1_attn_time_decay, L1_attn_time_first, L1_attn_ln_g, L1_attn_ln_b)
    x = x + _L1_ffn_ref(_layernorm(x, axis=-1), L1_ffn_gate_w, L1_ffn_gate_b, L1_ffn_w1, L1_ffn_b1, L1_ffn_w2, L1_ffn_b2)
    return x

_drawn_inputs = setup_inputs


def setup_inputs(seed=0):
    import zlib

    import numpy as np

    out = dict(_drawn_inputs(seed))
    spreads = {'L0_attn_g1': (1.0, 0.2),
     'L0_attn_g2': (1.0, 0.2),
     'L0_attn_g3': (1.0, 0.2),
     'L1_attn_ln_g': (1.0, 0.6),
     'L1_attn_ln_b': (0.0, 0.8)}
    factors = {'L0_ffn_gate_w': 8.0,
     'L0_ffn_w1': 8.0,
     'L0_ffn_w3': 8.0,
     'L0_ffn_w2': 8.0,
     'L0_ffn_sw1': 6.039,
     'L0_ffn_sw3': 5.949,
     'L0_ffn_sw2': 6.0,
     'L1_attn_Wk': 2.711,
     'L1_attn_Wr': 4.589,
     'L1_attn_tm_k': 8.0,
     'L1_attn_tm_v': 5.875,
     'L1_attn_tm_r': 8.0,
     'L1_attn_time_decay': 8.0,
     'L1_attn_time_first': 8.0,
     'L1_ffn_gate_w': 2.669,
     'L1_ffn_gate_b': 8.0,
     'L1_ffn_b1': 8.0,
     'L1_ffn_b2': 7.046}
    for name, (base, spread) in spreads.items():
        noise = np.random.default_rng([zlib.crc32(name.encode()), seed]).standard_normal(out[name].shape)
        drawn = base * np.exp(spread * noise) if base else spread * noise
        out[name] = jnp.asarray(drawn.astype(out[name].dtype))
    for name, factor in factors.items():
        out[name] = (out[name] * factor).astype(out[name].dtype)
    return out
```

```python
from contextlib import ExitStack, contextmanager

import numpy as np

import concourse.bass as bass
from concourse import mybir

ALU = mybir.AluOpType
ACT = mybir.ActivationFunctionType
F32 = mybir.dt.float32
F32R = mybir.dt.float32r
AX_X = mybir.AxisListType.X

P = 128
B, T, D = 8, 256, 256
TOK = B * T
NT = TOK // P
KB = D // P
S = T // P
NH, DH = 16, 16
NP = NH // 2
LN_EPS = 1e-5
RMS_EPS = 1.1920928955078125e-07


def f32(ap):
    return ap.bitcast(F32)


def at_least(eng, semaphore, value):
    if not (isinstance(value, int) and value <= 0):
        eng.wait_ge(semaphore, value)


def upto(value, most):
    return min(value, most) if isinstance(value, int) else value


def split_product(pe, out, lhs, rhs, k_blocks):
    steps = [(a, c, k) for k in range(k_blocks) for a, c in ((0, 0), (0, 1), (1, 0))]
    for n, (a, c, k) in enumerate(steps):
        last = pe.matmul(out, lhs(a, k), rhs(c, k), start=(n == 0), stop=(n == len(steps) - 1))
    return last


def aggregate(dve, m, aggr_done):
    for t in range(NT):
        last = dve.bn_aggr(m.mv[:, t, :], m.bn6[:, t, :])
    last.then_inc(aggr_done, 1)
    dve.wait_ge(aggr_done, 1)


class Names:
    pass


def shared_memory(nc, ctx):
    m = Names()
    sb = lambda name, shape, dt=F32: ctx.enter_context(nc.sbuf_tensor(name, shape, dt))
    m.x_res = sb("x_res", [P, NT, D])
    m.ident = sb("ident", [P, P])
    m.bn6 = sb("bn6", [P, NT, 6])
    m.mv = sb("mv", [P, NT, 2])
    m.var_eps = sb("var_eps", [P, NT])
    m.rstd = sb("rstd", [P, NT])
    m.neg_half = sb("neg_half", [P, 512])
    m.upper = sb("upper", [P, P])
    m.ones = sb("ones", [P, P])
    m.ones_r = sb("ones_r", [P, P], F32R)
    m.count_up = sb("count_up", [P, P])
    m.tile_starts = sb("tile_starts", [P, NT])
    m.token = sb("token", [P, 2 * NT])
    m.neg_row = sb("neg_row", [P, 1])
    m.expert_less = {tag: sb(f"expert_less_{tag}", [P, e]) for tag, e in (("f0", 4), ("f1", 8))}
    m.banks = ctx.enter_context(nc.psum_tensor("banks", [P, 8, 512], F32))
    return m


def setup_phase(nc, m, A, ctx):
    I32 = mybir.dt.int32
    ints = {n: ctx.enter_context(nc.sbuf_tensor(f"int_{n}", [P, w], I32)) for n, w in
            (("count_up", P), ("tile_starts", NT), ("token", 2 * NT), ("neg_row", 1), ("f0", 4), ("f1", 8))}
    iota_done = nc.alloc_semaphore("iota_done")
    upper_ready = nc.alloc_semaphore("upper_ready")
    x_here, id_zero, id_ready, half_ready, bn_done, aggr_done, eps_done, rstd_done = (
        nc.alloc_semaphore(n) for n in
        ("x_here", "id_zero", "id_ready", "half_ready", "bn_done", "aggr_done", "eps_done", "rstd_done"))
    block = ctx.enter_context(nc.Block())

    @block.sync
    def _(sp):
        x_tiles = A["L0_attn_x"].rearrange("(t p) d -> p t d", p=P)
        for half in range(2):
            sp.dma_start(m.x_res[:, half * NT // 2:(half + 1) * NT // 2, :],
                         x_tiles[:, half * NT // 2:(half + 1) * NT // 2, :]).then_inc(x_here, 16)

    @block.gpsimd
    def _(pool):
        pool.memset(m.ident[:], 0.0).then_inc(id_zero, 1)
        pool.memset(m.neg_half[:], -0.5).then_inc(half_ready, 1)
        pool.wait_ge(id_zero, 1)
        pool.affine_select(out=m.ident[:], in_=m.ident[:], compare_op=ALU.not_equal, fill=1.0, base=0,
                           pattern=[[-1, P]], channel_multiplier=1).then_inc(id_ready, 1)
        pool.memset(m.ones[:], 1.0).then_inc(upper_ready, 1)
        pool.wait_ge(upper_ready, 1)
        pool.affine_select(out=m.upper[:], in_=m.ones[:], compare_op=ALU.is_ge, fill=0.0, base=-1,
                           pattern=[[1, P]], channel_multiplier=-1).then_inc(upper_ready, 1)
        pool.iota(ints["count_up"][:], [[1, P]], base=0, channel_multiplier=0).then_inc(iota_done, 1)
        pool.iota(ints["tile_starts"][:], [[P, NT]], base=0, channel_multiplier=0).then_inc(iota_done, 1)
        pool.iota(ints["token"][:], [[0, 2], [P, NT]], base=0, channel_multiplier=1).then_inc(iota_done, 1)
        pool.iota(ints["neg_row"][:], [[0, 1]], base=0, channel_multiplier=-1).then_inc(iota_done, 1)
        pool.iota(ints["f0"][:], [[1, 4]], base=-4, channel_multiplier=0).then_inc(iota_done, 1)
        pool.iota(ints["f1"][:], [[1, 8]], base=-8, channel_multiplier=0).then_inc(iota_done, 1)
        pool.wait_ge(half_ready, 1)
        pool.wait_ge(eps_done, 1)
        pool.tensor_tensor(m.rstd[:], m.var_eps[:], m.neg_half[:, 0:NT], ALU.pow).then_inc(rstd_done, 1)

    @block.vector
    def _(dve):
        dve.wait_ge(iota_done, 6)
        dve.wait_ge(upper_ready, 1)
        for name, to in (("count_up", m.count_up), ("tile_starts", m.tile_starts), ("token", m.token),
                         ("neg_row", m.neg_row), ("f0", m.expert_less["f0"]), ("f1", m.expert_less["f1"])):
            dve.tensor_copy(to[:], ints[name][:])
        dve.tensor_copy(m.ones_r[:], m.ones[:])
        dve.wait_ge(x_here, 32)
        for t in range(NT):
            last = dve.bn_stats(m.bn6[:, t, :], m.x_res[:, t, :])
        last.then_inc(bn_done, 1)
        dve.wait_ge(bn_done, 1)
        aggregate(dve, m, aggr_done)
        dve.tensor_scalar(m.var_eps[:], m.mv[:, :, 1], LN_EPS, None, ALU.add).then_inc(eps_done, 1)


def attention_phase(nc, m, A, ctx):
    sb = lambda name, shape, dt=F32: ctx.enter_context(nc.sbuf_tensor(name, shape, dt))
    sem = lambda name: nc.alloc_semaphore(name)
    w_stage = sb("a_w_stage", [P, KB, D])
    wt_stage = sb("a_wt_stage", [P, KB, D])
    w_hi, w_lo = sb("a_w_hi", [P, KB, D], F32R), sb("a_w_lo", [P, KB, D], F32R)
    wt_hi, wt_lo = sb("a_wt_hi", [P, KB, D], F32R), sb("a_wt_lo", [P, KB, D], F32R)
    g1, g2, g3, gq = sb("g1", [P, DH]), sb("g2", [P, DH]), sb("g3", [P, DH]), sb("gq", [P, DH])
    xn = sb("a_xn", [P, S, D])
    xt_hi, xt_lo = sb("a_xt_hi", [P, KB * S * P], F32R), sb("a_xt_lo", [P, KB * S * P], F32R)
    sq = sb("a_sq", [P, S * NH, DH])
    ms, ms_eps, rr = sb("a_ms", [P, S * NH]), sb("a_ms_eps", [P, S * NH]), sb("a_rr", [P, S * NH])
    u, q = sb("a_u", [P, S * NH, DH]), sb("a_q", [P, S * NH, DH])
    qst, kst = sb("a_qst", [P, 2, S * NH, 4, DH], F32R), sb("a_kst", [P, 2, S * NH, 4, DH], F32R)
    vv = sb("a_vv", [P, 2, S * NH, 2, DH])
    qkt = sb("a_qkt", [P, 2, 4 * P], F32R)
    ebuf = sb("a_e", [P, 4, 4, T])
    ssum, rs = sb("a_ssum", [P, 2, NH * S]), sb("a_rs", [P, 2, NH * S])
    outt = sb("a_outt", [P, 2, T])
    ytmp, ytok = sb("a_ytmp", [P, S, 4, DH]), sb("a_ytok", [P, S, D])
    yt_hi, yt_lo = sb("a_yt_hi", [P, KB * S * P], F32R), sb("a_yt_lo", [P, KB * S * P], F32R)

    (loaded, gaps_zero, w_copied, w_split, gq_half, gq_ready, xn_ready, xt_in_psum, xth, xtl, w_ready, sq_done,
     ms_done, mse_done, rr_ready, u_ready, kh_done, kst_ready, q_done, qh_done, qst_ready, v_ready, qk_in_psum,
     qkt_ready, s_ready, exp_done, sum_done, rs_done, vr_ready, av_done, outt_ready, yraw_in_psum, ytmp_done,
     ytok_done, yt_in_psum, yth, ytl, proj_done, x1_done, bn_done, aggr_done, eps_done, rstd_done) = (
        sem("a_" + n) for n in
        "loaded gaps_zero w_copied w_split gq_half gq_ready xn_ready xt_in_psum xth xtl w_ready sq_done "
        "ms_done mse_done rr_ready u_ready kh_done kst_ready q_done qh_done qst_ready v_ready qk_in_psum "
        "qkt_ready s_ready exp_done sum_done rs_done vr_ready av_done outt_ready yraw_in_psum ytmp_done "
        "ytok_done yt_in_psum yth ytl proj_done x1_done bn_done aggr_done eps_done rstd_done".split())

    tr = m.banks[:, 0, :]
    proj = m.banks[:, 1, :]
    qkp = m.banks[:, 2, :]
    av = m.banks[:, 3, :].rearrange("p (g t) -> p g t", g=2)
    scores = m.banks[:, 4:8, :].rearrange("p (r h) (s t) -> p r h s t", r=2, s=S)

    def schedule(eng, w):
        def batch(b, z, first=False, last=False):
            for p in range(NP):
                if not last and p == 0:
                    w.prepare_0(b + 1, 1 - z)
                if not last and p == 1:
                    w.prepare_1(b + 1, 1 - z)
                if not (last and p == NP - 1):
                    w.ahead(b, p + 1, z) if p < NP - 1 else w.ahead(b + 1, 0, 1 - z)
                w.now(b, p, z)
                if p > 0:
                    w.late(b, p - 1, z)
                elif not first:
                    w.late(b - 1, NP - 1, 1 - z)
                if not (last and p == NP - 1):
                    w.score(b, p + 1, z) if p < NP - 1 else w.score(b + 1, 0, 1 - z)
                if p in (3, 5, 7):
                    w.rows(b, (p - 3) // 2, z)
                if p == 1 and not first:
                    w.rows(b - 1, 3, 1 - z)
                if p == 2 and not first:
                    w.turn(b - 1)
                if p == 4 and not first:
                    w.project(b - 1)
                if not last and p == 0:
                    w.prepare_0_end(b + 1)
                if not last and p == 1:
                    w.prepare_1_end(b + 1)
                if not last and p == 2:
                    w.prepare_2(b + 1)
                if not last and p == 3:
                    w.prepare_3(b + 1, 1 - z)

        w.prepare_0(0, 0)
        w.prepare_0_end(0)
        w.prepare_1(0, 0)
        w.prepare_1_end(0)
        w.prepare_2(0)
        w.prepare_3(0, 0)
        w.ahead(0, 0, 0)
        w.score(0, 0, 0)
        batch(0, 0, first=True)
        with eng.Fori(0, (B - 2) // 2) as i:
            batch(2 * i + 1, 1)
            batch(2 * i + 2, 0)
        batch(B - 1, 1, last=True)
        w.late(B - 1, NP - 1, 1)
        w.rows(B - 1, 3, 1)
        w.turn(B - 1)
        w.project(B - 1)

    class Work:
        def prepare_0(self, b, z): pass
        def prepare_0_end(self, b): pass
        def prepare_1(self, b, z): pass
        def prepare_1_end(self, b): pass
        def prepare_2(self, b): pass
        def prepare_3(self, b, z): pass
        def ahead(self, b, p, z): pass
        def now(self, b, p, z): pass
        def score(self, b, p, z): pass
        def late(self, b, p, z): pass
        def rows(self, b, g, z): pass
        def turn(self, b): pass
        def project(self, b): pass

    block = ctx.enter_context(nc.Block())

    @block.sync
    def _(sp):
        sp.dma_start(wt_stage[:], A["L0_attn_WT"].rearrange("(k p) n -> p k n", p=P)).then_inc(loaded, 16)
        sp.dma_start(w_stage[:], A["L0_attn_W"].rearrange("(k p) n -> p k n", p=P)).then_inc(loaded, 16)
        for g, name in ((g1, "L0_attn_g1"), (g2, "L0_attn_g2"), (g3, "L0_attn_g3")):
            sp.dma_start(g[:], A[name].rearrange("(o d) -> o d", o=1).broadcast_to([P, DH])).then_inc(loaded, 16)

    @block.tensor
    def _(pe):
        class PE(Work):
            def prepare_0_end(self, b):
                pe.wait_ge(xn_ready, b + 1)
                at_least(pe, ytok_done, 4 * b - 5)
                for k in range(KB):
                    for s in range(S):
                        last = pe.transpose(tr[:, (k * S + s) * P:(k * S + s + 1) * P],
                                            xn[:, s, k * P:(k + 1) * P], m.ident[:])
                last.then_inc(xt_in_psum, 1)

            def prepare_1_end(self, b):
                pe.wait_ge(xth, b + 1)
                pe.wait_ge(xtl, b + 1)
                at_least(pe, x1_done, b - 2)
                xt, wt = (xt_hi, xt_lo), (wt_hi, wt_lo)
                for s in range(S):
                    last = split_product(
                        pe, proj[:, s * D:(s + 1) * D],
                        lambda a, k: xt[a][:, (k * S + s) * P:(k * S + s + 1) * P],
                        lambda a, k: wt[a][:, k, :], KB)
                last.then_inc(w_ready, 1)

            def ahead(self, b, p, z):
                n = NP * b + p
                if p == 0:
                    pe.wait_ge(kst_ready, b + 1)
                    pe.wait_ge(qst_ready, b + 1)
                at_least(pe, qkt_ready, n)
                for j, st in enumerate((qst, kst)):
                    for s in range(S):
                        rows = st[:, z, s * NH + 2 * p:s * NH + 2 * p + 2, :, :]
                        last = pe.transpose(qkp[:, (2 * j + s) * P:(2 * j + s + 1) * P],
                                            f32(rows.rearrange("p h r d -> p (h r d)")), m.ident[:])
                last.then_inc(qk_in_psum, 1)

            def score(self, b, p, z):
                n = NP * b + p
                pe.wait_ge(qkt_ready, n + 1)
                at_least(pe, exp_done, n - 1)
                for h in range(2):
                    for s in range(S):
                        last = pe.matmul(scores[:, p % 2, h, s, :],
                                         qkt[64 * h:64 * h + 3 * DH, p % 2, s * P:(s + 1) * P],
                                         qkt[64 * h:64 * h + 3 * DH, p % 2, 2 * P:4 * P], start=True, stop=True)
                last.then_inc(s_ready, 1)

            def late(self, b, p, z):
                pe.wait_ge(vr_ready, NP * b + p + 1)
                if p % 2 == 0:
                    at_least(pe, outt_ready, 4 * b + p // 2)
                for s in range(S):
                    for h in range(2):
                        row = 32 * (2 * (p % 2) + h)
                        last = pe.matmul(av[row:row + 32, p // 2 % 2, :],
                                         vv[:, z, s * NH + 2 * p + h, :, :].rearrange("p r d -> p (r d)"),
                                         ebuf[:, p % 4, 2 * h + s, :], start=(s == 0), stop=(s == S - 1),
                                         skip_group_check=True)
                last.then_inc(av_done, 1)

            def rows(self, b, g, z):
                pe.wait_ge(outt_ready, 4 * b + g + 1)
                if g == 0:
                    at_least(pe, yth, b)
                    at_least(pe, ytl, b)
                else:
                    pe.wait_ge(ytok_done, 4 * b + g)
                if g == 3:
                    pe.wait_ge(xth, upto(b + 3, B))
                    pe.wait_ge(xtl, upto(b + 3, B))
                for s in range(S):
                    last = pe.transpose(tr[:, (g % 2 * S + s) * P:(g % 2 * S + s + 1) * P],
                                        outt[:, g % 2, s * P:(s + 1) * P], m.ident[:])
                last.then_inc(yraw_in_psum, 1)

            def turn(self, b):
                pe.wait_ge(ytok_done, 4 * b + 4)
                for k in range(KB):
                    for s in range(S):
                        last = pe.transpose(tr[:, (k * S + s) * P:(k * S + s + 1) * P],
                                            ytok[:, s, k * P:(k + 1) * P], m.ident[:])
                last.then_inc(yt_in_psum, 1)

            def project(self, b):
                pe.wait_ge(yth, b + 1)
                pe.wait_ge(ytl, b + 1)
                pe.wait_ge(u_ready, upto(b + 3, B))
                pe.wait_ge(sq_done, upto(b + 3, B))
                yt, w = (yt_hi, yt_lo), (w_hi, w_lo)
                for s in range(S):
                    last = split_product(
                        pe, proj[:, s * D:(s + 1) * D],
                        lambda a, k: yt[a][:, (k * S + s) * P:(k * S + s + 1) * P],
                        lambda a, k: w[a][:, k, :], KB)
                last.then_inc(proj_done, 1)

        pe.wait_ge(w_split, 2)
        schedule(pe, PE())

    @block.scalar
    def _(act):
        class Act(Work):
            def prepare_1(self, b, z):
                act.wait_ge(xt_in_psum, b + 1)
                at_least(act, w_ready, b)
                act.activation(xt_hi[:], tr, ACT.Copy).then_inc(xth, 1)

            def prepare_2(self, b):
                act.wait_ge(w_ready, b + 1)
                at_least(act, ms_done, b)
                act.activation(sq[:].rearrange("p h d -> p (h d)"), proj, ACT.Square).then_inc(sq_done, 1)

            def ahead(self, b, p, z):
                n = NP * b + p
                act.wait_ge(qk_in_psum, n + 1)
                at_least(act, s_ready, n - 1)
                act.activation(qkt[:, p % 2, :], qkp, ACT.Copy).then_inc(qkt_ready, 1)

            def late(self, b, p, z):
                if p % 2 == 1:
                    self.copy_group(b, p // 2)

            def score(self, b, p, z):
                n = NP * b + p
                act.wait_ge(s_ready, n + 1)
                at_least(act, av_done, n - 3)
                at_least(act, sum_done, n - 3)
                act.activation(ebuf[:, p % 4, :, :],
                               scores[:, p % 2, :, :, :].rearrange("p h s t -> p (h s) t"),
                               ACT.Exp).then_inc(exp_done, 1)

            def copy_group(self, b, g):
                act.wait_ge(av_done, NP * b + 2 * g + 2)
                at_least(act, yraw_in_psum, 4 * b + g - 1)
                act.activation(outt[:, g % 2, :], av[:, g % 2, :], ACT.Copy).then_inc(outt_ready, 1)

            def turn(self, b):
                act.wait_ge(yt_in_psum, b + 1)
                at_least(act, proj_done, b)
                act.activation(yt_hi[:], tr, ACT.Copy).then_inc(yth, 1)

        act.preload_act_table(ACT.Exp)


        schedule(act, Act())

    @block.vector
    def _(dve):
        class Dve(Work):
            def prepare_0(self, b, z):
                at_least(dve, xt_in_psum, b)
                for s in range(S):
                    at = bass.ds(S * b + s, 1)
                    last = dve.tensor_scalar(xn[:, s:s + 1, :], m.x_res[:, at, :], m.mv[:, at, 0],
                                             m.rstd[:, at], ALU.subtract, ALU.mult)
                last.then_inc(xn_ready, 1)

            def prepare_1(self, b, z):
                dve.wait_ge(xth, b + 1)
                at_least(dve, w_ready, b)
                dve.tensor_tensor(xt_lo[:], tr, f32(xt_hi[:]), ALU.subtract).then_inc(xtl, 1)

            def prepare_2(self, b):
                dve.wait_ge(sq_done, b + 1)
                at_least(dve, mse_done, b)
                dve.tensor_reduce(ms[:], sq[:], AX_X, ALU.add).then_inc(ms_done, 1)
                dve.wait_ge(ms_done, b + 1)
                at_least(dve, rr_ready, b)
                dve.tensor_scalar(ms_eps[:], ms[:], 1.0 / DH, RMS_EPS, ALU.mult, ALU.add).then_inc(mse_done, 1)

            def prepare_3(self, b, z):
                dve.wait_ge(rr_ready, b + 1)
                at_least(dve, q_done, b)
                at_least(dve, v_ready, b)
                at_least(dve, kst_ready, b)
                dve.tensor_tensor(u[:], proj.rearrange("p (h d) -> p h d", d=DH),
                                  rr[:].unsqueeze(2).broadcast_to([P, S * NH, DH]), ALU.mult).then_inc(u_ready, 1)
                dve.wait_ge(u_ready, b + 1)
                at_least(dve, qk_in_psum, NP * (b - 1))
                dve.tensor_copy(kst[:, z, :, 0:3:2, :],
                                u[:].unsqueeze(2).broadcast_to([P, S * NH, 2, DH])).then_inc(kh_done, 1)
                dve.wait_ge(kh_done, b + 1)
                dve.tensor_tensor(kst[:, z, :, 1, :], u[:], f32(kst[:, z, :, 0, :]), ALU.subtract).then_inc(kst_ready, 1)

            def now(self, b, p, z):
                n = NP * b + p
                dve.wait_ge(exp_done, n + 1)
                dve.tensor_reduce(ssum[:, z, 4 * p:4 * p + 4], ebuf[:, p % 4, :, :], AX_X, ALU.add).then_inc(sum_done, 1)
                dve.wait_ge(sum_done, n + 1)
                dve.reciprocal(rs[:, z, 4 * p:4 * p + 4], ssum[:, z, 4 * p:4 * p + 4]).then_inc(rs_done, 1)
                dve.wait_ge(rs_done, n + 1)
                if p == 0:
                    dve.wait_ge(v_ready, b + 1)
                v2 = vv[:, z, :, :, :].rearrange("p (s h) r d -> p s h r d", s=S)[:, :, 2 * p:2 * p + 2, :, :]
                r2 = rs[:, z, 4 * p:4 * p + 4].rearrange("p (h s) -> p s h", s=S)
                dve.tensor_tensor(v2[:, :, :, 1, :], v2[:, :, :, 0, :],
                                  r2.unsqueeze(3).broadcast_to([P, S, 2, DH]), ALU.mult).then_inc(vr_ready, 1)

            def rows(self, b, g, z):
                dve.wait_ge(yraw_in_psum, 4 * b + g + 1)
                at_least(dve, ytok_done, 4 * b + g)
                raw = tr[:, g % 2 * S * P:(g % 2 + 1) * S * P].rearrange("p (s h r d) -> p s h r d", s=S, h=4, r=2)
                r4 = rs[:, z, 4 * g * S:4 * (g + 1) * S].rearrange("p (h s) -> p s h", s=S)
                dve.tensor_tensor(ytmp[:], raw[:, :, :, 0, :], r4.unsqueeze(3).broadcast_to([P, S, 4, DH]),
                                  ALU.mult).then_inc(ytmp_done, 1)
                dve.wait_ge(ytmp_done, 4 * b + g + 1)
                if g == 0:
                    at_least(dve, yt_in_psum, b)
                dve.tensor_tensor(ytok[:, :, 4 * g * DH:4 * (g + 1) * DH].rearrange("p s (h d) -> p s h d", d=DH),
                                  raw[:, :, :, 1, :], ytmp[:], ALU.add).then_inc(ytok_done, 1)

            def turn(self, b):
                dve.wait_ge(yth, b + 1)
                at_least(dve, proj_done, b)
                dve.tensor_tensor(yt_lo[:], tr, f32(yt_hi[:]), ALU.subtract).then_inc(ytl, 1)

            def project(self, b):
                dve.wait_ge(proj_done, b + 1)
                two = m.x_res[:, bass.ds(S * b, S), :]
                dve.tensor_tensor(two, two, proj.rearrange("p (s c) -> p s c", s=S), ALU.add).then_inc(x1_done, 1)
                dve.wait_ge(x1_done, b + 1)
                for s in range(S):
                    at = bass.ds(S * b + s, 1)
                    last = dve.bn_stats(m.bn6[:, at, :].rearrange("p a c -> p (a c)"),
                                        m.x_res[:, at, :].rearrange("p a c -> p (a c)"))
                last.then_inc(bn_done, 1)

        schedule(dve, Dve())
        dve.wait_ge(bn_done, B)
        aggregate(dve, m, aggr_done)
        dve.tensor_scalar(m.var_eps[:], m.mv[:, :, 1], LN_EPS, None, ALU.add).then_inc(eps_done, 1)

    @block.gpsimd
    def _(pool):
        class Pool(Work):
            def prepare_2(self, b):
                pool.wait_ge(mse_done, b + 1)
                at_least(pool, u_ready, b)
                pool.tensor_tensor(rr[:], ms_eps[:], m.neg_half[:, 0:S * NH], ALU.pow).then_inc(rr_ready, 1)

            def prepare_3(self, b, z):
                wide = lambda g: g[:].unsqueeze(1).broadcast_to([P, S * NH, DH])
                pool.wait_ge(u_ready, b + 1)
                at_least(pool, qst_ready, b)
                pool.tensor_tensor(q[:], u[:], wide(gq), ALU.mult).then_inc(q_done, 1)
                at_least(pool, av_done, NP * (b - 1))
                pool.tensor_tensor(vv[:, z, :, 0, :], u[:], wide(g3), ALU.mult).then_inc(v_ready, 1)
                at_least(pool, qk_in_psum, NP * (b - 1))
                two = lambda ap, n: ap.unsqueeze(n).broadcast_to([P, S * NH, 2, DH])
                pool.tensor_tensor(qst[:, z, :, 0:2, :], two(u[:], 2),
                                   two(gq[:].unsqueeze(1), 1), ALU.mult).then_inc(qh_done, 1)
                pool.wait_ge(q_done, b + 1)
                pool.wait_ge(qh_done, b + 1)
                pool.tensor_tensor(qst[:, z, :, 2, :], q[:], f32(qst[:, z, :, 0, :]), ALU.subtract).then_inc(qst_ready, 1)

        pool.wait_ge(loaded, 80)
        for i, (stage, hi) in enumerate(((wt_stage, wt_hi), (w_stage, w_hi))):
            last = pool.tensor_copy(hi[:], stage[:])
        last.then_inc(w_copied, 1)
        pool.wait_ge(w_copied, 1)
        for stage, hi, lo in ((wt_stage, wt_hi, wt_lo), (w_stage, w_hi, w_lo)):
            pool.tensor_tensor(lo[:], stage[:], f32(hi[:]), ALU.subtract).then_inc(w_split, 1)
        pool.memset(f32(qst[:, :, :, 3, :]), 0.0)
        pool.memset(f32(kst[:, :, :, 3, :]), 0.0).then_inc(gaps_zero, 1)
        pool.tensor_tensor(gq[:], g1[:], g2[:], ALU.mult).then_inc(gq_half, 1)
        pool.wait_ge(gq_half, 1)
        pool.tensor_scalar(gq[:], gq[:], float(DH) ** -0.5, None, ALU.mult).then_inc(gq_ready, 1)
        pool.wait_ge(gq_ready, 1)
        pool.wait_ge(gaps_zero, 1)
        schedule(pool, Pool())
        pool.wait_ge(eps_done, 1)
        pool.tensor_tensor(m.rstd[:], m.var_eps[:], m.neg_half[:, 0:NT], ALU.pow).then_inc(rstd_done, 1)


class Mixture:
    def __init__(self, tag, experts, hidden, gated, shared, slope, lin_bias):
        self.tag, self.experts, self.hidden, self.shared = tag, experts, hidden, shared
        self.gated = gated
        self.slope = slope
        self.lin_bias = lin_bias
        self.tiles = 2 * NT + experts - 1
        self.hb = hidden // P


def mixture_memory(nc, v, ctx):
    k = Names()
    sb = lambda name, shape, dt=F32: ctx.enter_context(nc.sbuf_tensor(f"{v.tag}_{name}", shape, dt))
    k.w13_hi, k.w13_lo = (sb(n, [P, v.experts, KB, 2 * v.hidden], F32R) for n in ("w13_hi", "w13_lo"))
    k.w2_hi, k.w2_lo = (sb(n, [P, v.experts, v.hb, D], F32R) for n in ("w2_hi", "w2_lo"))
    k.logits = sb("logits", [P, v.experts, NT])
    k.weight = sb("weight", [P, 2, NT])
    k.pos = sb("pos", [P, 2, NT], mybir.dt.int32)
    k.token_of = sb("token_of", [P, v.tiles], mybir.dt.int32)
    k.expert_of = sb("expert_of", [P, v.tiles], mybir.dt.int32)
    if v.lin_bias:
        k.b1, k.b2 = sb("b1", [2, v.experts, 2 * v.hidden], F32R), sb("b2", [2, v.experts, D], F32R)
    k.xn_dram = nc.dram_tensor(f"{v.tag}_xn", [TOK, D], F32).ap()
    k.y_dram = nc.dram_tensor(f"{v.tag}_y", [v.tiles * P, D], F32).ap()
    return k


def router_phase(nc, m, A, v, k, ctx):
    E, HS = v.experts, 256
    HSB = HS // P
    sb = lambda name, shape, dt=F32: ctx.enter_context(nc.sbuf_tensor(f"{v.tag}r_{name}", shape, dt))
    sem = lambda name: nc.alloc_semaphore(f"{v.tag}r_{name}")
    xn = sb("xn", [P, 2, S, D])
    xt_hi, xt_lo = sb("xt_hi", [P, 2, KB, S * P], F32R), sb("xt_lo", [P, 2, KB, S * P], F32R)
    gate_stage = sb("gate_stage", [P, KB, E])
    gate_hi, gate_lo = sb("gate_hi", [P, KB, E], F32R), sb("gate_lo", [P, KB, E], F32R)
    gate_b = sb("gate_b", [P, E])
    stage = sb("stage", [P, 2, max(KB * 2 * v.hidden, v.hb * D)])
    if v.shared:
        s13_hi, s13_lo = sb("s13_hi", [P, KB, 2 * HS], F32R), sb("s13_lo", [P, KB, 2 * HS], F32R)
        s2_hi, s2_lo = sb("s2_hi", [P, HSB, D], F32R), sb("s2_lo", [P, HSB, D], F32R)
        th, s1, h = (sb(n, [P, 2, HSB * S * P]) for n in ("th", "s1", "h"))
        h_hi, h_lo = sb("h_hi", [P, 2, HSB, S * P], F32R), sb("h_lo", [P, 2, HSB, S * P], F32R)
    if v.lin_bias:
        bias_stage1, bias_stage2 = sb("bias1", [2, E, 2 * v.hidden]), sb("bias2", [2, E, D])

    (stage0_here, stage1_here, small_here, xn_ready, stored0, stored1, xt_in_psum, xth, xtl, lg_in_psum, lg_done, up_done,
     th_done, s1_done, h_done, hh_done, hl_done, down_done, added, hi_done, lo_done, gate_done, bias_done) = (
        sem(n) for n in
        "stage0_here stage1_here small_here xn_ready stored0 stored1 xt_in_psum xth xtl lg_in_psum lg_done up_done "
        "th_done s1_done h_done hh_done hl_done down_done added hi_done lo_done gate_done bias_done".split())
    stage_here, stored = (stage0_here, stage1_here), (stored0, stored1)
    if not v.shared:
        up_done = lg_in_psum

    pieces = []
    if v.shared:
        pieces.append((A["s13T"].rearrange("(k p) n -> p k n", p=P), s13_hi[:], s13_lo[:]))
        pieces.append((A["s2T"].rearrange("(k p) n -> p k n", p=P), s2_hi[:], s2_lo[:]))
    early = len(pieces)
    for e in range(E):
        pieces.append((A["w13T"][e].rearrange("(k p) n -> p k n", p=P), k.w13_hi[:, e], k.w13_lo[:, e]))
        pieces.append((A["w2T"][e].rearrange("(k p) n -> p k n", p=P), k.w2_hi[:, e], k.w2_lo[:, e]))

    def staged(i):
        view = pieces[i][0]
        a, b = view.shape[1], view.shape[2]
        return stage[:, i % 2, 0:a * b].rearrange("p (a b) -> p a b", a=a)

    C = B

    def schedule(eng, w):
        def slot(c, z, half, first=False, last=False):
            if not last:
                w.turn(c + 1, 1 - z, half + z)
            w.products(c, z)
            if v.shared and not first:
                w.down(c - 1, 1 - z)
        w.turn(0, 0, 0)
        slot(0, 0, 0, first=True)
        slot(1, 1, 0)
        with eng.Fori(0, (C - 4) // 2) as i:
            slot(2 * i + 2, 0, i + 1)
            slot(2 * i + 3, 1, i + 1)
        slot(C - 2, 0, (C - 2) // 2)
        slot(C - 1, 1, (C - 1) // 2, last=True)
        if v.shared:
            w.down(C - 1, 1)

    class Work:
        def turn(self, c, z, half): pass
        def products(self, c, z): pass
        def down(self, c, z): pass

    block = ctx.enter_context(nc.Block())
    small = 16 * (1 + 3 * bool(v.lin_bias))

    @block.sync
    def _(sp):
        sp.dma_start(gate_stage[:], A["gateT"].rearrange("(k p) n -> p k n", p=P)).then_inc(small_here, 16)
        if v.lin_bias:
            sp.dma_start(gate_b[:], A["gate_b"].rearrange("(o d) -> o d", o=1).broadcast_to([P, E])).then_inc(small_here, 16)
            sp.dma_start(bias_stage1[:], A["b1"].rearrange("(o e) n -> o e n", o=1).broadcast_to([2, E, 2 * v.hidden])).then_inc(small_here, 16)
            sp.dma_start(bias_stage2[:], A["b2"].rearrange("(o e) n -> o e n", o=1).broadcast_to([2, E, D])).then_inc(small_here, 16)

        def load(i):
            if i >= 2:
                sp.wait_ge(lo_done, i - 1)
            sp.dma_start(staged(i), pieces[i][0]).then_inc(stage_here[i % 2], 16)

        for i in range(2):
            load(i)

        class Sp(Work):
            def turn(self, c, z, half):
                sp.wait_ge(xn_ready, c + 1)
                sp.dma_start(k.xn_dram.rearrange("(c s p) d -> c p s d", s=S, p=P)[bass.ds(c, 1)].rearrange("c p s d -> p (c s) d"),
                             xn[:, z]).then_inc(stored[z], 16)

        schedule(sp, Sp())
        for i in range(2, len(pieces)):
            load(i)
        for z in range(2):
            sp.wait_ge(stored[z], 16 * C // 2)

    @block.tensor
    def _(pe):
        class PE(Work):
            def turn(self, c, z, half):
                pe.wait_ge(xn_ready, c + 1)
                at_least(pe, xth, c)
                at_least(pe, xtl, c)
                for kb in range(KB):
                    for s in range(S):
                        last = pe.transpose(m.banks[:, 0, (kb * S + s) * P:(kb * S + s + 1) * P],
                                            xn[:, z, s, kb * P:(kb + 1) * P], m.ident[:])
                last.then_inc(xt_in_psum, 1)

            def products(self, c, z):
                pe.wait_ge(xth, c + 1)
                pe.wait_ge(xtl, c + 1)
                at_least(pe, lg_done, c)
                xt, gate = (xt_hi, xt_lo), (gate_hi, gate_lo)
                for s in range(S):
                    last = split_product(pe, m.banks[:, 1, s * E:(s + 1) * E],
                                         lambda a, kb: xt[a][:, z, kb, s * P:(s + 1) * P],
                                         lambda a, kb: gate[a][:, kb, :], KB)
                last.then_inc(lg_in_psum, 1)
                if v.shared:
                    at_least(pe, h_done, c - 1)
                    s13 = (s13_hi, s13_lo)
                    for j in range(2):
                        for hb in range(HSB):
                            col = j * HS + hb * P
                            last = split_product(pe, m.banks[:, 2 + 2 * z + j, hb * S * P:(hb + 1) * S * P],
                                                 lambda a, kb: s13[a][:, kb, col:col + P],
                                                 lambda a, kb: xt[a][:, z, kb, :], KB)
                    last.then_inc(up_done, 1)

            def down(self, c, z):
                pe.wait_ge(hh_done, c + 1)
                pe.wait_ge(hl_done, c + 1)
                at_least(pe, added, c - 1)
                hp, s2 = (h_hi, h_lo), (s2_hi, s2_lo)
                for s in range(S):
                    last = split_product(pe, m.banks[:, 6 + z, s * D:(s + 1) * D],
                                         lambda a, kb: hp[a][:, z, kb, s * P:(s + 1) * P],
                                         lambda a, kb: s2[a][:, kb, :], HSB)
                last.then_inc(down_done, 1)

        pe.wait_ge(gate_done, 2)
        if early:
            pe.wait_ge(lo_done, early)
        schedule(pe, PE())

    @block.scalar
    def _(act):
        def first_part(i):
            act.wait_ge(stage_here[i % 2], 16 * (i // 2 + 1))
            act.activation(pieces[i][1], staged(i), ACT.Copy).then_inc(hi_done, 1)

        class Act(Work):
            def turn(self, c, z, half):
                act.wait_ge(xt_in_psum, c + 1)
                at_least(act, up_done, c - 1)
                act.activation(xt_hi[:, z].rearrange("p k t -> p (k t)"), m.banks[:, 0, :], ACT.Copy).then_inc(xth, 1)

            def products(self, c, z):
                if v.shared:
                    act.wait_ge(up_done, c + 1)
                    at_least(act, s1_done, c - 1)
                    act.activation(th[:, z], m.banks[:, 2 + 2 * z, :], ACT.Tanh, scale=v.slope / 2).then_inc(th_done, 1)

            def down(self, c, z):
                act.wait_ge(h_done, c + 1)
                at_least(act, down_done, c - 1)
                act.activation(h_hi[:, z].rearrange("p k t -> p (k t)"), h[:, z], ACT.Copy).then_inc(hh_done, 1)

        act.preload_act_table(ACT.Exp)
        for i in range(early):
            first_part(i)
        schedule(act, Act())
        for i in range(early, len(pieces)):
            first_part(i)

    @block.vector
    def _(dve):
        def second_part(i):
            dve.wait_ge(hi_done, i + 1)
            dve.tensor_tensor(pieces[i][2], staged(i), f32(pieces[i][1]), ALU.subtract).then_inc(lo_done, 1)

        class Dve(Work):
            def turn(self, c, z, half):
                at_least(dve, xt_in_psum, c - 1)
                if not (isinstance(c, int) and c < 2):
                    dve.wait_ge(stored[z], 16 * half)
                for s in range(S):
                    at = bass.ds(S * c + s, 1)
                    last = dve.tensor_scalar(xn[:, z, s:s + 1, :], m.x_res[:, at, :], m.mv[:, at, 0],
                                             m.rstd[:, at], ALU.subtract, ALU.mult)
                last.then_inc(xn_ready, 1)
                dve.wait_ge(xth, c + 1)
                at_least(dve, up_done, c - 1)
                dve.tensor_tensor(xt_lo[:, z].rearrange("p k t -> p (k t)"), m.banks[:, 0, :],
                                  f32(xt_hi[:, z]).rearrange("p k t -> p (k t)"), ALU.subtract).then_inc(xtl, 1)

            def products(self, c, z):
                dve.wait_ge(lg_in_psum, c + 1)
                out = k.logits[:, :, bass.ds(S * c, S)]
                lg = m.banks[:, 1, 0:S * E].rearrange("p (s e) -> p e s", s=S)
                if v.lin_bias:
                    ins = dve.tensor_tensor(out, lg, gate_b[:].unsqueeze(2).broadcast_to([P, E, S]), ALU.add)
                else:
                    ins = dve.tensor_copy(out, lg)
                ins.then_inc(lg_done, 1)
                if v.shared:
                    dve.wait_ge(th_done, c + 1)
                    at_least(dve, h_done, c - 1)
                    dve.scalar_tensor_tensor(out=s1[:, z], in0=th[:, z], scalar=1.0, in1=m.banks[:, 2 + 2 * z, :],
                                             op0=ALU.add, op1=ALU.mult).then_inc(s1_done, 1)
                    dve.wait_ge(s1_done, c + 1)
                    at_least(dve, hh_done, c - 1)
                    dve.scalar_tensor_tensor(out=h[:, z], in0=s1[:, z], scalar=0.5, in1=m.banks[:, 3 + 2 * z, :],
                                             op0=ALU.mult, op1=ALU.mult).then_inc(h_done, 1)

            def down(self, c, z):
                dve.wait_ge(hh_done, c + 1)
                at_least(dve, down_done, c - 1)
                dve.tensor_tensor(h_lo[:, z].rearrange("p k t -> p (k t)"), h[:, z],
                                  f32(h_hi[:, z]).rearrange("p k t -> p (k t)"), ALU.subtract).then_inc(hl_done, 1)
                dve.wait_ge(down_done, c + 1)
                two = m.x_res[:, bass.ds(S * c, S), :]
                dve.tensor_tensor(two, two, m.banks[:, 6 + z, :].rearrange("p (s c) -> p s c", s=S), ALU.add).then_inc(added, 1)

        dve.wait_ge(small_here, small)
        dve.tensor_copy(gate_hi[:], gate_stage[:]).then_inc(gate_done, 1)
        dve.wait_ge(gate_done, 1)
        dve.tensor_tensor(gate_lo[:], gate_stage[:], f32(gate_hi[:]), ALU.subtract).then_inc(gate_done, 1)
        if v.lin_bias:
            flat = lambda t: t[:].rearrange("p e n -> p (e n)")
            for st, out in ((bias_stage1, k.b1), (bias_stage2, k.b2)):
                last = dve.tensor_copy(out[:], st[:])
            last.then_inc(bias_done, 1)
            dve.wait_ge(bias_done, 1)
            for st, out in ((bias_stage1, k.b1), (bias_stage2, k.b2)):
                last = dve.scalar_tensor_tensor(out=flat(out), in0=f32(flat(out)), scalar=m.neg_row[0:2, 0:1],
                                                in1=flat(st), op0=ALU.mult, op1=ALU.add)
            last.then_inc(bias_done, 1)
        for i in range(early):
            second_part(i)
        schedule(dve, Dve())
        for i in range(early, len(pieces)):
            second_part(i)


def rank_phase(nc, m, v, k, ctx):
    E, NTL = v.experts, v.tiles
    I32, F16 = mybir.dt.int32, mybir.dt.float16
    sb = lambda name, shape, dt=F32: ctx.enter_context(nc.sbuf_tensor(f"{v.tag}k_{name}", shape, dt))
    sem = lambda name: nc.alloc_semaphore(f"{v.tag}k_{name}")
    lg = k.logits
    mx, oh, eq, imin = sb("mx", [P, 2, NT]), sb("oh", [P, 2, E, NT]), sb("eq", [P, E, NT]), sb("imin", [P, NT])
    lg2, both, ex, diff, ex2 = (sb("lg2", [P, E, NT]), sb("both", [P, E, NT]), sb("ex", [P, E, NT]),
                                sb("diff", [P, NT]), sb("ex2", [P, NT]))
    total = sb("total", [P, NT])
    count, before, zeros = sb("count", [P, E, NT]), sb("before", [P, E, NT]), sb("zeros", [P, E * NT])
    upto_here = sb("upto_here", [P, E, NT])
    ne, full, tile_end, base = sb("ne", [P, E]), sb("full", [P, E, NT]), sb("tile_end", [P, E]), sb("base", [P, E])
    nt_e = sb("nt_e", [P, E])
    rank, picked, posf = sb("rank", [P, E, NT]), sb("picked", [P, E, NT]), sb("posf", [P, 2, NT])
    tile_i, row_i = sb("tile_i", [P, 2 * NT], I32), sb("row_i", [P, 2 * NT], I32)
    tile_f, row_f = sb("tile_f", [P, 2 * NT]), sb("row_f", [P, 2 * NT])
    tile_oh, tile_tok = sb("tile_oh", [P, 2 * NT, NTL]), sb("tile_tok", [P, 2 * NT, NTL], F16)
    row_oh = sb("row_oh", [P, 2 * NT, P], F16)
    passed, ef = sb("passed", [P, NTL, E]), sb("ef", [P, NTL])
    step, scalar_step, picks, ranked, rows_ready, listed, zeros_ready = (
        sem(n) for n in "step scalar_step picks ranked rows_ready listed zeros_ready".split())

    e_last = lambda ap: ap.rearrange("p e t -> p t e")
    over_e = lambda ap: ap.unsqueeze(1).broadcast_to([P, E, NT])
    over_t = lambda ap: ap.unsqueeze(2).broadcast_to([P, E, NT])
    block = ctx.enter_context(nc.Block())

    @block.gpsimd
    def _(pool):
        pool.memset(zeros[:], 0.0).then_inc(zeros_ready, 1)

    @block.scalar
    def _(act):
        act.wait_ge(picks, 1)
        act.activation(ex[:], eq[:], ACT.Exp).then_inc(scalar_step, 1)
        act.activation(ex2[:], diff[:], ACT.Exp).then_inc(scalar_step, 1)

    @block.tensor
    def _(pe):
        pe.wait_ge(ranked, 1)
        flat = both[:].rearrange("p e t -> p (e t)")
        pe.matmul(m.banks[:, 0, 0:E * NT], m.upper[:], flat, start=True, stop=True)
        pe.matmul(m.banks[:, 1, 0:E * NT], m.ones[:], flat, start=True, stop=True).then_inc(listed, 1)
        pe.wait_ge(rows_ready, 1)
        for j in range(2 * NT):
            last = pe.matmul(m.banks[:, 2, 0:NTL], row_oh[:, j, :], tile_tok[:, j, :],
                             start=(j == 0), stop=(j == 2 * NT - 1))
        last.then_inc(listed, 1)

    @block.vector
    def _(dve):
        done = [0]

        def then(ins):
            done[0] += 1
            ins.then_inc(step, 1)
            dve.wait_ge(step, done[0])

        source = lg
        for c in range(2):
            then(dve.tensor_reduce(mx[:, c, :], e_last(source[:]), AX_X, ALU.max))
            then(dve.tensor_tensor(eq[:], source[:], over_e(mx[:, c, :]), ALU.is_equal))
            then(dve.tensor_tensor(eq[:], eq[:], over_t(m.expert_less[v.tag][:]), ALU.mult))
            then(dve.tensor_reduce(imin[:], e_last(eq[:]), AX_X, ALU.min))
            then(dve.tensor_tensor(oh[:, c], eq[:], over_e(imin[:]), ALU.is_equal))
            if c == 0:
                then(dve.scalar_tensor_tensor(out=lg2[:].rearrange("p e t -> p (e t)"),
                                              in0=oh[:, 0].rearrange("p e t -> p (e t)"), scalar=-3e38,
                                              in1=lg[:].rearrange("p e t -> p (e t)"), op0=ALU.mult, op1=ALU.add))
                source = lg2
        then(dve.tensor_tensor(both[:], oh[:, 0], oh[:, 1], ALU.add))
        dve.tensor_tensor(diff[:], mx[:, 1, :], mx[:, 0, :], ALU.subtract).then_inc(ranked, 1)
        dve.wait_ge(ranked, 1)
        dve.tensor_tensor(eq[:], lg[:], over_e(mx[:, 0, :]), ALU.subtract).then_inc(picks, 1)
        dve.wait_ge(scalar_step, 2)
        if v.gated == "all":
            then(dve.tensor_reduce(total[:], e_last(ex[:]), AX_X, ALU.add))
        else:
            then(dve.tensor_scalar(total[:], ex2[:], 1.0, None, ALU.add))
        then(dve.reciprocal(k.weight[:, 0, :], total[:]))
        then(dve.tensor_tensor(k.weight[:, 1, :], ex2[:], k.weight[:, 0, :], ALU.mult))

        dve.wait_ge(listed, 1)
        dve.wait_ge(zeros_ready, 1)
        flat = lambda t: t[:].rearrange("p e t -> p (e t)")
        then(dve.tensor_copy(flat(count), m.banks[:, 1, 0:E * NT]))
        then(dve.tensor_tensor_scan(flat(upto_here), flat(count), zeros[:], 0.0, ALU.add, ALU.add))
        then(dve.tensor_tensor(before[:], upto_here[:], count[:], ALU.subtract))
        then(dve.tensor_tensor(ne[:], upto_here[:, :, NT - 1], before[:, :, 0], ALU.subtract))
        then(dve.tensor_tensor(full[:], over_t(ne[:]), over_e(m.tile_starts[:]), ALU.is_gt))
        then(dve.tensor_reduce(nt_e[:], full[:], AX_X, ALU.add))
        then(dve.tensor_tensor_scan(tile_end[:], nt_e[:], zeros[:, 0:E], 0.0, ALU.add, ALU.add))
        then(dve.tensor_tensor(base[:], tile_end[:], nt_e[:], ALU.subtract))
        then(dve.scalar_tensor_tensor(out=base[:], in0=base[:], scalar=float(P), in1=before[:, :, 0],
                                      op0=ALU.mult, op1=ALU.subtract))
        then(dve.tensor_tensor(flat(rank), m.banks[:, 0, 0:E * NT], flat(before), ALU.add))
        then(dve.tensor_tensor(rank[:], rank[:], over_t(base[:]), ALU.add))
        for c in range(2):
            then(dve.tensor_tensor(picked[:], rank[:], oh[:, c], ALU.mult))
            then(dve.tensor_reduce(posf[:, c, :], e_last(picked[:]), AX_X, ALU.add))
        then(dve.tensor_copy(k.pos[:], posf[:]))
        pos = k.pos[:].rearrange("p c t -> p (c t)")
        dve.tensor_scalar(tile_i[:], pos, 7, None, ALU.arith_shift_right)
        then(dve.tensor_scalar(row_i[:], pos, P - 1, None, ALU.bitwise_and))
        dve.tensor_copy(tile_f[:], tile_i[:])
        then(dve.tensor_copy(row_f[:], row_i[:]))
        wide = lambda ap, n: ap.unsqueeze(2).broadcast_to([P, 2 * NT, n])
        dve.tensor_tensor(row_oh[:], wide(row_f[:], P), m.count_up[:].unsqueeze(1).broadcast_to([P, 2 * NT, P]), ALU.is_equal)
        then(dve.tensor_tensor(tile_oh[:], wide(tile_f[:], NTL),
                               m.count_up[:, 0:NTL].unsqueeze(1).broadcast_to([P, 2 * NT, NTL]), ALU.is_equal))
        dve.tensor_tensor(tile_tok[:], tile_oh[:], wide(m.token[:], NTL), ALU.mult).then_inc(rows_ready, 1)
        then(dve.tensor_tensor(passed[:], tile_end[:].unsqueeze(1).broadcast_to([P, NTL, E]),
                               m.count_up[:, 0:NTL].unsqueeze(2).broadcast_to([P, NTL, E]), ALU.is_le))
        then(dve.tensor_reduce(ef[:], passed[:], AX_X, ALU.add))
        then(dve.tensor_scalar(ef[:], ef[:], float(E - 1), None, ALU.min))
        then(dve.tensor_copy(k.expert_of[:], ef[:]))
        dve.wait_ge(listed, 2)
        then(dve.tensor_copy(k.token_of[:], m.banks[:, 2, 0:NTL]))


def expert_phase(nc, m, v, k, ctx):
    H2, HB, NTL = 2 * v.hidden, v.hb, v.tiles
    UB = max(1, H2 // 512)
    sb = lambda name, shape, dt=F32: ctx.enter_context(nc.sbuf_tensor(f"{v.tag}x_{name}", shape, dt))
    sem = lambda name: nc.alloc_semaphore(f"{v.tag}x_{name}")
    U32 = mybir.dt.uint32
    index, taken = sb("index", [P, 2], U32), sb("taken", [P, 2])
    xg = sb("xg", [P, 2, D])
    xt_hi, xt_lo = sb("xt_hi", [P, 2, KB * P], F32R), sb("xt_lo", [P, 2, KB * P], F32R)
    th, s1, h = (sb(n, [P, 2, v.hidden]) for n in ("th", "s1", "h"))
    ht_hi, ht_lo = sb("ht_hi", [P, 2, HB * P], F32R), sb("ht_lo", [P, 2, HB * P], F32R)
    yout = sb("yout", [P, 2, D])
    (gathered0, gathered1, index_done, xt_in_psum, xth, xtl, up_done, th_done, s1_done, h_done, ht_in_psum, hth, htl,
     down_done, y_done, stored0, stored1) = (
        sem(n) for n in
        "gathered0 gathered1 index_done xt_in_psum xth xtl up_done th_done s1_done h_done ht_in_psum hth htl "
        "down_done y_done stored0 stored1".split())
    gathered, stored = (gathered0, gathered1), (stored0, stored1)
    up = lambda z: m.banks[:, UB * z:UB * (z + 1), :].rearrange("p b n -> p (b n)")

    def schedule(eng, w):
        def slot(t, z, half, first=False, left=NTL):
            if left > 1:
                w.up(t + 1, 1 - z, half + z)
            w.turn_h(t, z)
            if left > 2:
                w.turn_x(t + 2, z, half + 1)
            if not first:
                w.down(t - 1, 1 - z, half - (1 - z))
        w.turn_x(0, 0, 0)
        w.turn_x(1, 1, 0)
        w.up(0, 0, 0)
        slot(0, 0, 0, first=True)
        slot(1, 1, 0)
        pairs = (NTL - 4) // 2
        with eng.Fori(0, pairs) as i:
            slot(2 * i + 2, 0, i + 1)
            slot(2 * i + 3, 1, i + 1)
        for t in range(2 * pairs + 2, NTL):
            slot(t, t % 2, t // 2, left=NTL - t)
        w.down(NTL - 1, (NTL - 1) % 2, (NTL - 1) // 2)

    class Work:
        def turn_x(self, t, z, half): pass
        def up(self, t, z, half): pass
        def turn_h(self, t, z): pass
        def down(self, t, z, half): pass

    block = ctx.enter_context(nc.Block())

    @block.gpsimd
    def _(pool):
        class Pool(Work):
            def turn_x(self, t, z, half):
                at_least(pool, xt_in_psum, t - 1)
                pool.tensor_copy(index[:, z:z + 1], k.token_of[:, bass.ds(t, 1)]).then_inc(index_done, 1)
                pool.wait_ge(index_done, t + 1)
                pool.tensor_tensor(taken[:, z:z + 1], m.neg_row[:], m.neg_row[:], ALU.add)
                pool.indirect_dma_start(xg[:, z, :], None, k.xn_dram,
                                        bass.IndirectOffsetOnAxis(ap=index[:, z:z + 1], axis=0)).then_inc(gathered[z], 16)
        schedule(pool, Pool())

    @block.sync
    def _(sp):
        class Sp(Work):
            def down(self, t, z, half):
                sp.wait_ge(y_done, t + 1)
                sp.dma_start(k.y_dram.rearrange("(t p) d -> p t d", p=P)[:, bass.ds(t, 1), :],
                             yout[:, z:z + 1, :]).then_inc(stored[z], 16)
        schedule(sp, Sp())
        sp.wait_ge(stored0, 16 * ((NTL + 1) // 2))
        sp.wait_ge(stored1, 16 * (NTL // 2))

    @block.tensor
    def _(pe):
        class PE(Work):
            def turn_x(self, t, z, half):
                pe.wait_ge(gathered[z], 16 * half + 16)
                at_least(pe, xth, t)
                at_least(pe, xtl, t)
                for kb in range(KB):
                    last = pe.transpose(m.banks[:, 5, kb * P:(kb + 1) * P], xg[:, z, kb * P:(kb + 1) * P], m.ident[:])
                last.then_inc(xt_in_psum, 1)

            def up(self, t, z, half):
                pe.wait_ge(xth, t + 1)
                pe.wait_ge(xtl, t + 1)
                at_least(pe, h_done, t - 1)
                e = pe.value_load(k.expert_of[0:1, bass.ds(t, 1)], min_val=0, max_val=v.experts - 1)
                xt, w13 = (xt_hi, xt_lo), (k.w13_hi, k.w13_lo)
                n = min(512, H2)
                for b in range(UB):
                    out = up(z)[:, b * n:(b + 1) * n]
                    steps = [(a, c, kb) for kb in range(KB) for a, c in ((0, 0), (0, 1), (1, 0))]
                    for i, (a, c, kb) in enumerate(steps):
                        last = pe.matmul(out, xt[a][:, z, kb * P:(kb + 1) * P],
                                         w13[c][:, bass.ds(e, 1), kb, b * n:(b + 1) * n],
                                         start=(i == 0), stop=(i == len(steps) - 1 and not v.lin_bias))
                    if v.lin_bias:
                        last = pe.matmul(out, m.ones_r[0:2, :], k.b1[:, bass.ds(e, 1), b * n:(b + 1) * n],
                                         start=False, stop=True)
                last.then_inc(up_done, 1)

            def turn_h(self, t, z):
                pe.wait_ge(h_done, t + 1)
                at_least(pe, hth, t)
                at_least(pe, htl, t)
                for hb in range(HB):
                    last = pe.transpose(m.banks[:, 4, hb * P:(hb + 1) * P], h[:, z, hb * P:(hb + 1) * P], m.ident[:])
                last.then_inc(ht_in_psum, 1)

            def down(self, t, z, half):
                pe.wait_ge(hth, t + 1)
                pe.wait_ge(htl, t + 1)
                at_least(pe, y_done, t - 1)
                e = pe.value_load(k.expert_of[0:1, bass.ds(t, 1)], min_val=0, max_val=v.experts - 1)
                ht, w2 = (ht_hi, ht_lo), (k.w2_hi, k.w2_lo)
                steps = [(a, c, hb) for hb in range(HB) for a, c in ((0, 0), (0, 1), (1, 0))]
                out = m.banks[:, 6 + z, 0:D]
                for i, (a, c, hb) in enumerate(steps):
                    last = pe.matmul(out, ht[a][:, z, hb * P:(hb + 1) * P], w2[c][:, bass.ds(e, 1), hb, :],
                                     start=(i == 0), stop=(i == len(steps) - 1 and not v.lin_bias))
                if v.lin_bias:
                    last = pe.matmul(out, m.ones_r[0:2, :], k.b2[:, bass.ds(e, 1), :], start=False, stop=True)
                last.then_inc(down_done, 1)

        schedule(pe, PE())

    @block.scalar
    def _(act):
        class Act(Work):
            def turn_x(self, t, z, half):
                act.wait_ge(xt_in_psum, t + 1)
                at_least(act, up_done, t - 1)
                act.activation(xt_hi[:, z, :], m.banks[:, 5, 0:D], ACT.Copy).then_inc(xth, 1)

            def up(self, t, z, half):
                act.wait_ge(up_done, t + 1)
                at_least(act, s1_done, t - 1)
                act.activation(th[:, z, :], up(z)[:, 0:v.hidden], ACT.Tanh, scale=v.slope / 2).then_inc(th_done, 1)

            def turn_h(self, t, z):
                act.wait_ge(ht_in_psum, t + 1)
                at_least(act, down_done, t - 1)
                act.activation(ht_hi[:, z, :], m.banks[:, 4, 0:v.hidden], ACT.Copy, scale=0.5).then_inc(hth, 1)

            def down(self, t, z, half):
                act.wait_ge(down_done, t + 1)
                if not (isinstance(t, int) and t < 2):
                    act.wait_ge(stored[z], 16 * half)
                act.activation(yout[:, z, :], m.banks[:, 6 + z, 0:D], ACT.Copy).then_inc(y_done, 1)

        act.preload_act_table(ACT.Tanh)
        schedule(act, Act())

    @block.vector
    def _(dve):
        class Dve(Work):
            def turn_x(self, t, z, half):
                dve.wait_ge(xth, t + 1)
                at_least(dve, up_done, t - 1)
                dve.tensor_tensor(xt_lo[:, z, :], m.banks[:, 5, 0:D], f32(xt_hi[:, z, :]), ALU.subtract).then_inc(xtl, 1)

            def up(self, t, z, half):
                dve.wait_ge(th_done, t + 1)
                at_least(dve, h_done, t - 1)
                dve.scalar_tensor_tensor(out=s1[:, z, :], in0=th[:, z, :], scalar=1.0, in1=up(z)[:, 0:v.hidden],
                                         op0=ALU.add, op1=ALU.mult).then_inc(s1_done, 1)
                dve.wait_ge(s1_done, t + 1)
                at_least(dve, ht_in_psum, t - 1)
                dve.scalar_tensor_tensor(out=h[:, z, :], in0=up(z)[:, v.hidden:H2], scalar=float(v.lin_bias),
                                         in1=s1[:, z, :], op0=ALU.add, op1=ALU.mult).then_inc(h_done, 1)

            def turn_h(self, t, z):
                dve.wait_ge(hth, t + 1)
                at_least(dve, down_done, t - 1)
                dve.scalar_tensor_tensor(out=ht_lo[:, z, :], in0=m.banks[:, 4, 0:v.hidden], scalar=0.5,
                                         in1=f32(ht_hi[:, z, :]), op0=ALU.mult, op1=ALU.subtract).then_inc(htl, 1)

        schedule(dve, Dve())


def combine_phase(nc, m, A, v, k, ctx, out=None):
    sb = lambda name, shape, dt=F32: ctx.enter_context(nc.sbuf_tensor(f"{v.tag}c_{name}", shape, dt))
    sem = lambda name: nc.alloc_semaphore(f"{v.tag}c_{name}")
    U32 = mybir.dt.uint32
    index, taken = sb("index", [P, 2, 2], U32), sb("taken", [P, 2])
    y = sb("y", [P, 2, 2, D])
    gathered = [[sem(f"gathered{z}{c}") for c in range(2)] for z in range(2)]
    index_done, one_added, both_added, stored, bn_done, aggr_done, eps_done, rstd_done = (
        sem(n) for n in "index_done one_added both_added stored bn_done aggr_done eps_done rstd_done".split())
    block = ctx.enter_context(nc.Block())

    @block.gpsimd
    def _(pool):
        def tile(t, z, half):
            at_least(pool, both_added, t - 1)
            for c in range(2):
                pool.tensor_copy(index[:, z, c:c + 1], k.pos[:, c, bass.ds(t, 1)]).then_inc(index_done, 1)
            pool.wait_ge(index_done, 2 * t + 2)
            pool.tensor_tensor(taken[:, z:z + 1], m.neg_row[:], m.neg_row[:], ALU.add)
            for c in range(2):
                pool.indirect_dma_start(y[:, z, c, :], None, k.y_dram,
                                        bass.IndirectOffsetOnAxis(ap=index[:, z, c:c + 1], axis=0)).then_inc(gathered[z][c], 16)
        tile(0, 0, 0)
        with pool.Fori(0, (NT - 2) // 2) as i:
            tile(2 * i + 1, 1, i)
            tile(2 * i + 2, 0, i + 1)
        tile(NT - 1, 1, NT // 2 - 1)
        if out is None:
            pool.wait_ge(eps_done, 1)
            pool.tensor_tensor(m.rstd[:], m.var_eps[:], m.neg_half[:, 0:NT], ALU.pow).then_inc(rstd_done, 1)

    @block.vector
    def _(dve):
        with dve.Fori(0, NT // 2) as i:
            for z in range(2):
                t = 2 * i + z
                at = bass.ds(t, 1)
                x_t = m.x_res[:, at, :].rearrange("p a d -> p (a d)")
                dve.wait_ge(gathered[z][0], 16 * i + 16)
                dve.scalar_tensor_tensor(out=x_t, in0=y[:, z, 0, :], scalar=k.weight[:, 0, at], in1=x_t,
                                         op0=ALU.mult, op1=ALU.add).then_inc(one_added, 1)
                dve.wait_ge(one_added, t + 1)
                dve.wait_ge(gathered[z][1], 16 * i + 16)
                dve.scalar_tensor_tensor(out=x_t, in0=y[:, z, 1, :], scalar=k.weight[:, 1, at], in1=x_t,
                                         op0=ALU.mult, op1=ALU.add).then_inc(both_added, 1)
                if out is None:
                    dve.wait_ge(both_added, t + 1)
                    dve.bn_stats(m.bn6[:, at, :].rearrange("p a c -> p (a c)"), x_t).then_inc(bn_done, 1)
        if out is None:
            dve.wait_ge(bn_done, NT)
            aggregate(dve, m, aggr_done)
            dve.tensor_scalar(m.var_eps[:], m.mv[:, :, 1], LN_EPS, None, ALU.add).then_inc(eps_done, 1)

    @block.sync
    def _(sp):
        if out is not None:
            with sp.Fori(0, NT) as t:
                sp.wait_ge(both_added, t + 1)
                sp.dma_start(out.rearrange("(t p) d -> p t d", p=P)[:, bass.ds(t, 1), :],
                             m.x_res[:, bass.ds(t, 1), :]).then_inc(stored, 16)
            sp.wait_ge(stored, 16 * NT)


def rwkv_phase(nc, m, A, ctx):
    EB = KB
    sb = lambda name, shape, dt=F32: ctx.enter_context(nc.sbuf_tensor("r_" + name, shape, dt))
    sem = lambda name: nc.alloc_semaphore("r_" + name)
    w_stage, w_mixed = sb("w_stage", [P, 4, KB, D]), sb("w_mixed", [P, 3, 2, KB, D])
    w_hi, w_lo = sb("w_hi", [P, 3, 2, KB, D], F32R), sb("w_lo", [P, 3, 2, KB, D], F32R)
    wo_hi, wo_lo = sb("wo_hi", [P, KB, D], F32R), sb("wo_lo", [P, KB, D], F32R)
    tm, tm_less = sb("tm", [P, 3, KB]), sb("tm_less", [P, 3, KB])
    decay, first, gain, shift = (sb(n, [P, EB]) for n in ("decay", "first", "gain", "shift"))
    grown = sb("grown", [P, EB])
    mean_of = sb("mean_of", [P, P])
    xn = sb("xn", [P, S, D])
    xt_hi, xt_lo = sb("xt_hi", [P, 2, KB, T + 1], F32R), sb("xt_lo", [P, 2, KB, T + 1], F32R)
    ks, vs, th = (sb(n, [P, 2, EB, T]) for n in ("k", "v", "th"))
    top, aa, bb = (sb(n, [P, EB, T + 1]) for n in ("top", "aa", "bb"))
    less, ex = sb("less", [P, 4, EB, T]), sb("ex", [P, 4, EB, T])
    dif, f2v, e2v, num, den, rden, wkv, c, sq, lnv, rw = (
        sb(n, [P, EB, T]) for n in ("dif", "f2v", "e2v", "num", "den", "rden", "wkv", "c", "sq", "lnv", "rw"))
    ve, rstd = sb("ve", [P, S]), sb("rstd", [P, S])
    rw_hi, rw_lo = sb("rw_hi", [P, EB, T], F32R), sb("rw_lo", [P, EB, T], F32R)
    names = ("loaded exp_decay half mixed whi wlo edges xn_ready xt_in_psum xth xtl kvr_done evac top_done dif_done "
             "less_done exp_done f2v_done e2v_done aa_done e1a_done num_done e1b_done den_done rden_done wkv_done "
             "mean_done c_done sq_done var_done ve_done rstd_done t_done ln_done rw_done rwh rwl out_done x_done "
             "bn_done aggr_done eps_done next_rstd prep spread")
    done = {n: sem(n) for n in names.split()}
    NEVER = -1e38

    def schedule(eng, w):
        def slot(b, z, first=False, last=False):
            if not isinstance(b, int) or b >= 2:
                w.add(b - 2)
            w.scores(b, z)
            if not first:
                w.centre(b - 1)
            if not last:
                w.turn(b + 1, 1 - z)
            if not first:
                w.vary(b - 1)
            w.weigh(b, z)
            if not last:
                w.products(b + 1, 1 - z)
            if not first:
                w.norm(b - 1, 1 - z)
            w.mean(b)
            if not first:
                w.out(b - 1)
        w.turn(0, 0)
        w.products(0, 0)
        slot(0, 0, first=True)
        slot(1, 1)
        with eng.Fori(0, (B - 4) // 2) as i:
            slot(2 * i + 2, 0)
            slot(2 * i + 3, 1)
        slot(B - 2, 0)
        slot(B - 1, 1, last=True)
        w.add(B - 2)
        w.centre(B - 1)
        w.vary(B - 1)
        w.norm(B - 1, 1)
        w.out(B - 1)
        w.add(B - 1)

    class Work:
        def add(self, b): pass
        def scores(self, b, z): pass
        def centre(self, b): pass
        def turn(self, b, z): pass
        def vary(self, b): pass
        def weigh(self, b, z): pass
        def norm(self, b, z): pass
        def products(self, b, z): pass
        def mean(self, b): pass
        def out(self, b): pass

    flat = lambda t: t.rearrange("p e t -> p (e t)")
    block = ctx.enter_context(nc.Block())

    @block.sync
    def _(sp):
        for i, n in enumerate("kvro"):
            sp.dma_start(w_stage[:, i], A[f"W{n}T"].rearrange("(k p) n -> p k n", p=P)).then_inc(done["loaded"], 16)
        for i, n in enumerate("kvr"):
            sp.dma_start(tm[:, i, :], A[f"tm_{n}"].rearrange("(k p) -> p k", p=P),
                         allow_slow_non_contiguous=True).then_inc(done["loaded"], 16)
        for t, n in ((decay, "time_decay"), (first, "time_first"), (gain, "ln_g"), (shift, "ln_b")):
            sp.dma_start(t[:], A[n].rearrange("(k p) -> p k", p=P), allow_slow_non_contiguous=True).then_inc(done["loaded"], 16)

    @block.tensor
    def _(pe):
        class PE(Work):
            def turn(self, b, z):
                pe.wait_ge(done["xn_ready"], b + 1)
                at_least(pe, done["xth"], b)
                at_least(pe, done["xtl"], b)
                for kb in range(KB):
                    for s in range(S):
                        last = pe.transpose(m.banks[:, 0, (kb * S + s) * P:(kb * S + s + 1) * P],
                                            xn[:, s, kb * P:(kb + 1) * P], m.ident[:])
                last.then_inc(done["xt_in_psum"], 1)

            def products(self, b, z):
                pe.wait_ge(done["xth"], b + 1)
                pe.wait_ge(done["xtl"], b + 1)
                at_least(pe, done["evac"], 3 * b)
                xt, w = (xt_hi, xt_lo), (w_hi, w_lo)
                for kind in range(3):
                    for eb in range(EB):
                        last = split_product(
                            pe, m.banks[:, 1 + kind, eb * T:(eb + 1) * T],
                            lambda a, j: w[a][:, kind, j // KB, j % KB, eb * P:(eb + 1) * P],
                            lambda a, j: xt[a][:, z, j % KB, 1 - j // KB:T + 1 - j // KB], 2 * KB)
                    last.then_inc(done["kvr_done"], 1)

            def mean(self, b):
                pe.wait_ge(done["wkv_done"], b + 1)
                at_least(pe, done["c_done"], b)
                for eb in range(EB):
                    last = pe.matmul(m.banks[:, 4, 0:T], mean_of[:], wkv[:, eb, :], start=(eb == 0), stop=(eb == EB - 1))
                last.then_inc(done["mean_done"], 1)

            def vary(self, b):
                pe.wait_ge(done["sq_done"], b + 1)
                at_least(pe, done["ve_done"], b)
                for s in range(S):
                    for eb in range(EB):
                        last = pe.matmul(m.banks[:, 5, s:s + 1], sq[:, eb, s * P:(s + 1) * P], mean_of[:, 0:1],
                                         start=(eb == 0), stop=(eb == EB - 1))
                last.then_inc(done["var_done"], 1)

            def norm(self, b, z):
                pe.wait_ge(done["rstd_done"], b + 1)
                at_least(pe, done["t_done"], b)
                for s in range(S):
                    last = pe.matmul(m.banks[:, 7, s * P:(s + 1) * P], rstd[:, s:s + 1].broadcast_to([P, P]), m.ident[:],
                                     start=True, stop=True)
                last.then_inc(done["spread"], 1)

            def out(self, b):
                pe.wait_ge(done["rwh"], b + 1)
                pe.wait_ge(done["rwl"], b + 1)
                at_least(pe, done["x_done"], b)
                r, w = (rw_hi, rw_lo), (wo_hi, wo_lo)
                for s in range(S):
                    last = split_product(pe, m.banks[:, 6, s * D:(s + 1) * D],
                                         lambda a, kb: r[a][:, kb, s * P:(s + 1) * P],
                                         lambda a, kb: w[a][:, kb, :], EB)
                last.then_inc(done["out_done"], 1)

        pe.wait_ge(done["wlo"], 2)
        schedule(pe, PE())

    @block.scalar
    def _(act):
        class Act(Work):
            def turn(self, b, z):
                act.wait_ge(done["xt_in_psum"], b + 1)
                at_least(act, done["kvr_done"], 3 * (b - 1))
                act.activation(xt_hi[:, z, :, 1:T + 1], m.banks[:, 0, :].rearrange("p (k t) -> p k t", k=KB),
                               ACT.Copy).then_inc(done["xth"], 1)

            def products(self, b, z):
                at_least(act, done["wkv_done"], b - 1)
                at_least(act, done["rw_done"], b - 1)
                for kind, (to, func, scale) in enumerate(((ks, ACT.Copy, 1.0), (vs, ACT.Copy, 1.0), (th, ACT.Tanh, 0.5))):
                    act.wait_ge(done["kvr_done"], 3 * b + kind + 1)
                    act.activation(flat(to[:, z]), m.banks[:, 1 + kind, :], func, scale=scale).then_inc(done["evac"], 1)

            def scores(self, b, z):
                act.wait_ge(done["less_done"], b + 1)
                at_least(act, done["wkv_done"], b)
                act.activation(ex[:], less[:], ACT.Exp).then_inc(done["exp_done"], 1)

            def centre(self, b):
                act.wait_ge(done["c_done"], b + 1)
                at_least(act, done["var_done"], b)
                act.activation(sq[:], c[:], ACT.Square).then_inc(done["sq_done"], 1)

            def norm(self, b, z):
                act.wait_ge(done["rw_done"], b + 1)
                at_least(act, done["out_done"], b)
                act.activation(rw_hi[:], rw[:], ACT.Copy).then_inc(done["rwh"], 1)

        act.preload_act_table(ACT.Exp)
        act.wait_ge(done["loaded"], 16 * 11)
        act.activation(grown[:], decay[:], ACT.Exp).then_inc(done["exp_decay"], 1)
        act.wait_ge(done["mixed"], 6)
        act.activation(w_hi[:], w_mixed[:], ACT.Copy)
        act.activation(wo_hi[:], w_stage[:, 3], ACT.Copy).then_inc(done["whi"], 1)
        schedule(act, Act())

    @block.vector
    def _(dve):
        class Dve(Work):
            def turn(self, b, z):
                at_least(dve, done["xt_in_psum"], b)
                for s in range(S):
                    at = bass.ds(S * b + s, 1)
                    last = dve.tensor_scalar(xn[:, s:s + 1, :], m.x_res[:, at, :], m.mv[:, at, 0],
                                             m.rstd[:, at], ALU.subtract, ALU.mult)
                last.then_inc(done["xn_ready"], 1)
                dve.wait_ge(done["xth"], b + 1)
                at_least(dve, done["kvr_done"], 3 * (b - 1))
                dve.tensor_tensor(xt_lo[:, z, :, 1:T + 1], m.banks[:, 0, :].rearrange("p (k t) -> p k t", k=KB),
                                  f32(xt_hi[:, z, :, 1:T + 1]), ALU.subtract).then_inc(done["xtl"], 1)

            def scores(self, b, z):
                dve.wait_ge(done["evac"], 3 * b + 3)
                at_least(dve, done["less_done"], b)
                for eb in range(EB):
                    last = dve.tensor_tensor_scan(top[:, eb, 1:T + 1], grown[:, eb:eb + 1].broadcast_to([P, T]),
                                                  ks[:, z, eb, :], NEVER, ALU.add, ALU.max)
                last.then_inc(done["top_done"], 1)
                dve.wait_ge(done["top_done"], b + 1)
                for eb in range(EB):
                    last = dve.scalar_tensor_tensor(out=dif[:, eb, :], in0=ks[:, z, eb, :], scalar=first[:, eb:eb + 1],
                                                    in1=top[:, eb, 0:T], op0=ALU.add, op1=ALU.subtract)
                last.then_inc(done["dif_done"], 1)
                at_least(dve, done["exp_done"], b)
                dve.tensor_tensor(less[:, 2], top[:, :, 0:T], top[:, :, 1:T + 1], ALU.subtract)
                dve.tensor_tensor(less[:, 3], ks[:, z], top[:, :, 1:T + 1], ALU.subtract)
                dve.wait_ge(done["dif_done"], b + 1)
                dve.tensor_scalar(less[:, 0], dif[:], 0.0, None, ALU.min)
                dve.tensor_scalar(less[:, 1], dif[:], -1.0, 0.0, ALU.mult, ALU.min).then_inc(done["less_done"], 1)

            def weigh(self, b, z):
                def then(ins, name):
                    ins.then_inc(done[name], 1)
                    dve.wait_ge(done[name], b + 1)

                dve.wait_ge(done["exp_done"], b + 1)
                then(dve.tensor_tensor(f2v[:], ex[:, 3], vs[:, z], ALU.mult), "f2v_done")
                for eb in range(EB):
                    dve.tensor_tensor_scan(aa[:, eb, 1:T + 1], ex[:, 2, eb, :], f2v[:, eb, :], 0.0, ALU.mult, ALU.add)
                for eb in range(EB):
                    last = dve.tensor_tensor_scan(bb[:, eb, 1:T + 1], ex[:, 2, eb, :], ex[:, 3, eb, :], 0.0, ALU.mult, ALU.add)
                then(last, "aa_done")
                dve.tensor_tensor(num[:], ex[:, 1], aa[:, :, 0:T], ALU.mult).then_inc(done["e1a_done"], 1)
                then(dve.tensor_tensor(den[:], ex[:, 1], bb[:, :, 0:T], ALU.mult), "e1b_done")
                then(dve.tensor_tensor(den[:], den[:], ex[:, 0], ALU.add), "den_done")
                dve.wait_ge(done["e2v_done"], b + 1)
                dve.tensor_tensor(num[:], num[:], e2v[:], ALU.add).then_inc(done["num_done"], 1)
                then(dve.reciprocal(rden[:], den[:]), "rden_done")
                at_least(dve, done["mean_done"], b)
                dve.tensor_tensor(wkv[:], num[:], rden[:], ALU.mult).then_inc(done["wkv_done"], 1)

            def centre(self, b):
                dve.wait_ge(done["mean_done"], b + 1)
                at_least(dve, done["sq_done"], b)
                dve.tensor_tensor(c[:], wkv[:], m.banks[:, 4, 0:T].unsqueeze(1).broadcast_to([P, EB, T]),
                                  ALU.subtract).then_inc(done["c_done"], 1)

            def vary(self, b):
                dve.wait_ge(done["var_done"], b + 1)
                at_least(dve, done["rstd_done"], b)
                dve.tensor_scalar(ve[:], m.banks[:, 5, 0:S], LN_EPS, None, ALU.add).then_inc(done["ve_done"], 1)

            def norm(self, b, z):
                dve.wait_ge(done["spread"], b + 1)
                dve.tensor_tensor(lnv[:], c[:], m.banks[:, 7, 0:T].unsqueeze(1).broadcast_to([P, EB, T]), ALU.mult).then_inc(done["t_done"], 1)
                dve.wait_ge(done["t_done"], b + 1)
                for eb in range(EB):
                    last = dve.tensor_scalar(lnv[:, eb, :], lnv[:, eb, :], gain[:, eb:eb + 1], shift[:, eb:eb + 1],
                                             ALU.mult, ALU.add)
                last.then_inc(done["ln_done"], 1)
                dve.wait_ge(done["ln_done"], b + 1)
                at_least(dve, done["rwh"], b)
                dve.scalar_tensor_tensor(out=flat(rw[:]), in0=flat(th[:, z]), scalar=1.0, in1=flat(lnv[:]),
                                         op0=ALU.add, op1=ALU.mult).then_inc(done["rw_done"], 1)
                dve.wait_ge(done["rwh"], b + 1)
                at_least(dve, done["out_done"], b)
                dve.tensor_tensor(rw_lo[:], rw[:], f32(rw_hi[:]), ALU.subtract).then_inc(done["rwl"], 1)

            def add(self, b):
                dve.wait_ge(done["out_done"], b + 1)
                two = m.x_res[:, bass.ds(S * b, S), :]
                dve.tensor_tensor(two, two, m.banks[:, 6, :].rearrange("p (s c) -> p s c", s=S), ALU.add).then_inc(done["x_done"], 1)
                dve.wait_ge(done["x_done"], b + 1)
                for s in range(S):
                    at = bass.ds(S * b + s, 1)
                    last = dve.bn_stats(m.bn6[:, at, :].rearrange("p a c -> p (a c)"),
                                        m.x_res[:, at, :].rearrange("p a c -> p (a c)"))
                last.then_inc(done["bn_done"], 1)

        dve.wait_ge(done["loaded"], 16 * 11)
        dve.tensor_scalar(tm_less[:], tm[:], -1.0, 1.0, ALU.mult, ALU.add).then_inc(done["prep"], 1)
        dve.tensor_scalar(gain[:], gain[:], 0.5, None, ALU.mult)
        dve.tensor_scalar(shift[:], shift[:], 0.5, None, ALU.mult).then_inc(done["prep"], 1)
        dve.wait_ge(done["exp_decay"], 1)
        dve.wait_ge(done["prep"], 2)
        dve.tensor_scalar(grown[:], grown[:], -1.0, None, ALU.mult).then_inc(done["prep"], 1)
        for kind in range(3):
            for kb in range(KB):
                dve.tensor_scalar(w_mixed[:, kind, 0, kb, :], w_stage[:, kind, kb, :], tm[:, kind, kb:kb + 1], None, ALU.mult)
                dve.tensor_scalar(w_mixed[:, kind, 1, kb, :], w_stage[:, kind, kb, :], tm_less[:, kind, kb:kb + 1], None,
                                  ALU.mult).then_inc(done["mixed"], 1)
        dve.wait_ge(done["whi"], 1)
        dve.tensor_tensor(w_lo[:], w_mixed[:], f32(w_hi[:]), ALU.subtract).then_inc(done["wlo"], 1)
        dve.tensor_tensor(wo_lo[:], w_stage[:, 3], f32(wo_hi[:]), ALU.subtract).then_inc(done["wlo"], 1)
        dve.wait_ge(done["edges"], 1)
        schedule(dve, Dve())
        dve.wait_ge(done["bn_done"], B)
        aggregate(dve, m, done["aggr_done"])
        dve.tensor_scalar(m.var_eps[:], m.mv[:, :, 1], LN_EPS, None, ALU.add).then_inc(done["eps_done"], 1)

    @block.gpsimd
    def _(pool):
        class Pool(Work):
            def vary(self, b):
                pool.wait_ge(done["ve_done"], b + 1)
                at_least(pool, done["spread"], b)
                pool.tensor_tensor(rstd[:], ve[:], m.neg_half[:, 0:S], ALU.pow).then_inc(done["rstd_done"], 1)

            def weigh(self, b, z):
                pool.wait_ge(done["exp_done"], b + 1)
                pool.wait_ge(done["evac"], 3 * b + 3)
                at_least(pool, done["num_done"], b)
                pool.tensor_tensor(e2v[:], ex[:, 0], vs[:, z], ALU.mult).then_inc(done["e2v_done"], 1)

        for part in (xt_hi, xt_lo):
            pool.memset(f32(part[:, :, :, 0]), 0.0)
        pool.memset(top[:, :, 0], NEVER)
        pool.memset(aa[:, :, 0], 0.0)
        pool.memset(mean_of[:], 1.0 / D)
        pool.memset(bb[:, :, 0], 0.0).then_inc(done["edges"], 1)
        pool.wait_ge(done["edges"], 1)
        schedule(pool, Pool())
        pool.wait_ge(done["eps_done"], 1)
        pool.tensor_tensor(m.rstd[:], m.var_eps[:], m.neg_half[:, 0:NT], ALU.pow).then_inc(done["next_rstd"], 1)


def build_program(nc, A, out):
    with ExitStack() as ctx:
        m = shared_memory(nc, ctx)
        with phase(nc) as scope:
            setup_phase(nc, m, A, scope)
        with phase(nc) as scope:
            attention_phase(nc, m, A, scope)
        mixture_layer(nc, m, {name[3:]: ap for name, ap in A.items() if name.startswith("f0_")},
                      Mixture("f0", 4, 512, "all", True, 1.0, 0))
        with phase(nc) as scope:
            rwkv_phase(nc, m, A, scope)
        mixture_layer(nc, m, {name[3:]: ap for name, ap in A.items() if name.startswith("f1_")},
                      Mixture("f1", 8, 256, "two", False, 1.702, 1), out)


@contextmanager
def phase(nc):
    before = nc.snapshot_sems()
    with ExitStack() as scope:
        yield scope
    nc.clear_and_free_semaphores(nc.allocated_since(before))
    nc.all_engine_barrier()


def mixture_layer(nc, m, A, v, out=None):
    with ExitStack() as layer:
        k = mixture_memory(nc, v, layer)
        with phase(nc) as scope:
            router_phase(nc, m, A, v, k, scope)
        with phase(nc) as scope:
            rank_phase(nc, m, v, k, scope)
        with phase(nc) as scope:
            expert_phase(nc, m, v, k, scope)
        with phase(nc) as scope:
            combine_phase(nc, m, A, v, k, scope, out)


def laid_out(inputs):
    i = {name: np.asarray(a) for name, a in inputs.items()}
    turned = lambda a: np.swapaxes(a, -1, -2)
    halves = lambda a: np.concatenate([a[:, 0::2], a[:, 1::2]], axis=1)
    a = {
        "L0_attn_x": i["L0_attn_x"].reshape(TOK, D),
        "L0_attn_W": i["L0_attn_W"], "L0_attn_WT": turned(i["L0_attn_W"]),
        "L0_attn_g1": i["L0_attn_g1"], "L0_attn_g2": i["L0_attn_g2"], "L0_attn_g3": i["L0_attn_g3"],
        "f0_gateT": turned(i["L0_ffn_gate_w"]),
        "f0_w13T": turned(np.concatenate([i["L0_ffn_w1"], i["L0_ffn_w3"]], axis=1)),
        "f0_w2T": turned(i["L0_ffn_w2"]),
        "f0_s13T": turned(np.concatenate([i["L0_ffn_sw1"], i["L0_ffn_sw3"]], axis=0)),
        "f0_s2T": turned(i["L0_ffn_sw2"]),
        "f1_gateT": turned(i["L1_ffn_gate_w"]), "f1_gate_b": i["L1_ffn_gate_b"],
        "f1_w13T": turned(halves(i["L1_ffn_w1"])), "f1_w2T": turned(i["L1_ffn_w2"]),
        "f1_b1": halves(i["L1_ffn_b1"]), "f1_b2": i["L1_ffn_b2"],
    }
    for n in "kvro":
        a[f"W{n}T"] = turned(i[f"L1_attn_W{n}"])
    for n in ("tm_k", "tm_v", "tm_r", "time_decay", "time_first", "ln_g", "ln_b"):
        a[n] = i[f"L1_attn_{n}"].reshape(D)
    return {name: np.ascontiguousarray(v) for name, v in a.items()}


def kernel(**inputs):
    import concourse.bacc as bacc
    from concourse.bass_utils import run_bass_kernel_spmd

    arrays = {f"in_{name}": a for name, a in laid_out(inputs).items()}
    nc = bacc.Bacc("TRN2", target_bir_lowering=False, num_devices=1)
    A = {name[3:]: nc.dram_tensor(name, a.shape, mybir.dt.from_np(a.dtype), kind="ExternalInput").ap()
         for name, a in arrays.items()}
    out = nc.dram_tensor("out_x", (TOK, D), F32, kind="ExternalOutput").ap()
    build_program(nc, A, out)
    result = run_bass_kernel_spmd(nc, [arrays], core_ids=[0])
    return result.results[0]["out_x"].reshape(B, T, D)
```

```python
from contextlib import ExitStack, contextmanager

import numpy as np

import concourse.bass as bass
from concourse import mybir

ALU = mybir.AluOpType
ACT = mybir.ActivationFunctionType
F32 = mybir.dt.float32
F32R = mybir.dt.float32r
AX_X = mybir.AxisListType.X

P = 128
B, T, D = 8, 256, 256
TOK = B * T
NT = TOK // P
KB = D // P
S = T // P
NH, DH = 16, 16
NP = NH // 2
LN_EPS = 1e-5
RMS_EPS = 1.1920928955078125e-07


def f32(ap):
    return ap.bitcast(F32)


def at_least(eng, semaphore, value):
    if not (isinstance(value, int) and value <= 0):
        eng.wait_ge(semaphore, value)


def upto(value, most):
    return min(value, most) if isinstance(value, int) else value


def split_product(pe, out, lhs, rhs, k_blocks):
    steps = [(a, c, k) for k in range(k_blocks) for a, c in ((0, 0), (0, 1), (1, 0))]
    for n, (a, c, k) in enumerate(steps):
        last = pe.matmul(out, lhs(a, k), rhs(c, k), start=(n == 0), stop=(n == len(steps) - 1))
    return last


def aggregate(dve, m, aggr_done):
    for t in range(NT):
        last = dve.bn_aggr(m.mv[:, t, :], m.bn6[:, t, :])
    last.then_inc(aggr_done, 1)
    dve.wait_ge(aggr_done, 1)


class Names:
    pass


def shared_memory(nc, ctx):
    m = Names()
    sb = lambda name, shape, dt=F32: ctx.enter_context(nc.sbuf_tensor(name, shape, dt))
    m.x_res = sb("x_res", [P, NT, D])
    m.ident = sb("ident", [P, P])
    m.bn6 = sb("bn6", [P, NT, 6])
    m.mv = sb("mv", [P, NT, 2])
    m.var_eps = sb("var_eps", [P, NT])
    m.rstd = sb("rstd", [P, NT])
    m.neg_half = sb("neg_half", [P, 512])
    m.upper = sb("upper", [P, P])
    m.ones = sb("ones", [P, P])
    m.ones_r = sb("ones_r", [P, P], F32R)
    m.count_up = sb("count_up", [P, P])
    m.group_starts = sb("group_starts", [P, NT])
    m.token = sb("token", [P, 2 * NT])
    m.neg_row = sb("neg_row", [P, 1])
    m.expert_less = {tag: sb(f"expert_less_{tag}", [P, e]) for tag, e in (("f0", 4), ("f1", 8))}
    m.banks = ctx.enter_context(nc.psum_tensor("banks", [P, 8, 512], F32))
    return m


def setup_phase(nc, m, A, ctx):
    I32 = mybir.dt.int32
    ints = {n: ctx.enter_context(nc.sbuf_tensor(f"int_{n}", [P, w], I32)) for n, w in
            (("count_up", P), ("group_starts", NT), ("token", 2 * NT), ("neg_row", 1), ("f0", 4), ("f1", 8))}
    iota_done = nc.alloc_semaphore("iota_done")
    upper_ready = nc.alloc_semaphore("upper_ready")
    x_here, id_zero, id_ready, half_ready, bn_done, aggr_done, eps_done, rstd_done = (
        nc.alloc_semaphore(n) for n in
        ("x_here", "id_zero", "id_ready", "half_ready", "bn_done", "aggr_done", "eps_done", "rstd_done"))
    block = ctx.enter_context(nc.Block())

    @block.sync
    def _(sp):
        x_tiles = A["L0_attn_x"].rearrange("(t p) d -> p t d", p=P)
        for half in range(2):
            sp.dma_start(m.x_res[:, half * NT // 2:(half + 1) * NT // 2, :],
                         x_tiles[:, half * NT // 2:(half + 1) * NT // 2, :]).then_inc(x_here, 16)

    @block.gpsimd
    def _(pool):
        pool.memset(m.ident[:], 0.0).then_inc(id_zero, 1)
        pool.memset(m.neg_half[:], -0.5).then_inc(half_ready, 1)
        pool.wait_ge(id_zero, 1)
        pool.affine_select(out=m.ident[:], in_=m.ident[:], compare_op=ALU.not_equal, fill=1.0, base=0,
                           pattern=[[-1, P]], channel_multiplier=1).then_inc(id_ready, 1)
        pool.memset(m.ones[:], 1.0).then_inc(upper_ready, 1)
        pool.wait_ge(upper_ready, 1)
        pool.affine_select(out=m.upper[:], in_=m.ones[:], compare_op=ALU.is_ge, fill=0.0, base=-1,
                           pattern=[[1, P]], channel_multiplier=-1).then_inc(upper_ready, 1)
        pool.iota(ints["count_up"][:], [[1, P]], base=0, channel_multiplier=0).then_inc(iota_done, 1)
        pool.iota(ints["group_starts"][:], [[S * P, NT]], base=0, channel_multiplier=0).then_inc(iota_done, 1)
        pool.iota(ints["token"][:], [[0, 2], [P, NT]], base=0, channel_multiplier=1).then_inc(iota_done, 1)
        pool.iota(ints["neg_row"][:], [[0, 1]], base=0, channel_multiplier=-1).then_inc(iota_done, 1)
        pool.iota(ints["f0"][:], [[1, 4]], base=-4, channel_multiplier=0).then_inc(iota_done, 1)
        pool.iota(ints["f1"][:], [[1, 8]], base=-8, channel_multiplier=0).then_inc(iota_done, 1)
        pool.wait_ge(half_ready, 1)
        pool.wait_ge(eps_done, 1)
        pool.tensor_tensor(m.rstd[:], m.var_eps[:], m.neg_half[:, 0:NT], ALU.pow).then_inc(rstd_done, 1)

    @block.vector
    def _(dve):
        dve.wait_ge(iota_done, 6)
        dve.wait_ge(upper_ready, 1)
        for name, to in (("count_up", m.count_up), ("group_starts", m.group_starts), ("token", m.token),
                         ("neg_row", m.neg_row), ("f0", m.expert_less["f0"]), ("f1", m.expert_less["f1"])):
            dve.tensor_copy(to[:], ints[name][:])
        dve.tensor_copy(m.ones_r[:], m.ones[:])
        dve.wait_ge(x_here, 32)
        for t in range(NT):
            last = dve.bn_stats(m.bn6[:, t, :], m.x_res[:, t, :])
        last.then_inc(bn_done, 1)
        dve.wait_ge(bn_done, 1)
        aggregate(dve, m, aggr_done)
        dve.tensor_scalar(m.var_eps[:], m.mv[:, :, 1], LN_EPS, None, ALU.add).then_inc(eps_done, 1)


def attention_phase(nc, m, A, ctx):
    sb = lambda name, shape, dt=F32: ctx.enter_context(nc.sbuf_tensor(name, shape, dt))
    sem = lambda name: nc.alloc_semaphore(name)
    w_stage = sb("a_w_stage", [P, KB, D])
    wt_stage = sb("a_wt_stage", [P, KB, D])
    w_hi, w_lo = sb("a_w_hi", [P, KB, D], F32R), sb("a_w_lo", [P, KB, D], F32R)
    wt_hi, wt_lo = sb("a_wt_hi", [P, KB, D], F32R), sb("a_wt_lo", [P, KB, D], F32R)
    g1, g2, g3, gq = sb("g1", [P, DH]), sb("g2", [P, DH]), sb("g3", [P, DH]), sb("gq", [P, DH])
    xn = sb("a_xn", [P, S, D])
    xt_hi, xt_lo = sb("a_xt_hi", [P, KB * S * P], F32R), sb("a_xt_lo", [P, KB * S * P], F32R)
    sq = sb("a_sq", [P, S * NH, DH])
    ms, ms_eps, rr = sb("a_ms", [P, S * NH]), sb("a_ms_eps", [P, S * NH]), sb("a_rr", [P, S * NH])
    u, q = sb("a_u", [P, S * NH, DH]), sb("a_q", [P, S * NH, DH])
    qst, kst = sb("a_qst", [P, 2, S * NH, 4, DH], F32R), sb("a_kst", [P, 2, S * NH, 4, DH], F32R)
    vv = sb("a_vv", [P, 2, S * NH, 2, DH])
    qkt = sb("a_qkt", [P, 2, 4 * P], F32R)
    ebuf = sb("a_e", [P, 4, 4, T])
    ssum, rs = sb("a_ssum", [P, 2, NH * S]), sb("a_rs", [P, 2, NH * S])
    outt = sb("a_outt", [P, 2, T])
    ytmp, ytok = sb("a_ytmp", [P, S, 4, DH]), sb("a_ytok", [P, S, D])
    yt_hi, yt_lo = sb("a_yt_hi", [P, KB * S * P], F32R), sb("a_yt_lo", [P, KB * S * P], F32R)

    (loaded, gaps_zero, w_copied, w_split, gq_half, gq_ready, xn_ready, xt_in_psum, xth, xtl, w_ready, sq_done,
     ms_done, mse_done, rr_ready, u_ready, kh_done, kst_ready, q_done, qh_done, qst_ready, v_ready, qk_in_psum,
     qkt_ready, s_ready, exp_done, sum_done, rs_done, vr_ready, av_done, outt_ready, yraw_in_psum, ytmp_done,
     ytok_done, yt_in_psum, yth, ytl, proj_done, x1_done, bn_done, aggr_done, eps_done, rstd_done) = (
        sem("a_" + n) for n in
        "loaded gaps_zero w_copied w_split gq_half gq_ready xn_ready xt_in_psum xth xtl w_ready sq_done "
        "ms_done mse_done rr_ready u_ready kh_done kst_ready q_done qh_done qst_ready v_ready qk_in_psum "
        "qkt_ready s_ready exp_done sum_done rs_done vr_ready av_done outt_ready yraw_in_psum ytmp_done "
        "ytok_done yt_in_psum yth ytl proj_done x1_done bn_done aggr_done eps_done rstd_done".split())

    tr = m.banks[:, 0, :]
    proj = m.banks[:, 1, :]
    qkp = m.banks[:, 2, :]
    av = m.banks[:, 3, :].rearrange("p (g t) -> p g t", g=2)
    scores = m.banks[:, 4:8, :].rearrange("p (r h) (s t) -> p r h s t", r=2, s=S)

    def schedule(eng, w):
        def batch(b, z, first=False, last=False):
            for p in range(NP):
                if not last and p == 0:
                    w.prepare_0(b + 1, 1 - z)
                if not last and p == 1:
                    w.prepare_1(b + 1, 1 - z)
                if not (last and p == NP - 1):
                    w.ahead(b, p + 1, z) if p < NP - 1 else w.ahead(b + 1, 0, 1 - z)
                w.now(b, p, z)
                if p > 0:
                    w.late(b, p - 1, z)
                elif not first:
                    w.late(b - 1, NP - 1, 1 - z)
                if not (last and p == NP - 1):
                    w.score(b, p + 1, z) if p < NP - 1 else w.score(b + 1, 0, 1 - z)
                if p in (3, 5, 7):
                    w.rows(b, (p - 3) // 2, z)
                if p == 1 and not first:
                    w.rows(b - 1, 3, 1 - z)
                if p == 2 and not first:
                    w.turn(b - 1)
                if p == 4 and not first:
                    w.project(b - 1)
                if not last and p == 0:
                    w.prepare_0_end(b + 1)
                if not last and p == 1:
                    w.prepare_1_end(b + 1)
                if not last and p == 2:
                    w.prepare_2(b + 1)
                if not last and p == 3:
                    w.prepare_3(b + 1, 1 - z)

        w.prepare_0(0, 0)
        w.prepare_0_end(0)
        w.prepare_1(0, 0)
        w.prepare_1_end(0)
        w.prepare_2(0)
        w.prepare_3(0, 0)
        w.ahead(0, 0, 0)
        w.score(0, 0, 0)
        batch(0, 0, first=True)
        with eng.Fori(0, (B - 2) // 2) as i:
            batch(2 * i + 1, 1)
            batch(2 * i + 2, 0)
        batch(B - 1, 1, last=True)
        w.late(B - 1, NP - 1, 1)
        w.rows(B - 1, 3, 1)
        w.turn(B - 1)
        w.project(B - 1)

    class Work:
        def prepare_0(self, b, z): pass
        def prepare_0_end(self, b): pass
        def prepare_1(self, b, z): pass
        def prepare_1_end(self, b): pass
        def prepare_2(self, b): pass
        def prepare_3(self, b, z): pass
        def ahead(self, b, p, z): pass
        def now(self, b, p, z): pass
        def score(self, b, p, z): pass
        def late(self, b, p, z): pass
        def rows(self, b, g, z): pass
        def turn(self, b): pass
        def project(self, b): pass

    block = ctx.enter_context(nc.Block())

    @block.sync
    def _(sp):
        sp.dma_start(wt_stage[:], A["L0_attn_WT"].rearrange("(k p) n -> p k n", p=P)).then_inc(loaded, 16)
        sp.dma_start(w_stage[:], A["L0_attn_W"].rearrange("(k p) n -> p k n", p=P)).then_inc(loaded, 16)
        for g, name in ((g1, "L0_attn_g1"), (g2, "L0_attn_g2"), (g3, "L0_attn_g3")):
            sp.dma_start(g[:], A[name].rearrange("(o d) -> o d", o=1).broadcast_to([P, DH])).then_inc(loaded, 16)

    @block.tensor
    def _(pe):
        class PE(Work):
            def prepare_0_end(self, b):
                pe.wait_ge(xn_ready, b + 1)
                at_least(pe, ytok_done, 4 * b - 5)
                for k in range(KB):
                    for s in range(S):
                        last = pe.transpose(tr[:, (k * S + s) * P:(k * S + s + 1) * P],
                                            xn[:, s, k * P:(k + 1) * P], m.ident[:])
                last.then_inc(xt_in_psum, 1)

            def prepare_1_end(self, b):
                pe.wait_ge(xth, b + 1)
                pe.wait_ge(xtl, b + 1)
                at_least(pe, x1_done, b - 2)
                xt, wt = (xt_hi, xt_lo), (wt_hi, wt_lo)
                for s in range(S):
                    last = split_product(
                        pe, proj[:, s * D:(s + 1) * D],
                        lambda a, k: xt[a][:, (k * S + s) * P:(k * S + s + 1) * P],
                        lambda a, k: wt[a][:, k, :], KB)
                last.then_inc(w_ready, 1)

            def ahead(self, b, p, z):
                n = NP * b + p
                if p == 0:
                    pe.wait_ge(kst_ready, b + 1)
                    pe.wait_ge(qst_ready, b + 1)
                at_least(pe, qkt_ready, n)
                for j, st in enumerate((qst, kst)):
                    for s in range(S):
                        rows = st[:, z, s * NH + 2 * p:s * NH + 2 * p + 2, :, :]
                        last = pe.transpose(qkp[:, (2 * j + s) * P:(2 * j + s + 1) * P],
                                            f32(rows.rearrange("p h r d -> p (h r d)")), m.ident[:])
                last.then_inc(qk_in_psum, 1)

            def score(self, b, p, z):
                n = NP * b + p
                pe.wait_ge(qkt_ready, n + 1)
                at_least(pe, exp_done, n - 1)
                for h in range(2):
                    for s in range(S):
                        last = pe.matmul(scores[:, p % 2, h, s, :],
                                         qkt[64 * h:64 * h + 3 * DH, p % 2, s * P:(s + 1) * P],
                                         qkt[64 * h:64 * h + 3 * DH, p % 2, 2 * P:4 * P], start=True, stop=True)
                last.then_inc(s_ready, 1)

            def late(self, b, p, z):
                pe.wait_ge(vr_ready, NP * b + p + 1)
                if p % 2 == 0:
                    at_least(pe, outt_ready, 4 * b + p // 2)
                for s in range(S):
                    for h in range(2):
                        row = 32 * (2 * (p % 2) + h)
                        last = pe.matmul(av[row:row + 32, p // 2 % 2, :],
                                         vv[:, z, s * NH + 2 * p + h, :, :].rearrange("p r d -> p (r d)"),
                                         ebuf[:, p % 4, 2 * h + s, :], start=(s == 0), stop=(s == S - 1),
                                         skip_group_check=True)
                last.then_inc(av_done, 1)

            def rows(self, b, g, z):
                pe.wait_ge(outt_ready, 4 * b + g + 1)
                if g == 0:
                    at_least(pe, yth, b)
                    at_least(pe, ytl, b)
                else:
                    pe.wait_ge(ytok_done, 4 * b + g)
                if g == 3:
                    pe.wait_ge(xth, upto(b + 3, B))
                    pe.wait_ge(xtl, upto(b + 3, B))
                for s in range(S):
                    last = pe.transpose(tr[:, (g % 2 * S + s) * P:(g % 2 * S + s + 1) * P],
                                        outt[:, g % 2, s * P:(s + 1) * P], m.ident[:])
                last.then_inc(yraw_in_psum, 1)

            def turn(self, b):
                pe.wait_ge(ytok_done, 4 * b + 4)
                for k in range(KB):
                    for s in range(S):
                        last = pe.transpose(tr[:, (k * S + s) * P:(k * S + s + 1) * P],
                                            ytok[:, s, k * P:(k + 1) * P], m.ident[:])
                last.then_inc(yt_in_psum, 1)

            def project(self, b):
                pe.wait_ge(yth, b + 1)
                pe.wait_ge(ytl, b + 1)
                pe.wait_ge(u_ready, upto(b + 3, B))
                pe.wait_ge(sq_done, upto(b + 3, B))
                yt, w = (yt_hi, yt_lo), (w_hi, w_lo)
                for s in range(S):
                    last = split_product(
                        pe, proj[:, s * D:(s + 1) * D],
                        lambda a, k: yt[a][:, (k * S + s) * P:(k * S + s + 1) * P],
                        lambda a, k: w[a][:, k, :], KB)
                last.then_inc(proj_done, 1)

        pe.wait_ge(w_split, 2)
        schedule(pe, PE())

    @block.scalar
    def _(act):
        class Act(Work):
            def prepare_1(self, b, z):
                act.wait_ge(xt_in_psum, b + 1)
                at_least(act, w_ready, b)
                act.activation(xt_hi[:], tr, ACT.Copy).then_inc(xth, 1)

            def prepare_2(self, b):
                act.wait_ge(w_ready, b + 1)
                at_least(act, ms_done, b)
                act.activation(sq[:].rearrange("p h d -> p (h d)"), proj, ACT.Square).then_inc(sq_done, 1)

            def ahead(self, b, p, z):
                n = NP * b + p
                act.wait_ge(qk_in_psum, n + 1)
                at_least(act, s_ready, n - 1)
                act.activation(qkt[:, p % 2, :], qkp, ACT.Copy).then_inc(qkt_ready, 1)

            def late(self, b, p, z):
                if p % 2 == 1:
                    self.copy_group(b, p // 2)

            def score(self, b, p, z):
                n = NP * b + p
                act.wait_ge(s_ready, n + 1)
                at_least(act, av_done, n - 3)
                at_least(act, sum_done, n - 3)
                act.activation(ebuf[:, p % 4, :, :],
                               scores[:, p % 2, :, :, :].rearrange("p h s t -> p (h s) t"),
                               ACT.Exp).then_inc(exp_done, 1)

            def copy_group(self, b, g):
                act.wait_ge(av_done, NP * b + 2 * g + 2)
                at_least(act, yraw_in_psum, 4 * b + g - 1)
                act.activation(outt[:, g % 2, :], av[:, g % 2, :], ACT.Copy).then_inc(outt_ready, 1)

            def turn(self, b):
                act.wait_ge(yt_in_psum, b + 1)
                at_least(act, proj_done, b)
                act.activation(yt_hi[:], tr, ACT.Copy).then_inc(yth, 1)

        act.preload_act_table(ACT.Exp)


        schedule(act, Act())

    @block.vector
    def _(dve):
        class Dve(Work):
            def prepare_0(self, b, z):
                at_least(dve, xt_in_psum, b)
                for s in range(S):
                    at = bass.ds(S * b + s, 1)
                    last = dve.tensor_scalar(xn[:, s:s + 1, :], m.x_res[:, at, :], m.mv[:, at, 0],
                                             m.rstd[:, at], ALU.subtract, ALU.mult)
                last.then_inc(xn_ready, 1)

            def prepare_1(self, b, z):
                dve.wait_ge(xth, b + 1)
                at_least(dve, w_ready, b)
                dve.tensor_tensor(xt_lo[:], tr, f32(xt_hi[:]), ALU.subtract).then_inc(xtl, 1)

            def prepare_2(self, b):
                dve.wait_ge(sq_done, b + 1)
                at_least(dve, mse_done, b)
                dve.tensor_reduce(ms[:], sq[:], AX_X, ALU.add).then_inc(ms_done, 1)
                dve.wait_ge(ms_done, b + 1)
                at_least(dve, rr_ready, b)
                dve.tensor_scalar(ms_eps[:], ms[:], 1.0 / DH, RMS_EPS, ALU.mult, ALU.add).then_inc(mse_done, 1)

            def prepare_3(self, b, z):
                dve.wait_ge(rr_ready, b + 1)
                at_least(dve, q_done, b)
                at_least(dve, v_ready, b)
                at_least(dve, kst_ready, b)
                dve.tensor_tensor(u[:], proj.rearrange("p (h d) -> p h d", d=DH),
                                  rr[:].unsqueeze(2).broadcast_to([P, S * NH, DH]), ALU.mult).then_inc(u_ready, 1)
                dve.wait_ge(u_ready, b + 1)
                at_least(dve, qk_in_psum, NP * (b - 1))
                dve.tensor_copy(kst[:, z, :, 0:3:2, :],
                                u[:].unsqueeze(2).broadcast_to([P, S * NH, 2, DH])).then_inc(kh_done, 1)
                dve.wait_ge(kh_done, b + 1)
                dve.tensor_tensor(kst[:, z, :, 1, :], u[:], f32(kst[:, z, :, 0, :]), ALU.subtract).then_inc(kst_ready, 1)

            def now(self, b, p, z):
                n = NP * b + p
                dve.wait_ge(exp_done, n + 1)
                dve.tensor_reduce(ssum[:, z, 4 * p:4 * p + 4], ebuf[:, p % 4, :, :], AX_X, ALU.add).then_inc(sum_done, 1)
                dve.wait_ge(sum_done, n + 1)
                dve.reciprocal(rs[:, z, 4 * p:4 * p + 4], ssum[:, z, 4 * p:4 * p + 4]).then_inc(rs_done, 1)
                dve.wait_ge(rs_done, n + 1)
                if p == 0:
                    dve.wait_ge(v_ready, b + 1)
                v2 = vv[:, z, :, :, :].rearrange("p (s h) r d -> p s h r d", s=S)[:, :, 2 * p:2 * p + 2, :, :]
                r2 = rs[:, z, 4 * p:4 * p + 4].rearrange("p (h s) -> p s h", s=S)
                dve.tensor_tensor(v2[:, :, :, 1, :], v2[:, :, :, 0, :],
                                  r2.unsqueeze(3).broadcast_to([P, S, 2, DH]), ALU.mult).then_inc(vr_ready, 1)

            def rows(self, b, g, z):
                dve.wait_ge(yraw_in_psum, 4 * b + g + 1)
                at_least(dve, ytok_done, 4 * b + g)
                raw = tr[:, g % 2 * S * P:(g % 2 + 1) * S * P].rearrange("p (s h r d) -> p s h r d", s=S, h=4, r=2)
                r4 = rs[:, z, 4 * g * S:4 * (g + 1) * S].rearrange("p (h s) -> p s h", s=S)
                dve.tensor_tensor(ytmp[:], raw[:, :, :, 0, :], r4.unsqueeze(3).broadcast_to([P, S, 4, DH]),
                                  ALU.mult).then_inc(ytmp_done, 1)
                dve.wait_ge(ytmp_done, 4 * b + g + 1)
                if g == 0:
                    at_least(dve, yt_in_psum, b)
                dve.tensor_tensor(ytok[:, :, 4 * g * DH:4 * (g + 1) * DH].rearrange("p s (h d) -> p s h d", d=DH),
                                  raw[:, :, :, 1, :], ytmp[:], ALU.add).then_inc(ytok_done, 1)

            def turn(self, b):
                dve.wait_ge(yth, b + 1)
                at_least(dve, proj_done, b)
                dve.tensor_tensor(yt_lo[:], tr, f32(yt_hi[:]), ALU.subtract).then_inc(ytl, 1)

            def project(self, b):
                dve.wait_ge(proj_done, b + 1)
                two = m.x_res[:, bass.ds(S * b, S), :]
                dve.tensor_tensor(two, two, proj.rearrange("p (s c) -> p s c", s=S), ALU.add).then_inc(x1_done, 1)
                dve.wait_ge(x1_done, b + 1)
                for s in range(S):
                    at = bass.ds(S * b + s, 1)
                    last = dve.bn_stats(m.bn6[:, at, :].rearrange("p a c -> p (a c)"),
                                        m.x_res[:, at, :].rearrange("p a c -> p (a c)"))
                last.then_inc(bn_done, 1)

        schedule(dve, Dve())
        dve.wait_ge(bn_done, B)
        aggregate(dve, m, aggr_done)
        dve.tensor_scalar(m.var_eps[:], m.mv[:, :, 1], LN_EPS, None, ALU.add).then_inc(eps_done, 1)

    @block.gpsimd
    def _(pool):
        class Pool(Work):
            def prepare_2(self, b):
                pool.wait_ge(mse_done, b + 1)
                at_least(pool, u_ready, b)
                pool.tensor_tensor(rr[:], ms_eps[:], m.neg_half[:, 0:S * NH], ALU.pow).then_inc(rr_ready, 1)

            def prepare_3(self, b, z):
                wide = lambda g: g[:].unsqueeze(1).broadcast_to([P, S * NH, DH])
                pool.wait_ge(u_ready, b + 1)
                at_least(pool, qst_ready, b)
                pool.tensor_tensor(q[:], u[:], wide(gq), ALU.mult).then_inc(q_done, 1)
                at_least(pool, av_done, NP * (b - 1))
                pool.tensor_tensor(vv[:, z, :, 0, :], u[:], wide(g3), ALU.mult).then_inc(v_ready, 1)
                at_least(pool, qk_in_psum, NP * (b - 1))
                two = lambda ap, n: ap.unsqueeze(n).broadcast_to([P, S * NH, 2, DH])
                pool.tensor_tensor(qst[:, z, :, 0:2, :], two(u[:], 2),
                                   two(gq[:].unsqueeze(1), 1), ALU.mult).then_inc(qh_done, 1)
                pool.wait_ge(q_done, b + 1)
                pool.wait_ge(qh_done, b + 1)
                pool.tensor_tensor(qst[:, z, :, 2, :], q[:], f32(qst[:, z, :, 0, :]), ALU.subtract).then_inc(qst_ready, 1)

        pool.wait_ge(loaded, 80)
        for i, (stage, hi) in enumerate(((wt_stage, wt_hi), (w_stage, w_hi))):
            last = pool.tensor_copy(hi[:], stage[:])
        last.then_inc(w_copied, 1)
        pool.wait_ge(w_copied, 1)
        for stage, hi, lo in ((wt_stage, wt_hi, wt_lo), (w_stage, w_hi, w_lo)):
            pool.tensor_tensor(lo[:], stage[:], f32(hi[:]), ALU.subtract).then_inc(w_split, 1)
        pool.memset(f32(qst[:, :, :, 3, :]), 0.0)
        pool.memset(f32(kst[:, :, :, 3, :]), 0.0).then_inc(gaps_zero, 1)
        pool.tensor_tensor(gq[:], g1[:], g2[:], ALU.mult).then_inc(gq_half, 1)
        pool.wait_ge(gq_half, 1)
        pool.tensor_scalar(gq[:], gq[:], float(DH) ** -0.5, None, ALU.mult).then_inc(gq_ready, 1)
        pool.wait_ge(gq_ready, 1)
        pool.wait_ge(gaps_zero, 1)
        schedule(pool, Pool())
        pool.wait_ge(eps_done, 1)
        pool.tensor_tensor(m.rstd[:], m.var_eps[:], m.neg_half[:, 0:NT], ALU.pow).then_inc(rstd_done, 1)


class Mixture:
    def __init__(self, tag, experts, hidden, gated, shared, slope, lin_bias):
        self.tag, self.experts, self.hidden, self.shared = tag, experts, hidden, shared
        self.gated = gated
        self.slope = slope
        self.lin_bias = lin_bias
        self.groups = NT + experts - 1
        self.tiles = S * self.groups
        self.hb = hidden // P


def mixture_memory(nc, v, ctx):
    k = Names()
    sb = lambda name, shape, dt=F32: ctx.enter_context(nc.sbuf_tensor(f"{v.tag}_{name}", shape, dt))
    k.w13_hi, k.w13_lo = (sb(n, [P, v.experts, KB, 2 * v.hidden], F32R) for n in ("w13_hi", "w13_lo"))
    k.w2_hi, k.w2_lo = (sb(n, [P, v.experts, v.hb, D], F32R) for n in ("w2_hi", "w2_lo"))
    k.logits = sb("logits", [P, v.experts, NT])
    k.weight = sb("weight", [P, 2, NT])
    k.pos = sb("pos", [P, 2, NT], mybir.dt.int32)
    k.token_of = sb("token_of", [P, v.tiles], mybir.dt.int32)
    k.expert_of = sb("expert_of", [P, v.groups], mybir.dt.int32)
    if v.lin_bias:
        k.b1, k.b2 = sb("b1", [2, v.experts, 2 * v.hidden], F32R), sb("b2", [2, v.experts, D], F32R)
    k.xn_dram = nc.dram_tensor(f"{v.tag}_xn", [TOK, D], F32).ap()
    k.y_dram = nc.dram_tensor(f"{v.tag}_y", [v.tiles * P, D], F32).ap()
    return k


def router_phase(nc, m, A, v, k, ctx):
    E, HS = v.experts, 256
    HSB = HS // P
    sb = lambda name, shape, dt=F32: ctx.enter_context(nc.sbuf_tensor(f"{v.tag}r_{name}", shape, dt))
    sem = lambda name: nc.alloc_semaphore(f"{v.tag}r_{name}")
    xn = sb("xn", [P, 2, S, D])
    xt_hi, xt_lo = sb("xt_hi", [P, 2, KB, S * P], F32R), sb("xt_lo", [P, 2, KB, S * P], F32R)
    gate_stage = sb("gate_stage", [P, KB, E])
    gate_hi, gate_lo = sb("gate_hi", [P, KB, E], F32R), sb("gate_lo", [P, KB, E], F32R)
    gate_b = sb("gate_b", [P, E])
    w_shapes = ((KB, 2 * v.hidden), (v.hb, D))
    w_kinds = ((0,), (1,)) if 2 * E == B else ((0, 1), (0, 1))
    stages = {(kind, z): sb(f"stage{kind}{z}", [P, *w_shapes[kind]]) for z in range(2) for kind in w_kinds[z]}
    if v.shared:
        s13_hi, s13_lo = sb("s13_hi", [P, KB, 2 * HS], F32R), sb("s13_lo", [P, KB, 2 * HS], F32R)
        s13_stage, s2_stage = sb("s13_stage", [P, KB, 2 * HS]), sb("s2_stage", [P, HSB, D])
        s2_hi, s2_lo = sb("s2_hi", [P, HSB, D], F32R), sb("s2_lo", [P, HSB, D], F32R)
        th, s1, h = (sb(n, [P, 2, HSB * S * P]) for n in ("th", "s1", "h"))
        h_hi, h_lo = sb("h_hi", [P, 2, HSB, S * P], F32R), sb("h_lo", [P, 2, HSB, S * P], F32R)
    if v.lin_bias:
        bias_stage1, bias_stage2 = sb("bias1", [2, E, 2 * v.hidden]), sb("bias2", [2, E, D])

    (small_here, shared_here, xn_ready, stored0, stored1, xt_in_psum, xth, xtl, lg_in_psum, lg_done, up_done,
     th_done, s1_done, h_done, hh_done, hl_done, down_done, added, hi_done, lo_done, gate_done, bias_done) = (
        sem(n) for n in
        "small_here shared_here xn_ready stored0 stored1 xt_in_psum xth xtl lg_in_psum lg_done up_done "
        "th_done s1_done h_done hh_done hl_done down_done added hi_done lo_done gate_done bias_done".split())
    stage_here, w_hi_done, w_lo_done = ({key: sem(f"{n}{key[0]}{key[1]}") for key in stages}
                                        for n in ("stage_here", "w_hi_done", "w_lo_done"))
    stored = (stored0, stored1)
    if not v.shared:
        up_done = lg_in_psum
    w_dram = (A["w13T"].rearrange("e (k p) n -> p e k n", p=P), A["w2T"].rearrange("e (k p) n -> p e k n", p=P))
    w_parts = ((k.w13_hi, k.w13_lo), (k.w2_hi, k.w2_lo))
    expert_at = lambda c, half: bass.ds(half if 2 * E == B else c, 1)
    one = lambda ap: ap.rearrange("p o k n -> p (o k) n")

    C = B

    def schedule(eng, w):
        def slot(c, z, half):
            at = c if isinstance(c, int) else 1
            if v.shared and at > 0:
                w.second_h(c - 1, 1 - z)
            if at < C - 2:
                w.norm(c + 2, z, half + 1)
            if at < C - 1:
                w.turn(c + 1, 1 - z)
            w.products(c, z)
            if v.shared and at > 0:
                w.down(c - 1, 1 - z)
            w.weights(c, z, half)
        w.norm(0, 0, 0)
        w.norm(1, 1, 0)
        w.turn(0, 0)
        slot(0, 0, 0)
        slot(1, 1, 0)
        with eng.Fori(0, (C - 4) // 2) as i:
            slot(2 * i + 2, 0, i + 1)
            slot(2 * i + 3, 1, i + 1)
        for c in (C - 2, C - 1):
            slot(c, c % 2, c // 2)
        if v.shared:
            w.second_h(C - 1, 1)
            w.down(C - 1, 1)

    class Work:
        def norm(self, c, z, half): pass
        def turn(self, c, z): pass
        def products(self, c, z): pass
        def second_h(self, c, z): pass
        def down(self, c, z): pass
        def weights(self, c, z, half): pass

    block = ctx.enter_context(nc.Block())
    small = 16 * (1 + 3 * bool(v.lin_bias))

    @block.sync
    def _(sp):
        sp.dma_start(gate_stage[:], A["gateT"].rearrange("(k p) n -> p k n", p=P)).then_inc(small_here, 16)
        if v.lin_bias:
            sp.dma_start(gate_b[:], A["gate_b"].rearrange("(o d) -> o d", o=1).broadcast_to([P, E])).then_inc(small_here, 16)
            sp.dma_start(bias_stage1[:], A["b1"].rearrange("(o e) n -> o e n", o=1).broadcast_to([2, E, 2 * v.hidden])).then_inc(small_here, 16)
            sp.dma_start(bias_stage2[:], A["b2"].rearrange("(o e) n -> o e n", o=1).broadcast_to([2, E, D])).then_inc(small_here, 16)

        if v.shared:
            sp.dma_start(s13_stage[:], A["s13T"].rearrange("(k p) n -> p k n", p=P)).then_inc(shared_here, 16)
            sp.dma_start(s2_stage[:], A["s2T"].rearrange("(k p) n -> p k n", p=P)).then_inc(shared_here, 16)

        class Sp(Work):
            def norm(self, c, z, half):
                sp.wait_ge(xn_ready, c + 1)
                sp.dma_start(k.xn_dram.rearrange("(c s p) d -> c p s d", s=S, p=P)[bass.ds(c, 1)].rearrange("c p s d -> p (c s) d"),
                             xn[:, z]).then_inc(stored[z], 16)

            def weights(self, c, z, half, first=False):
                if isinstance(c, int) and c >= C - 2:
                    return
                for kind in w_kinds[z]:
                    if not first:
                        sp.wait_ge(w_lo_done[kind, z], half + 1)
                    sp.dma_start(stages[kind, z][:].unsqueeze(1), w_dram[kind][:, expert_at(c + 2, half + 1), :, :]).then_inc(stage_here[kind, z], 16)

        Sp().weights(-2, 0, -1, first=True)
        Sp().weights(-1, 1, -1, first=True)
        schedule(sp, Sp())
        for z in range(2):
            sp.wait_ge(stored[z], 16 * C // 2)

    @block.tensor
    def _(pe):
        class PE(Work):
            def turn(self, c, z):
                pe.wait_ge(xn_ready, c + 1)
                at_least(pe, xth, c)
                at_least(pe, xtl, c)
                for kb in range(KB):
                    for s in range(S):
                        last = pe.transpose(m.banks[:, 0, (kb * S + s) * P:(kb * S + s + 1) * P],
                                            xn[:, z, s, kb * P:(kb + 1) * P], m.ident[:])
                last.then_inc(xt_in_psum, 1)

            def products(self, c, z):
                pe.wait_ge(xth, c + 1)
                pe.wait_ge(xtl, c + 1)
                at_least(pe, lg_done, c)
                xt, gate = (xt_hi, xt_lo), (gate_hi, gate_lo)
                for s in range(S):
                    last = split_product(pe, m.banks[:, 1, s * E:(s + 1) * E],
                                         lambda a, kb: xt[a][:, z, kb, s * P:(s + 1) * P],
                                         lambda a, kb: gate[a][:, kb, :], KB)
                last.then_inc(lg_in_psum, 1)
                if v.shared:
                    at_least(pe, h_done, c - 1)
                    s13 = (s13_hi, s13_lo)
                    for j in range(2):
                        for hb in range(HSB):
                            col = j * HS + hb * P
                            last = split_product(pe, m.banks[:, 2 + 2 * z + j, hb * S * P:(hb + 1) * S * P],
                                                 lambda a, kb: s13[a][:, kb, col:col + P],
                                                 lambda a, kb: xt[a][:, z, kb, :], KB)
                    last.then_inc(up_done, 1)

            def down(self, c, z):
                pe.wait_ge(hh_done, c + 1)
                pe.wait_ge(hl_done, c + 1)
                at_least(pe, added, c)
                hp, s2 = (h_hi, h_lo), (s2_hi, s2_lo)
                for s in range(S):
                    last = split_product(pe, m.banks[:, 6 + z, s * D:(s + 1) * D],
                                         lambda a, kb: hp[a][:, z, kb, s * P:(s + 1) * P],
                                         lambda a, kb: s2[a][:, kb, :], HSB)
                last.then_inc(down_done, 1)

        pe.wait_ge(gate_done, 2)
        if v.shared:
            pe.wait_ge(lo_done, 1)
        schedule(pe, PE())

    @block.scalar
    def _(act):
        class Act(Work):
            def turn(self, c, z):
                act.wait_ge(xt_in_psum, c + 1)
                at_least(act, up_done, c - 1)
                act.activation(xt_hi[:, z].rearrange("p k t -> p (k t)"), m.banks[:, 0, :], ACT.Copy).then_inc(xth, 1)

            def products(self, c, z):
                if v.shared:
                    act.wait_ge(up_done, c + 1)
                    at_least(act, s1_done, c - 1)
                    act.activation(th[:, z], m.banks[:, 2 + 2 * z, :], ACT.Tanh, scale=v.slope / 2).then_inc(th_done, 1)

            def second_h(self, c, z):
                act.wait_ge(h_done, c + 1)
                at_least(act, down_done, c)
                act.activation(h_hi[:, z].rearrange("p k t -> p (k t)"), h[:, z], ACT.Copy).then_inc(hh_done, 1)

            def weights(self, c, z, half):
                for kind in w_kinds[z]:
                    act.wait_ge(stage_here[kind, z], 16 * (half + 1))
                    act.activation(one(w_parts[kind][0][:, expert_at(c, half), :, :]), stages[kind, z][:],
                                   ACT.Copy).then_inc(w_hi_done[kind, z], 1)

        act.preload_act_table(ACT.Exp)
        if v.shared:
            act.wait_ge(shared_here, 32)
            act.activation(s13_hi[:], s13_stage[:], ACT.Copy)
            act.activation(s2_hi[:], s2_stage[:], ACT.Copy).then_inc(hi_done, 1)
        schedule(act, Act())

    @block.vector
    def _(dve):
        class Dve(Work):
            def norm(self, c, z, half):
                at_least(dve, xt_in_psum, c - 1)
                if not (isinstance(c, int) and c < 2):
                    dve.wait_ge(stored[z], 16 * half)
                for s in range(S):
                    at = bass.ds(S * c + s, 1)
                    last = dve.tensor_scalar(xn[:, z, s:s + 1, :], m.x_res[:, at, :], m.mv[:, at, 0],
                                             m.rstd[:, at], ALU.subtract, ALU.mult)
                last.then_inc(xn_ready, 1)

            def turn(self, c, z):
                dve.wait_ge(xth, c + 1)
                at_least(dve, up_done, c - 1)
                dve.tensor_tensor(xt_lo[:, z].rearrange("p k t -> p (k t)"), m.banks[:, 0, :],
                                  f32(xt_hi[:, z]).rearrange("p k t -> p (k t)"), ALU.subtract).then_inc(xtl, 1)

            def products(self, c, z):
                dve.wait_ge(lg_in_psum, c + 1)
                out = k.logits[:, :, bass.ds(S * c, S)]
                lg = m.banks[:, 1, 0:S * E].rearrange("p (s e) -> p e s", s=S)
                if v.lin_bias:
                    ins = dve.tensor_tensor(out, lg, gate_b[:].unsqueeze(2).broadcast_to([P, E, S]), ALU.add)
                else:
                    ins = dve.tensor_copy(out, lg)
                ins.then_inc(lg_done, 1)
                if v.shared:
                    dve.wait_ge(th_done, c + 1)
                    at_least(dve, h_done, c - 1)
                    dve.scalar_tensor_tensor(out=s1[:, z], in0=th[:, z], scalar=1.0, in1=m.banks[:, 2 + 2 * z, :],
                                             op0=ALU.add, op1=ALU.mult).then_inc(s1_done, 1)
                    dve.wait_ge(s1_done, c + 1)
                    at_least(dve, hh_done, c - 1)
                    dve.scalar_tensor_tensor(out=h[:, z], in0=s1[:, z], scalar=0.5, in1=m.banks[:, 3 + 2 * z, :],
                                             op0=ALU.mult, op1=ALU.mult).then_inc(h_done, 1)

            def second_h(self, c, z):
                dve.wait_ge(hh_done, c + 1)
                at_least(dve, down_done, c)
                dve.tensor_tensor(h_lo[:, z].rearrange("p k t -> p (k t)"), h[:, z],
                                  f32(h_hi[:, z]).rearrange("p k t -> p (k t)"), ALU.subtract).then_inc(hl_done, 1)

            def down(self, c, z):
                dve.wait_ge(down_done, c + 1)
                two = m.x_res[:, bass.ds(S * c, S), :]
                dve.tensor_tensor(two, two, m.banks[:, 6 + z, :].rearrange("p (s c) -> p s c", s=S), ALU.add).then_inc(added, 1)

            def weights(self, c, z, half):
                for kind in w_kinds[z]:
                    dve.wait_ge(w_hi_done[kind, z], half + 1)
                    hi, lo = (one(part[:, expert_at(c, half), :, :]) for part in w_parts[kind])
                    dve.tensor_tensor(lo, stages[kind, z][:], f32(hi), ALU.subtract).then_inc(w_lo_done[kind, z], 1)

        dve.wait_ge(small_here, small)
        dve.tensor_copy(gate_hi[:], gate_stage[:]).then_inc(gate_done, 1)
        dve.wait_ge(gate_done, 1)
        dve.tensor_tensor(gate_lo[:], gate_stage[:], f32(gate_hi[:]), ALU.subtract).then_inc(gate_done, 1)
        if v.lin_bias:
            flat = lambda t: t[:].rearrange("p e n -> p (e n)")
            for st, out in ((bias_stage1, k.b1), (bias_stage2, k.b2)):
                last = dve.tensor_copy(out[:], st[:])
            last.then_inc(bias_done, 1)
            dve.wait_ge(bias_done, 1)
            for st, out in ((bias_stage1, k.b1), (bias_stage2, k.b2)):
                last = dve.scalar_tensor_tensor(out=flat(out), in0=f32(flat(out)), scalar=m.neg_row[0:2, 0:1],
                                                in1=flat(st), op0=ALU.mult, op1=ALU.add)
            last.then_inc(bias_done, 1)
        if v.shared:
            dve.wait_ge(hi_done, 1)
            dve.tensor_tensor(s13_lo[:], s13_stage[:], f32(s13_hi[:]), ALU.subtract)
            dve.tensor_tensor(s2_lo[:], s2_stage[:], f32(s2_hi[:]), ALU.subtract).then_inc(lo_done, 1)
        schedule(dve, Dve())


def rank_phase(nc, m, v, k, ctx):
    E, NTL, NG = v.experts, v.tiles, v.groups
    I32, F16 = mybir.dt.int32, mybir.dt.float16
    sb = lambda name, shape, dt=F32: ctx.enter_context(nc.sbuf_tensor(f"{v.tag}k_{name}", shape, dt))
    sem = lambda name: nc.alloc_semaphore(f"{v.tag}k_{name}")
    lg = k.logits
    mx, oh, eq, imin = sb("mx", [P, 2, NT]), sb("oh", [P, 2, E, NT]), sb("eq", [P, E, NT]), sb("imin", [P, NT])
    lg2, both, ex, diff, ex2 = (sb("lg2", [P, E, NT]), sb("both", [P, E, NT]), sb("ex", [P, E, NT]),
                                sb("diff", [P, NT]), sb("ex2", [P, NT]))
    total = sb("total", [P, NT])
    count, before, zeros = sb("count", [P, E, NT]), sb("before", [P, E, NT]), sb("zeros", [P, E * NT])
    upto_here = sb("upto_here", [P, E, NT])
    ne, full, group_end, base = sb("ne", [P, E]), sb("full", [P, E, NT]), sb("group_end", [P, E]), sb("base", [P, E])
    groups_of = sb("groups_of", [P, E])
    rank, picked, posf = sb("rank", [P, E, NT]), sb("picked", [P, E, NT]), sb("posf", [P, 2, NT])
    tile_i, row_i = sb("tile_i", [P, 2 * NT], I32), sb("row_i", [P, 2 * NT], I32)
    tile_f, row_f = sb("tile_f", [P, 2 * NT]), sb("row_f", [P, 2 * NT])
    tile_oh, tile_tok = sb("tile_oh", [P, 2 * NT, NTL]), sb("tile_tok", [P, 2 * NT, NTL], F16)
    row_oh = sb("row_oh", [P, 2 * NT, P], F16)
    passed, ef = sb("passed", [P, NG, E]), sb("ef", [P, NG])
    step, scalar_step, picks, ranked, rows_ready, listed, zeros_ready = (
        sem(n) for n in "step scalar_step picks ranked rows_ready listed zeros_ready".split())

    e_last = lambda ap: ap.rearrange("p e t -> p t e")
    over_e = lambda ap: ap.unsqueeze(1).broadcast_to([P, E, NT])
    over_t = lambda ap: ap.unsqueeze(2).broadcast_to([P, E, NT])
    block = ctx.enter_context(nc.Block())

    @block.gpsimd
    def _(pool):
        pool.memset(zeros[:], 0.0).then_inc(zeros_ready, 1)

    @block.scalar
    def _(act):
        act.wait_ge(picks, 1)
        act.activation(ex[:], eq[:], ACT.Exp).then_inc(scalar_step, 1)
        act.activation(ex2[:], diff[:], ACT.Exp).then_inc(scalar_step, 1)

    @block.tensor
    def _(pe):
        pe.wait_ge(ranked, 1)
        flat = both[:].rearrange("p e t -> p (e t)")
        pe.matmul(m.banks[:, 0, 0:E * NT], m.upper[:], flat, start=True, stop=True)
        pe.matmul(m.banks[:, 1, 0:E * NT], m.ones[:], flat, start=True, stop=True).then_inc(listed, 1)
        pe.wait_ge(rows_ready, 1)
        for j in range(2 * NT):
            last = pe.matmul(m.banks[:, 2, 0:NTL], row_oh[:, j, :], tile_tok[:, j, :],
                             start=(j == 0), stop=(j == 2 * NT - 1))
        last.then_inc(listed, 1)

    @block.vector
    def _(dve):
        done = [0]

        def then(ins):
            done[0] += 1
            ins.then_inc(step, 1)
            dve.wait_ge(step, done[0])

        source = lg
        for c in range(2):
            then(dve.tensor_reduce(mx[:, c, :], e_last(source[:]), AX_X, ALU.max))
            then(dve.tensor_tensor(eq[:], source[:], over_e(mx[:, c, :]), ALU.is_equal))
            then(dve.tensor_tensor(eq[:], eq[:], over_t(m.expert_less[v.tag][:]), ALU.mult))
            then(dve.tensor_reduce(imin[:], e_last(eq[:]), AX_X, ALU.min))
            then(dve.tensor_tensor(oh[:, c], eq[:], over_e(imin[:]), ALU.is_equal))
            if c == 0:
                then(dve.scalar_tensor_tensor(out=lg2[:].rearrange("p e t -> p (e t)"),
                                              in0=oh[:, 0].rearrange("p e t -> p (e t)"), scalar=-3e38,
                                              in1=lg[:].rearrange("p e t -> p (e t)"), op0=ALU.mult, op1=ALU.add))
                source = lg2
        then(dve.tensor_tensor(both[:], oh[:, 0], oh[:, 1], ALU.add))
        dve.tensor_tensor(diff[:], mx[:, 1, :], mx[:, 0, :], ALU.subtract).then_inc(ranked, 1)
        dve.wait_ge(ranked, 1)
        dve.tensor_tensor(eq[:], lg[:], over_e(mx[:, 0, :]), ALU.subtract).then_inc(picks, 1)
        dve.wait_ge(scalar_step, 2)
        if v.gated == "all":
            then(dve.tensor_reduce(total[:], e_last(ex[:]), AX_X, ALU.add))
        else:
            then(dve.tensor_scalar(total[:], ex2[:], 1.0, None, ALU.add))
        then(dve.reciprocal(k.weight[:, 0, :], total[:]))
        then(dve.tensor_tensor(k.weight[:, 1, :], ex2[:], k.weight[:, 0, :], ALU.mult))

        dve.wait_ge(listed, 1)
        dve.wait_ge(zeros_ready, 1)
        flat = lambda t: t[:].rearrange("p e t -> p (e t)")
        then(dve.tensor_copy(flat(count), m.banks[:, 1, 0:E * NT]))
        then(dve.tensor_tensor_scan(flat(upto_here), flat(count), zeros[:], 0.0, ALU.add, ALU.add))
        then(dve.tensor_tensor(before[:], upto_here[:], count[:], ALU.subtract))
        then(dve.tensor_tensor(ne[:], upto_here[:, :, NT - 1], before[:, :, 0], ALU.subtract))
        then(dve.tensor_tensor(full[:], over_t(ne[:]), over_e(m.group_starts[:]), ALU.is_gt))
        then(dve.tensor_reduce(groups_of[:], full[:], AX_X, ALU.add))
        then(dve.tensor_tensor_scan(group_end[:], groups_of[:], zeros[:, 0:E], 0.0, ALU.add, ALU.add))
        then(dve.tensor_tensor(base[:], group_end[:], groups_of[:], ALU.subtract))
        then(dve.scalar_tensor_tensor(out=base[:], in0=base[:], scalar=float(S * P), in1=before[:, :, 0],
                                      op0=ALU.mult, op1=ALU.subtract))
        then(dve.tensor_tensor(flat(rank), m.banks[:, 0, 0:E * NT], flat(before), ALU.add))
        then(dve.tensor_tensor(rank[:], rank[:], over_t(base[:]), ALU.add))
        for c in range(2):
            then(dve.tensor_tensor(picked[:], rank[:], oh[:, c], ALU.mult))
            then(dve.tensor_reduce(posf[:, c, :], e_last(picked[:]), AX_X, ALU.add))
        then(dve.tensor_copy(k.pos[:], posf[:]))
        pos = k.pos[:].rearrange("p c t -> p (c t)")
        dve.tensor_scalar(tile_i[:], pos, 7, None, ALU.arith_shift_right)
        then(dve.tensor_scalar(row_i[:], pos, P - 1, None, ALU.bitwise_and))
        dve.tensor_copy(tile_f[:], tile_i[:])
        then(dve.tensor_copy(row_f[:], row_i[:]))
        wide = lambda ap, n: ap.unsqueeze(2).broadcast_to([P, 2 * NT, n])
        dve.tensor_tensor(row_oh[:], wide(row_f[:], P), m.count_up[:].unsqueeze(1).broadcast_to([P, 2 * NT, P]), ALU.is_equal)
        then(dve.tensor_tensor(tile_oh[:], wide(tile_f[:], NTL),
                               m.count_up[:, 0:NTL].unsqueeze(1).broadcast_to([P, 2 * NT, NTL]), ALU.is_equal))
        dve.tensor_tensor(tile_tok[:], tile_oh[:], wide(m.token[:], NTL), ALU.mult).then_inc(rows_ready, 1)
        then(dve.tensor_tensor(passed[:], group_end[:].unsqueeze(1).broadcast_to([P, NG, E]),
                               m.count_up[:, 0:NG].unsqueeze(2).broadcast_to([P, NG, E]), ALU.is_le))
        then(dve.tensor_reduce(ef[:], passed[:], AX_X, ALU.add))
        then(dve.tensor_scalar(ef[:], ef[:], float(E - 1), None, ALU.min))
        then(dve.tensor_copy(k.expert_of[:], ef[:]))
        dve.wait_ge(listed, 2)
        then(dve.tensor_copy(k.token_of[:], m.banks[:, 2, 0:NTL]))


def expert_phase(nc, m, v, k, ctx):
    HB, NG, HJ = v.hb, v.groups, S * v.hidden
    sb = lambda name, shape, dt=F32: ctx.enter_context(nc.sbuf_tensor(f"{v.tag}x_{name}", shape, dt))
    sem = lambda name: nc.alloc_semaphore(f"{v.tag}x_{name}")
    index, taken = sb("index", [P, 2, S], mybir.dt.uint32), sb("taken", [P, 2])
    xg = sb("xg", [P, 2, S, D])
    xt_hi, xt_lo = sb("xt_hi", [P, S * KB * P], F32R), sb("xt_lo", [P, S * KB * P], F32R)
    th, s1, h = (sb(n, [P, HJ]) for n in ("th", "s1", "h"))
    ht_hi, ht_lo = sb("ht_hi", [P, HJ], F32R), sb("ht_lo", [P, HJ], F32R)
    yout = sb("yout", [P, 2, S, D])
    (gathered0, gathered1, index_done, xt_in_psum, xth, xtl, glu_done, lin_done, th_done, s1_done, h_done,
     ht_in_psum, hth, htl, down_done, y_done, stored0, stored1) = (
        sem(n) for n in
        "gathered0 gathered1 index_done xt_in_psum xth xtl glu_done lin_done th_done s1_done h_done "
        "ht_in_psum hth htl down_done y_done stored0 stored1".split())
    gathered, stored = (gathered0, gathered1), (stored0, stored1)
    U = HJ // 512
    turns = 4 // (2 * U)
    glu = lambda z: m.banks[:, 2 * U * (z % turns):2 * U * (z % turns) + U, :].rearrange("p b n -> p (b n)")
    lin = lambda z: m.banks[:, 2 * U * (z % turns) + U:2 * U * (z % turns) + 2 * U, :].rearrange("p b n -> p (b n)")
    h_turned = m.banks[:, 4:4 + U, :].rearrange("p b n -> p (b n)")

    def schedule(eng, w):
        def slot(g, z, half, left=NG):
            if left > 2:
                w.gather(g + 2, z, half + 1)
            if left > 1:
                w.turn_x(g + 1, 1 - z, half + z)
            if not (isinstance(g, int) and g == 0):
                w.down(g - 1, 1 - z, half - (1 - z))
            w.turn_h(g)
            if left > 1:
                w.up(g + 1, 1 - z)
        w.gather(0, 0, 0)
        w.gather(1, 1, 0)
        w.turn_x(0, 0, 0)
        w.up(0, 0)
        for g in range(3):
            slot(g, g % 2, g // 2)
        pairs = (NG - 5) // 2
        with eng.Fori(0, pairs) as i:
            slot(2 * i + 3, 1, i + 1)
            slot(2 * i + 4, 0, i + 2)
        for g in range(2 * pairs + 3, NG):
            slot(g, g % 2, g // 2, left=NG - g)
        w.down(NG - 1, (NG - 1) % 2, (NG - 1) // 2)

    class Work:
        def gather(self, g, z, half): pass
        def turn_x(self, g, z, half): pass
        def up(self, g, z): pass
        def turn_h(self, g): pass
        def down(self, g, z, half): pass

    block = ctx.enter_context(nc.Block())

    @block.gpsimd
    def _(pool):
        class Pool(Work):
            def gather(self, g, z, half):
                at_least(pool, xt_in_psum, g - 1)
                pool.tensor_copy(index[:, z, :], k.token_of[:, bass.ds(S * g, S)]).then_inc(index_done, 1)
                pool.wait_ge(index_done, g + 1)
                pool.tensor_tensor(taken[:, z:z + 1], m.neg_row[:], m.neg_row[:], ALU.add)
                for j in range(S):
                    pool.indirect_dma_start(xg[:, z, j, :], None, k.xn_dram,
                                            bass.IndirectOffsetOnAxis(ap=index[:, z, j:j + 1], axis=0)).then_inc(gathered[z], 16)
        schedule(pool, Pool())

    @block.sync
    def _(sp):
        class Sp(Work):
            def down(self, g, z, half):
                sp.wait_ge(y_done, g + 1)
                sp.dma_start(k.y_dram.rearrange("(t p) d -> p t d", p=P)[:, bass.ds(S * g, S), :],
                             yout[:, z, :, :]).then_inc(stored[z], 16)
        schedule(sp, Sp())
        sp.wait_ge(stored0, 16 * ((NG + 1) // 2))
        sp.wait_ge(stored1, 16 * (NG // 2))

    @block.tensor
    def _(pe):
        class PE(Work):
            def turn_x(self, g, z, half):
                pe.wait_ge(gathered[z], 16 * S * (half + 1))
                at_least(pe, xtl, g)
                for j in range(S):
                    for kb in range(KB):
                        last = pe.transpose(m.banks[:, 6, (j * KB + kb) * P:(j * KB + kb + 1) * P],
                                            xg[:, z, j, kb * P:(kb + 1) * P], m.ident[:])
                last.then_inc(xt_in_psum, 1)

            def up(self, g, z):
                pe.wait_ge(xth, g + 1)
                pe.wait_ge(xtl, g + 1)
                at_least(pe, h_done, g + 1 - turns)
                e = pe.value_load(k.expert_of[0:1, bass.ds(g, 1)], min_val=0, max_val=v.experts - 1)
                xt, w13 = (xt_hi, xt_lo), (k.w13_hi, k.w13_lo)
                for b, (half, done) in enumerate(((glu(z), glu_done), (lin(z), lin_done))):
                    cols = slice(b * v.hidden, (b + 1) * v.hidden)
                    steps = [(kb, c) for kb in range(KB) for c in range(2)]
                    for i, (kb, c) in enumerate(steps):
                        weights = w13[c][:, bass.ds(e, 1), kb, cols]
                        for j in range(S):
                            out = half[:, j * v.hidden:(j + 1) * v.hidden]
                            for a in range(2 - c):
                                last = pe.matmul(out, xt[a][:, (j * KB + kb) * P:(j * KB + kb + 1) * P], weights,
                                                 start=(i == 0 and a == 0 and (j == 0 or U == S)),
                                                 stop=(i == len(steps) - 1 and not v.lin_bias and (j == 1 or U == S)))
                    if v.lin_bias:
                        for j in range(S):
                            last = pe.matmul(half[:, j * v.hidden:(j + 1) * v.hidden], m.ones_r[0:2, :],
                                             k.b1[:, bass.ds(e, 1), cols], start=False, stop=(j == S - 1))
                    last.then_inc(done, 1)

            def turn_h(self, g):
                pe.wait_ge(h_done, g + 1)
                at_least(pe, htl, g)
                for j in range(S * HB):
                    last = pe.transpose(h_turned[:, j * P:(j + 1) * P], h[:, j * P:(j + 1) * P], m.ident[:])
                last.then_inc(ht_in_psum, 1)

            def down(self, g, z, half):
                pe.wait_ge(hth, g + 1)
                pe.wait_ge(htl, g + 1)
                at_least(pe, y_done, g)
                e = pe.value_load(k.expert_of[0:1, bass.ds(g, 1)], min_val=0, max_val=v.experts - 1)
                ht, w2 = (ht_hi, ht_lo), (k.w2_hi, k.w2_lo)
                steps = [(hb, c) for hb in range(HB) for c in range(2)]
                for j in range(S):
                    out = m.banks[:, 7, j * D:(j + 1) * D]
                    for i, (hb, c) in enumerate(steps):
                        for a in range(2 - c):
                            last = pe.matmul(out, ht[a][:, (j * HB + hb) * P:(j * HB + hb + 1) * P],
                                             w2[c][:, bass.ds(e, 1), hb, :],
                                             start=(i == 0 and a == 0), stop=(i == len(steps) - 1 and not v.lin_bias))
                    if v.lin_bias:
                        last = pe.matmul(out, m.ones_r[0:2, :], k.b2[:, bass.ds(e, 1), :], start=False, stop=True)
                last.then_inc(down_done, 1)

        schedule(pe, PE())

    @block.scalar
    def _(act):
        class Act(Work):
            def turn_x(self, g, z, half):
                act.wait_ge(xt_in_psum, g + 1)
                at_least(act, lin_done, g)
                act.activation(xt_hi[:], m.banks[:, 6, :], ACT.Copy).then_inc(xth, 1)

            def up(self, g, z):
                act.wait_ge(glu_done, g + 1)
                at_least(act, s1_done, g)
                act.activation(th[:], glu(z), ACT.Tanh, scale=v.slope / 2).then_inc(th_done, 1)

            def turn_h(self, g):
                act.wait_ge(ht_in_psum, g + 1)
                at_least(act, down_done, g)
                act.activation(ht_hi[:], h_turned, ACT.Copy, scale=0.5).then_inc(hth, 1)

            def down(self, g, z, half):
                act.wait_ge(down_done, g + 1)
                if not (isinstance(g, int) and g < 2):
                    act.wait_ge(stored[z], 16 * half)
                act.activation(yout[:, z, :, :].rearrange("p j d -> p (j d)"), m.banks[:, 7, :], ACT.Copy).then_inc(y_done, 1)

        act.preload_act_table(ACT.Tanh)
        schedule(act, Act())

    @block.vector
    def _(dve):
        class Dve(Work):
            def turn_x(self, g, z, half):
                dve.wait_ge(xth, g + 1)
                at_least(dve, lin_done, g)
                dve.tensor_tensor(xt_lo[:], m.banks[:, 6, :], f32(xt_hi[:]), ALU.subtract).then_inc(xtl, 1)

            def up(self, g, z):
                dve.wait_ge(th_done, g + 1)
                at_least(dve, h_done, g)
                dve.scalar_tensor_tensor(out=s1[:], in0=th[:], scalar=1.0, in1=glu(z), op0=ALU.add,
                                         op1=ALU.mult).then_inc(s1_done, 1)
                dve.wait_ge(s1_done, g + 1)
                dve.wait_ge(lin_done, g + 1)
                at_least(dve, ht_in_psum, g)
                dve.scalar_tensor_tensor(out=h[:], in0=lin(z), scalar=float(v.lin_bias), in1=s1[:], op0=ALU.add,
                                         op1=ALU.mult).then_inc(h_done, 1)

            def turn_h(self, g):
                dve.wait_ge(hth, g + 1)
                at_least(dve, down_done, g)
                dve.scalar_tensor_tensor(out=ht_lo[:], in0=h_turned, scalar=0.5, in1=f32(ht_hi[:]), op0=ALU.mult,
                                         op1=ALU.subtract).then_inc(htl, 1)

        schedule(dve, Dve())


def combine_phase(nc, m, A, v, k, ctx, out=None):
    sb = lambda name, shape, dt=F32: ctx.enter_context(nc.sbuf_tensor(f"{v.tag}c_{name}", shape, dt))
    sem = lambda name: nc.alloc_semaphore(f"{v.tag}c_{name}")
    U32 = mybir.dt.uint32
    index, taken = sb("index", [P, 2, 2], U32), sb("taken", [P, 2])
    y = sb("y", [P, 2, 2, D])
    gathered = [[sem(f"gathered{z}{c}") for c in range(2)] for z in range(2)]
    index_done, one_added, both_added, stored, bn_done, aggr_done, eps_done, rstd_done = (
        sem(n) for n in "index_done one_added both_added stored bn_done aggr_done eps_done rstd_done".split())
    block = ctx.enter_context(nc.Block())

    @block.gpsimd
    def _(pool):
        def tile(t, z, half):
            at_least(pool, both_added, t - 1)
            for c in range(2):
                pool.tensor_copy(index[:, z, c:c + 1], k.pos[:, c, bass.ds(t, 1)]).then_inc(index_done, 1)
            pool.wait_ge(index_done, 2 * t + 2)
            pool.tensor_tensor(taken[:, z:z + 1], m.neg_row[:], m.neg_row[:], ALU.add)
            for c in range(2):
                pool.indirect_dma_start(y[:, z, c, :], None, k.y_dram,
                                        bass.IndirectOffsetOnAxis(ap=index[:, z, c:c + 1], axis=0)).then_inc(gathered[z][c], 16)
        tile(0, 0, 0)
        with pool.Fori(0, (NT - 2) // 2) as i:
            tile(2 * i + 1, 1, i)
            tile(2 * i + 2, 0, i + 1)
        tile(NT - 1, 1, NT // 2 - 1)
        if out is None:
            pool.wait_ge(eps_done, 1)
            pool.tensor_tensor(m.rstd[:], m.var_eps[:], m.neg_half[:, 0:NT], ALU.pow).then_inc(rstd_done, 1)

    @block.vector
    def _(dve):
        with dve.Fori(0, NT // 2) as i:
            for z in range(2):
                t = 2 * i + z
                at = bass.ds(t, 1)
                x_t = m.x_res[:, at, :].rearrange("p a d -> p (a d)")
                dve.wait_ge(gathered[z][0], 16 * i + 16)
                dve.scalar_tensor_tensor(out=x_t, in0=y[:, z, 0, :], scalar=k.weight[:, 0, at], in1=x_t,
                                         op0=ALU.mult, op1=ALU.add).then_inc(one_added, 1)
                dve.wait_ge(one_added, t + 1)
                dve.wait_ge(gathered[z][1], 16 * i + 16)
                dve.scalar_tensor_tensor(out=x_t, in0=y[:, z, 1, :], scalar=k.weight[:, 1, at], in1=x_t,
                                         op0=ALU.mult, op1=ALU.add).then_inc(both_added, 1)
                if out is None:
                    dve.wait_ge(both_added, t + 1)
                    dve.bn_stats(m.bn6[:, at, :].rearrange("p a c -> p (a c)"), x_t).then_inc(bn_done, 1)
        if out is None:
            dve.wait_ge(bn_done, NT)
            aggregate(dve, m, aggr_done)
            dve.tensor_scalar(m.var_eps[:], m.mv[:, :, 1], LN_EPS, None, ALU.add).then_inc(eps_done, 1)

    @block.sync
    def _(sp):
        if out is not None:
            with sp.Fori(0, NT) as t:
                sp.wait_ge(both_added, t + 1)
                sp.dma_start(out.rearrange("(t p) d -> p t d", p=P)[:, bass.ds(t, 1), :],
                             m.x_res[:, bass.ds(t, 1), :]).then_inc(stored, 16)
            sp.wait_ge(stored, 16 * NT)


def rwkv_phase(nc, m, A, ctx):
    EB = KB
    sb = lambda name, shape, dt=F32: ctx.enter_context(nc.sbuf_tensor("r_" + name, shape, dt))
    sem = lambda name: nc.alloc_semaphore("r_" + name)
    w_stage, w_mixed = sb("w_stage", [P, 4, KB, D]), sb("w_mixed", [P, 3, 2, KB, D])
    w_hi, w_lo = sb("w_hi", [P, 3, 2, KB, D], F32R), sb("w_lo", [P, 3, 2, KB, D], F32R)
    wo_hi, wo_lo = sb("wo_hi", [P, KB, D], F32R), sb("wo_lo", [P, KB, D], F32R)
    tm, tm_less = sb("tm", [P, 3, KB]), sb("tm_less", [P, 3, KB])
    decay, first, gain, shift = (sb(n, [P, EB]) for n in ("decay", "first", "gain", "shift"))
    grown = sb("grown", [P, EB])
    mean_of = sb("mean_of", [P, P])
    xn = sb("xn", [P, S, D])
    xt_hi, xt_lo = sb("xt_hi", [P, 2, KB, T + 1], F32R), sb("xt_lo", [P, 2, KB, T + 1], F32R)
    ks, vs, th = (sb(n, [P, 2, EB, T]) for n in ("k", "v", "th"))
    top, aa, bb = (sb(n, [P, EB, T + 1]) for n in ("top", "aa", "bb"))
    less, ex = sb("less", [P, 4, EB, T]), sb("ex", [P, 4, EB, T])
    dif, f2v, e2v, num, den, rden, wkv, c, sq, lnv, rw = (
        sb(n, [P, EB, T]) for n in ("dif", "f2v", "e2v", "num", "den", "rden", "wkv", "c", "sq", "lnv", "rw"))
    ve, rstd = sb("ve", [P, S]), sb("rstd", [P, S])
    rw_hi, rw_lo = sb("rw_hi", [P, EB, T], F32R), sb("rw_lo", [P, EB, T], F32R)
    names = ("loaded exp_decay half mixed whi wlo edges xn_ready xt_in_psum xth xtl kvr_done evac top_done dif_done "
             "less_done exp_done f2v_done e2v_done aa_done e1a_done num_done e1b_done den_done rden_done wkv_done "
             "mean_done c_done sq_done var_done ve_done rstd_done t_done ln_done rw_done rwh rwl out_done x_done "
             "bn_done aggr_done eps_done next_rstd prep spread")
    done = {n: sem(n) for n in names.split()}
    NEVER = -1e38

    def schedule(eng, w):
        def slot(b, z, first=False, last=False):
            if not isinstance(b, int) or b >= 2:
                w.add(b - 2)
            w.scores(b, z)
            if not first:
                w.centre(b - 1)
            if not last:
                w.turn(b + 1, 1 - z)
            if not first:
                w.vary(b - 1)
            w.weigh(b, z)
            if not last:
                w.products(b + 1, 1 - z)
            if not first:
                w.norm(b - 1, 1 - z)
            w.mean(b)
            if not first:
                w.out(b - 1)
        w.turn(0, 0)
        w.products(0, 0)
        slot(0, 0, first=True)
        slot(1, 1)
        with eng.Fori(0, (B - 4) // 2) as i:
            slot(2 * i + 2, 0)
            slot(2 * i + 3, 1)
        slot(B - 2, 0)
        slot(B - 1, 1, last=True)
        w.add(B - 2)
        w.centre(B - 1)
        w.vary(B - 1)
        w.norm(B - 1, 1)
        w.out(B - 1)
        w.add(B - 1)

    class Work:
        def add(self, b): pass
        def scores(self, b, z): pass
        def centre(self, b): pass
        def turn(self, b, z): pass
        def vary(self, b): pass
        def weigh(self, b, z): pass
        def norm(self, b, z): pass
        def products(self, b, z): pass
        def mean(self, b): pass
        def out(self, b): pass

    flat = lambda t: t.rearrange("p e t -> p (e t)")
    block = ctx.enter_context(nc.Block())

    @block.sync
    def _(sp):
        for i, n in enumerate("kvro"):
            sp.dma_start(w_stage[:, i], A[f"W{n}T"].rearrange("(k p) n -> p k n", p=P)).then_inc(done["loaded"], 16)
        for i, n in enumerate("kvr"):
            sp.dma_start(tm[:, i, :], A[f"tm_{n}"].rearrange("(k p) -> p k", p=P),
                         allow_slow_non_contiguous=True).then_inc(done["loaded"], 16)
        for t, n in ((decay, "time_decay"), (first, "time_first"), (gain, "ln_g"), (shift, "ln_b")):
            sp.dma_start(t[:], A[n].rearrange("(k p) -> p k", p=P), allow_slow_non_contiguous=True).then_inc(done["loaded"], 16)

    @block.tensor
    def _(pe):
        class PE(Work):
            def turn(self, b, z):
                pe.wait_ge(done["xn_ready"], b + 1)
                at_least(pe, done["xth"], b)
                at_least(pe, done["xtl"], b)
                for kb in range(KB):
                    for s in range(S):
                        last = pe.transpose(m.banks[:, 0, (kb * S + s) * P:(kb * S + s + 1) * P],
                                            xn[:, s, kb * P:(kb + 1) * P], m.ident[:])
                last.then_inc(done["xt_in_psum"], 1)

            def products(self, b, z):
                pe.wait_ge(done["xth"], b + 1)
                pe.wait_ge(done["xtl"], b + 1)
                at_least(pe, done["evac"], 3 * b)
                xt, w = (xt_hi, xt_lo), (w_hi, w_lo)
                for kind in range(3):
                    for eb in range(EB):
                        last = split_product(
                            pe, m.banks[:, 1 + kind, eb * T:(eb + 1) * T],
                            lambda a, j: w[a][:, kind, j // KB, j % KB, eb * P:(eb + 1) * P],
                            lambda a, j: xt[a][:, z, j % KB, 1 - j // KB:T + 1 - j // KB], 2 * KB)
                    last.then_inc(done["kvr_done"], 1)

            def mean(self, b):
                pe.wait_ge(done["wkv_done"], b + 1)
                at_least(pe, done["c_done"], b)
                for eb in range(EB):
                    last = pe.matmul(m.banks[:, 4, 0:T], mean_of[:], wkv[:, eb, :], start=(eb == 0), stop=(eb == EB - 1))
                last.then_inc(done["mean_done"], 1)

            def vary(self, b):
                pe.wait_ge(done["sq_done"], b + 1)
                at_least(pe, done["ve_done"], b)
                for s in range(S):
                    for eb in range(EB):
                        last = pe.matmul(m.banks[:, 5, s:s + 1], sq[:, eb, s * P:(s + 1) * P], mean_of[:, 0:1],
                                         start=(eb == 0), stop=(eb == EB - 1))
                last.then_inc(done["var_done"], 1)

            def norm(self, b, z):
                pe.wait_ge(done["rstd_done"], b + 1)
                at_least(pe, done["t_done"], b)
                for s in range(S):
                    last = pe.matmul(m.banks[:, 7, s * P:(s + 1) * P], rstd[:, s:s + 1].broadcast_to([P, P]), m.ident[:],
                                     start=True, stop=True)
                last.then_inc(done["spread"], 1)

            def out(self, b):
                pe.wait_ge(done["rwh"], b + 1)
                pe.wait_ge(done["rwl"], b + 1)
                at_least(pe, done["x_done"], b)
                r, w = (rw_hi, rw_lo), (wo_hi, wo_lo)
                for s in range(S):
                    last = split_product(pe, m.banks[:, 6, s * D:(s + 1) * D],
                                         lambda a, kb: r[a][:, kb, s * P:(s + 1) * P],
                                         lambda a, kb: w[a][:, kb, :], EB)
                last.then_inc(done["out_done"], 1)

        pe.wait_ge(done["wlo"], 2)
        schedule(pe, PE())

    @block.scalar
    def _(act):
        class Act(Work):
            def turn(self, b, z):
                act.wait_ge(done["xt_in_psum"], b + 1)
                at_least(act, done["kvr_done"], 3 * (b - 1))
                act.activation(xt_hi[:, z, :, 1:T + 1], m.banks[:, 0, :].rearrange("p (k t) -> p k t", k=KB),
                               ACT.Copy).then_inc(done["xth"], 1)

            def products(self, b, z):
                at_least(act, done["wkv_done"], b - 1)
                at_least(act, done["rw_done"], b - 1)
                for kind, (to, func, scale) in enumerate(((ks, ACT.Copy, 1.0), (vs, ACT.Copy, 1.0), (th, ACT.Tanh, 0.5))):
                    act.wait_ge(done["kvr_done"], 3 * b + kind + 1)
                    act.activation(flat(to[:, z]), m.banks[:, 1 + kind, :], func, scale=scale).then_inc(done["evac"], 1)

            def scores(self, b, z):
                act.wait_ge(done["less_done"], b + 1)
                at_least(act, done["wkv_done"], b)
                act.activation(ex[:], less[:], ACT.Exp).then_inc(done["exp_done"], 1)

            def centre(self, b):
                act.wait_ge(done["c_done"], b + 1)
                at_least(act, done["var_done"], b)
                act.activation(sq[:], c[:], ACT.Square).then_inc(done["sq_done"], 1)

            def norm(self, b, z):
                act.wait_ge(done["rw_done"], b + 1)
                at_least(act, done["out_done"], b)
                act.activation(rw_hi[:], rw[:], ACT.Copy).then_inc(done["rwh"], 1)

        act.preload_act_table(ACT.Exp)
        act.wait_ge(done["loaded"], 16 * 11)
        act.activation(grown[:], decay[:], ACT.Exp).then_inc(done["exp_decay"], 1)
        act.wait_ge(done["mixed"], 6)
        act.activation(w_hi[:], w_mixed[:], ACT.Copy)
        act.activation(wo_hi[:], w_stage[:, 3], ACT.Copy).then_inc(done["whi"], 1)
        schedule(act, Act())

    @block.vector
    def _(dve):
        class Dve(Work):
            def turn(self, b, z):
                at_least(dve, done["xt_in_psum"], b)
                for s in range(S):
                    at = bass.ds(S * b + s, 1)
                    last = dve.tensor_scalar(xn[:, s:s + 1, :], m.x_res[:, at, :], m.mv[:, at, 0],
                                             m.rstd[:, at], ALU.subtract, ALU.mult)
                last.then_inc(done["xn_ready"], 1)
                dve.wait_ge(done["xth"], b + 1)
                at_least(dve, done["kvr_done"], 3 * (b - 1))
                dve.tensor_tensor(xt_lo[:, z, :, 1:T + 1], m.banks[:, 0, :].rearrange("p (k t) -> p k t", k=KB),
                                  f32(xt_hi[:, z, :, 1:T + 1]), ALU.subtract).then_inc(done["xtl"], 1)

            def scores(self, b, z):
                dve.wait_ge(done["evac"], 3 * b + 3)
                at_least(dve, done["less_done"], b)
                for eb in range(EB):
                    last = dve.tensor_tensor_scan(top[:, eb, 1:T + 1], grown[:, eb:eb + 1].broadcast_to([P, T]),
                                                  ks[:, z, eb, :], NEVER, ALU.add, ALU.max)
                last.then_inc(done["top_done"], 1)
                dve.wait_ge(done["top_done"], b + 1)
                for eb in range(EB):
                    last = dve.scalar_tensor_tensor(out=dif[:, eb, :], in0=ks[:, z, eb, :], scalar=first[:, eb:eb + 1],
                                                    in1=top[:, eb, 0:T], op0=ALU.add, op1=ALU.subtract)
                last.then_inc(done["dif_done"], 1)
                at_least(dve, done["exp_done"], b)
                dve.tensor_tensor(less[:, 2], top[:, :, 0:T], top[:, :, 1:T + 1], ALU.subtract)
                dve.tensor_tensor(less[:, 3], ks[:, z], top[:, :, 1:T + 1], ALU.subtract)
                dve.wait_ge(done["dif_done"], b + 1)
                dve.tensor_scalar(less[:, 0], dif[:], 0.0, None, ALU.min)
                dve.tensor_scalar(less[:, 1], dif[:], -1.0, 0.0, ALU.mult, ALU.min).then_inc(done["less_done"], 1)

            def weigh(self, b, z):
                def then(ins, name):
                    ins.then_inc(done[name], 1)
                    dve.wait_ge(done[name], b + 1)

                dve.wait_ge(done["exp_done"], b + 1)
                then(dve.tensor_tensor(f2v[:], ex[:, 3], vs[:, z], ALU.mult), "f2v_done")
                for eb in range(EB):
                    dve.tensor_tensor_scan(aa[:, eb, 1:T + 1], ex[:, 2, eb, :], f2v[:, eb, :], 0.0, ALU.mult, ALU.add)
                for eb in range(EB):
                    last = dve.tensor_tensor_scan(bb[:, eb, 1:T + 1], ex[:, 2, eb, :], ex[:, 3, eb, :], 0.0, ALU.mult, ALU.add)
                then(last, "aa_done")
                dve.tensor_tensor(num[:], ex[:, 1], aa[:, :, 0:T], ALU.mult).then_inc(done["e1a_done"], 1)
                then(dve.tensor_tensor(den[:], ex[:, 1], bb[:, :, 0:T], ALU.mult), "e1b_done")
                then(dve.tensor_tensor(den[:], den[:], ex[:, 0], ALU.add), "den_done")
                dve.wait_ge(done["e2v_done"], b + 1)
                dve.tensor_tensor(num[:], num[:], e2v[:], ALU.add).then_inc(done["num_done"], 1)
                then(dve.reciprocal(rden[:], den[:]), "rden_done")
                at_least(dve, done["mean_done"], b)
                dve.tensor_tensor(wkv[:], num[:], rden[:], ALU.mult).then_inc(done["wkv_done"], 1)

            def centre(self, b):
                dve.wait_ge(done["mean_done"], b + 1)
                at_least(dve, done["sq_done"], b)
                dve.tensor_tensor(c[:], wkv[:], m.banks[:, 4, 0:T].unsqueeze(1).broadcast_to([P, EB, T]),
                                  ALU.subtract).then_inc(done["c_done"], 1)

            def vary(self, b):
                dve.wait_ge(done["var_done"], b + 1)
                at_least(dve, done["rstd_done"], b)
                dve.tensor_scalar(ve[:], m.banks[:, 5, 0:S], LN_EPS, None, ALU.add).then_inc(done["ve_done"], 1)

            def norm(self, b, z):
                dve.wait_ge(done["spread"], b + 1)
                dve.tensor_tensor(lnv[:], c[:], m.banks[:, 7, 0:T].unsqueeze(1).broadcast_to([P, EB, T]), ALU.mult).then_inc(done["t_done"], 1)
                dve.wait_ge(done["t_done"], b + 1)
                for eb in range(EB):
                    last = dve.tensor_scalar(lnv[:, eb, :], lnv[:, eb, :], gain[:, eb:eb + 1], shift[:, eb:eb + 1],
                                             ALU.mult, ALU.add)
                last.then_inc(done["ln_done"], 1)
                dve.wait_ge(done["ln_done"], b + 1)
                at_least(dve, done["rwh"], b)
                dve.scalar_tensor_tensor(out=flat(rw[:]), in0=flat(th[:, z]), scalar=1.0, in1=flat(lnv[:]),
                                         op0=ALU.add, op1=ALU.mult).then_inc(done["rw_done"], 1)
                dve.wait_ge(done["rwh"], b + 1)
                at_least(dve, done["out_done"], b)
                dve.tensor_tensor(rw_lo[:], rw[:], f32(rw_hi[:]), ALU.subtract).then_inc(done["rwl"], 1)

            def add(self, b):
                dve.wait_ge(done["out_done"], b + 1)
                two = m.x_res[:, bass.ds(S * b, S), :]
                dve.tensor_tensor(two, two, m.banks[:, 6, :].rearrange("p (s c) -> p s c", s=S), ALU.add).then_inc(done["x_done"], 1)
                dve.wait_ge(done["x_done"], b + 1)
                for s in range(S):
                    at = bass.ds(S * b + s, 1)
                    last = dve.bn_stats(m.bn6[:, at, :].rearrange("p a c -> p (a c)"),
                                        m.x_res[:, at, :].rearrange("p a c -> p (a c)"))
                last.then_inc(done["bn_done"], 1)

        dve.wait_ge(done["loaded"], 16 * 11)
        dve.tensor_scalar(tm_less[:], tm[:], -1.0, 1.0, ALU.mult, ALU.add).then_inc(done["prep"], 1)
        dve.tensor_scalar(gain[:], gain[:], 0.5, None, ALU.mult)
        dve.tensor_scalar(shift[:], shift[:], 0.5, None, ALU.mult).then_inc(done["prep"], 1)
        dve.wait_ge(done["exp_decay"], 1)
        dve.wait_ge(done["prep"], 2)
        dve.tensor_scalar(grown[:], grown[:], -1.0, None, ALU.mult).then_inc(done["prep"], 1)
        for kind in range(3):
            for kb in range(KB):
                dve.tensor_scalar(w_mixed[:, kind, 0, kb, :], w_stage[:, kind, kb, :], tm[:, kind, kb:kb + 1], None, ALU.mult)
                dve.tensor_scalar(w_mixed[:, kind, 1, kb, :], w_stage[:, kind, kb, :], tm_less[:, kind, kb:kb + 1], None,
                                  ALU.mult).then_inc(done["mixed"], 1)
        dve.wait_ge(done["whi"], 1)
        dve.tensor_tensor(w_lo[:], w_mixed[:], f32(w_hi[:]), ALU.subtract).then_inc(done["wlo"], 1)
        dve.tensor_tensor(wo_lo[:], w_stage[:, 3], f32(wo_hi[:]), ALU.subtract).then_inc(done["wlo"], 1)
        dve.wait_ge(done["edges"], 1)
        schedule(dve, Dve())
        dve.wait_ge(done["bn_done"], B)
        aggregate(dve, m, done["aggr_done"])
        dve.tensor_scalar(m.var_eps[:], m.mv[:, :, 1], LN_EPS, None, ALU.add).then_inc(done["eps_done"], 1)

    @block.gpsimd
    def _(pool):
        class Pool(Work):
            def vary(self, b):
                pool.wait_ge(done["ve_done"], b + 1)
                at_least(pool, done["spread"], b)
                pool.tensor_tensor(rstd[:], ve[:], m.neg_half[:, 0:S], ALU.pow).then_inc(done["rstd_done"], 1)

            def weigh(self, b, z):
                pool.wait_ge(done["exp_done"], b + 1)
                pool.wait_ge(done["evac"], 3 * b + 3)
                at_least(pool, done["num_done"], b)
                pool.tensor_tensor(e2v[:], ex[:, 0], vs[:, z], ALU.mult).then_inc(done["e2v_done"], 1)

        for part in (xt_hi, xt_lo):
            pool.memset(f32(part[:, :, :, 0]), 0.0)
        pool.memset(top[:, :, 0], NEVER)
        pool.memset(aa[:, :, 0], 0.0)
        pool.memset(mean_of[:], 1.0 / D)
        pool.memset(bb[:, :, 0], 0.0).then_inc(done["edges"], 1)
        pool.wait_ge(done["edges"], 1)
        schedule(pool, Pool())
        pool.wait_ge(done["eps_done"], 1)
        pool.tensor_tensor(m.rstd[:], m.var_eps[:], m.neg_half[:, 0:NT], ALU.pow).then_inc(done["next_rstd"], 1)


def build_program(nc, A, out):
    with ExitStack() as ctx:
        m = shared_memory(nc, ctx)
        with phase(nc) as scope:
            setup_phase(nc, m, A, scope)
        with phase(nc) as scope:
            attention_phase(nc, m, A, scope)
        mixture_layer(nc, m, {name[3:]: ap for name, ap in A.items() if name.startswith("f0_")},
                      Mixture("f0", 4, 512, "all", True, 1.0, 0))
        with phase(nc) as scope:
            rwkv_phase(nc, m, A, scope)
        mixture_layer(nc, m, {name[3:]: ap for name, ap in A.items() if name.startswith("f1_")},
                      Mixture("f1", 8, 256, "two", False, 1.702, 1), out)


@contextmanager
def phase(nc):
    before = nc.snapshot_sems()
    with ExitStack() as scope:
        yield scope
    nc.clear_and_free_semaphores(nc.allocated_since(before))
    nc.all_engine_barrier()


def mixture_layer(nc, m, A, v, out=None):
    with ExitStack() as layer:
        k = mixture_memory(nc, v, layer)
        with phase(nc) as scope:
            router_phase(nc, m, A, v, k, scope)
        with phase(nc) as scope:
            rank_phase(nc, m, v, k, scope)
        with phase(nc) as scope:
            expert_phase(nc, m, v, k, scope)
        with phase(nc) as scope:
            combine_phase(nc, m, A, v, k, scope, out)


def laid_out(inputs):
    i = {name: np.asarray(a) for name, a in inputs.items()}
    turned = lambda a: np.swapaxes(a, -1, -2)
    halves = lambda a: np.concatenate([a[:, 0::2], a[:, 1::2]], axis=1)
    a = {
        "L0_attn_x": i["L0_attn_x"].reshape(TOK, D),
        "L0_attn_W": i["L0_attn_W"], "L0_attn_WT": turned(i["L0_attn_W"]),
        "L0_attn_g1": i["L0_attn_g1"], "L0_attn_g2": i["L0_attn_g2"], "L0_attn_g3": i["L0_attn_g3"],
        "f0_gateT": turned(i["L0_ffn_gate_w"]),
        "f0_w13T": turned(np.concatenate([i["L0_ffn_w1"], i["L0_ffn_w3"]], axis=1)),
        "f0_w2T": turned(i["L0_ffn_w2"]),
        "f0_s13T": turned(np.concatenate([i["L0_ffn_sw1"], i["L0_ffn_sw3"]], axis=0)),
        "f0_s2T": turned(i["L0_ffn_sw2"]),
        "f1_gateT": turned(i["L1_ffn_gate_w"]), "f1_gate_b": i["L1_ffn_gate_b"],
        "f1_w13T": turned(halves(i["L1_ffn_w1"])), "f1_w2T": turned(i["L1_ffn_w2"]),
        "f1_b1": halves(i["L1_ffn_b1"]), "f1_b2": i["L1_ffn_b2"],
    }
    for n in "kvro":
        a[f"W{n}T"] = turned(i[f"L1_attn_W{n}"])
    for n in ("tm_k", "tm_v", "tm_r", "time_decay", "time_first", "ln_g", "ln_b"):
        a[n] = i[f"L1_attn_{n}"].reshape(D)
    return {name: np.ascontiguousarray(v) for name, v in a.items()}


def kernel(**inputs):
    import concourse.bacc as bacc
    from concourse.bass_utils import run_bass_kernel_spmd

    arrays = {f"in_{name}": a for name, a in laid_out(inputs).items()}
    nc = bacc.Bacc("TRN2", target_bir_lowering=False, num_devices=1)
    A = {name[3:]: nc.dram_tensor(name, a.shape, mybir.dt.from_np(a.dtype), kind="ExternalInput").ap()
         for name, a in arrays.items()}
    out = nc.dram_tensor("out_x", (TOK, D), F32, kind="ExternalOutput").ap()
    build_program(nc, A, out)
    result = run_bass_kernel_spmd(nc, [arrays], core_ids=[0])
    return result.results[0]["out_x"].reshape(B, T, D)
```

```python
from contextlib import ExitStack, contextmanager

import numpy as np

import concourse.bass as bass
from concourse import mybir

ALU = mybir.AluOpType
ACT = mybir.ActivationFunctionType
F32 = mybir.dt.float32
F32R = mybir.dt.float32r
AX_X = mybir.AxisListType.X

P = 128
B, T, D = 8, 256, 256
TOK = B * T
NT = TOK // P
KB = D // P
S = T // P
NH, DH = 16, 16
NP = NH // 2
LN_EPS = 1e-5
RMS_EPS = 1.1920928955078125e-07


def f32(ap):
    return ap.bitcast(F32)


def at_least(eng, semaphore, value):
    if not (isinstance(value, int) and value <= 0):
        eng.wait_ge(semaphore, value)


def upto(value, most):
    return min(value, most) if isinstance(value, int) else value


def split_product(pe, out, lhs, rhs, k_blocks):
    steps = [(a, c, k) for k in range(k_blocks) for a, c in ((0, 0), (0, 1), (1, 0))]
    for n, (a, c, k) in enumerate(steps):
        last = pe.matmul(out, lhs(a, k), rhs(c, k), start=(n == 0), stop=(n == len(steps) - 1))
    return last


def aggregate(dve, m, aggr_done):
    for t in range(NT):
        last = dve.bn_aggr(m.mv[:, t, :], m.bn6[:, t, :])
    last.then_inc(aggr_done, 1)
    dve.wait_ge(aggr_done, 1)


class Names:
    pass


def shared_memory(nc, ctx):
    m = Names()
    sb = lambda name, shape, dt=F32: ctx.enter_context(nc.sbuf_tensor(name, shape, dt))
    m.x_res = sb("x_res", [P, NT, D])
    m.ident = sb("ident", [P, P])
    m.bn6 = sb("bn6", [P, NT, 6])
    m.mv = sb("mv", [P, NT, 2])
    m.var_eps = sb("var_eps", [P, NT])
    m.rstd = sb("rstd", [P, NT])
    m.neg_half = sb("neg_half", [P, 512])
    m.upper = sb("upper", [P, P])
    m.ones = sb("ones", [P, P])
    m.ones_r = sb("ones_r", [P, P], F32R)
    m.count_up = sb("count_up", [P, P])
    m.group_starts = sb("group_starts", [P, NT])
    m.token = sb("token", [P, 2 * NT])
    m.neg_row = sb("neg_row", [P, 1])
    m.expert_less = {tag: sb(f"expert_less_{tag}", [P, e]) for tag, e in (("f0", 4), ("f1", 8))}
    m.banks = ctx.enter_context(nc.psum_tensor("banks", [P, 8, 512], F32))
    return m


def setup_phase(nc, m, A, ctx):
    I32 = mybir.dt.int32
    ints = {n: ctx.enter_context(nc.sbuf_tensor(f"int_{n}", [P, w], I32)) for n, w in
            (("count_up", P), ("group_starts", NT), ("token", 2 * NT), ("neg_row", 1), ("f0", 4), ("f1", 8))}
    iota_done = nc.alloc_semaphore("iota_done")
    upper_ready = nc.alloc_semaphore("upper_ready")
    x_here, id_zero, id_ready, half_ready, bn_done, aggr_done, eps_done, rstd_done = (
        nc.alloc_semaphore(n) for n in
        ("x_here", "id_zero", "id_ready", "half_ready", "bn_done", "aggr_done", "eps_done", "rstd_done"))
    block = ctx.enter_context(nc.Block())

    @block.sync
    def _(sp):
        x_tiles = A["L0_attn_x"].rearrange("(t p) d -> p t d", p=P)
        for half in range(2):
            sp.dma_start(m.x_res[:, half * NT // 2:(half + 1) * NT // 2, :],
                         x_tiles[:, half * NT // 2:(half + 1) * NT // 2, :]).then_inc(x_here, 16)

    @block.gpsimd
    def _(pool):
        pool.memset(m.ident[:], 0.0).then_inc(id_zero, 1)
        pool.memset(m.neg_half[:], -0.5).then_inc(half_ready, 1)
        pool.wait_ge(id_zero, 1)
        pool.affine_select(out=m.ident[:], in_=m.ident[:], compare_op=ALU.not_equal, fill=1.0, base=0,
                           pattern=[[-1, P]], channel_multiplier=1).then_inc(id_ready, 1)
        pool.memset(m.ones[:], 1.0).then_inc(upper_ready, 1)
        pool.wait_ge(upper_ready, 1)
        pool.affine_select(out=m.upper[:], in_=m.ones[:], compare_op=ALU.is_ge, fill=0.0, base=-1,
                           pattern=[[1, P]], channel_multiplier=-1).then_inc(upper_ready, 1)
        pool.iota(ints["count_up"][:], [[1, P]], base=0, channel_multiplier=0).then_inc(iota_done, 1)
        pool.iota(ints["group_starts"][:], [[S * P, NT]], base=0, channel_multiplier=0).then_inc(iota_done, 1)
        pool.iota(ints["token"][:], [[0, 2], [P, NT]], base=0, channel_multiplier=1).then_inc(iota_done, 1)
        pool.iota(ints["neg_row"][:], [[0, 1]], base=0, channel_multiplier=-1).then_inc(iota_done, 1)
        pool.iota(ints["f0"][:], [[1, 4]], base=-4, channel_multiplier=0).then_inc(iota_done, 1)
        pool.iota(ints["f1"][:], [[1, 8]], base=-8, channel_multiplier=0).then_inc(iota_done, 1)
        pool.wait_ge(half_ready, 1)
        pool.wait_ge(eps_done, 1)
        pool.tensor_tensor(m.rstd[:], m.var_eps[:], m.neg_half[:, 0:NT], ALU.pow).then_inc(rstd_done, 1)

    @block.vector
    def _(dve):
        dve.wait_ge(iota_done, 6)
        dve.wait_ge(upper_ready, 1)
        for name, to in (("count_up", m.count_up), ("group_starts", m.group_starts), ("token", m.token),
                         ("neg_row", m.neg_row), ("f0", m.expert_less["f0"]), ("f1", m.expert_less["f1"])):
            dve.tensor_copy(to[:], ints[name][:])
        dve.tensor_copy(m.ones_r[:], m.ones[:])
        dve.wait_ge(x_here, 32)
        for t in range(NT):
            last = dve.bn_stats(m.bn6[:, t, :], m.x_res[:, t, :])
        last.then_inc(bn_done, 1)
        dve.wait_ge(bn_done, 1)
        aggregate(dve, m, aggr_done)
        dve.tensor_scalar(m.var_eps[:], m.mv[:, :, 1], LN_EPS, None, ALU.add).then_inc(eps_done, 1)


def attention_phase(nc, m, A, ctx):
    SMALL_BOUND = 60.0
    sb = lambda name, shape, dt=F32: ctx.enter_context(nc.sbuf_tensor(name, shape, dt))
    sem = lambda name: nc.alloc_semaphore(name)
    w_stage = sb("a_w_stage", [P, KB, D])
    wt_stage = sb("a_wt_stage", [P, KB, D])
    w_hi, w_lo = sb("a_w_hi", [P, KB, D], F32R), sb("a_w_lo", [P, KB, D], F32R)
    wt_hi, wt_lo = sb("a_wt_hi", [P, KB, D], F32R), sb("a_wt_lo", [P, KB, D], F32R)
    g1, g2, g3, gq = sb("g1", [P, DH]), sb("g2", [P, DH]), sb("g3", [P, DH]), sb("gq", [P, DH])
    neg_gq, abs_gq, most_gq = sb("neg_gq", [P, DH]), sb("abs_gq", [P, DH]), sb("most_gq", [P, 1])
    bound_large, is_large = sb("bound_large", [P, 1]), sb("is_large", [P, 1], mybir.dt.int32)
    xn = sb("a_xn", [P, S, D])
    xt_hi, xt_lo = sb("a_xt_hi", [P, KB * S * P], F32R), sb("a_xt_lo", [P, KB * S * P], F32R)
    sq = sb("a_sq", [P, S * NH, DH])
    ms, ms_eps, rr = sb("a_ms", [P, S * NH]), sb("a_ms_eps", [P, S * NH]), sb("a_rr", [P, S * NH])
    u, q = sb("a_u", [P, S * NH, DH]), sb("a_q", [P, S * NH, DH])
    qst, kst = sb("a_qst", [P, 2, S * NH, 4, DH], F32R), sb("a_kst", [P, 2, S * NH, 4, DH], F32R)
    vv, vs = sb("a_vv", [P, 2, S * NH, 2, DH]), sb("a_vs", [P, 2, S * NH, 2, DH])
    qkt = sb("a_qkt", [P, 2, 4 * P], F32R)
    ebuf = sb("a_e", [P, 4, 4, T])
    ssum, rs = sb("a_ssum", [P, 2, NH * S]), sb("a_rs", [P, 2, NH * S])
    neg_max = sb("a_neg_max", [P, 2, 2 * S])
    row_max = sb("a_row_max", [P, 2, 2 * S])
    turned = sb("a_turned", [P, 2 * S, T])
    outt = sb("a_outt", [P, 2, T])
    ytmp, ytok = sb("a_ytmp", [P, S, 4, DH]), sb("a_ytok", [P, 2, S, D])
    yt_hi, yt_lo = sb("a_yt_hi", [P, KB * S * P], F32R), sb("a_yt_lo", [P, KB * S * P], F32R)

    (loaded, gaps_zero, whi_done, w_split, gq_step, gq_ready, xn_ready, xt_in_psum, xth, xtl, w_ready, sq_done,
     ms_done, mse_done, rr_ready, u_ready, kh_done, kst_ready, q_done, qh_done, qst_ready, v_ready, qk_in_psum,
     qkt_ready, s_ready, exp_done, sum_done, rs_done, vr_ready, av_done, outt_ready,
     yraw_in_psum, ytmp_done, ytok_done, yt_in_psum, yth, ytl, proj_done, x1_done, bn_done, aggr_done, eps_done, rstd_done,
     max_found, max_ready, turned_in_psum, turned_ready) = (
        sem("a_" + n) for n in
        "loaded gaps_zero whi_done w_split gq_step gq_ready xn_ready xt_in_psum xth xtl w_ready sq_done "
        "ms_done mse_done rr_ready u_ready kh_done kst_ready q_done qh_done qst_ready v_ready qk_in_psum "
        "qkt_ready s_ready exp_done sum_done rs_done vr_ready av_done outt_ready yraw_in_psum ytmp_done "
        "ytok_done yt_in_psum yth ytl proj_done x1_done bn_done aggr_done eps_done rstd_done "
        "max_found max_ready turned_in_psum turned_ready".split())

    tr = m.banks[:, 0, :]
    qkp = m.banks[:, 2, :]
    av = lambda g: m.banks[:, 1 + 2 * (g % 2), 0:T]
    yraw = lambda g: m.banks[:, 1 + 2 * (g % 2), T:2 * T]
    scores = m.banks[:, 4:8, :].rearrange("p (r h) (s t) -> p r h s t", r=2, s=S)

    def schedule(eng, w):
        def batch(b, z):
            at = b if isinstance(b, int) else 1
            first, last, before_last = at == 0, at == B - 1, at >= B - 2
            for p in range(NP):
                w.now(b, p, z)
                if not last:
                    if p == 1:
                        w.head_norm(b + 1, 1 - z)
                    if p == 2:
                        w.stack(b + 1, 1 - z)
                    if p == 4:
                        w.stack_low(b + 1, 1 - z)
                if p == 3 and not first:
                    w.split_y(b - 1)
                if not before_last:
                    if p == 6:
                        w.split_x(b + 2)
                if p == 7 and not before_last:
                    w.squares(b + 2)
                if p > 0:
                    w.late(b, p - 1, z)
                elif not first:
                    w.late(b - 1, NP - 1, 1 - z)
                if p < NP - 2:
                    w.ahead(b, p + 2, z)
                elif not last:
                    w.ahead(b + 1, p + 2 - NP, 1 - z)
                if not (last and p == NP - 1):
                    w.score(b, p + 1, z) if p < NP - 1 else w.score(b + 1, 0, 1 - z)
                if p in (3, 5, 7):
                    w.rows(b, (p - 3) // 2, z)
                if not first:
                    if p == 1:
                        w.rows(b - 1, 3, 1 - z)
                    if p == 2:
                        w.turn_y(b - 1, 1 - z)
                    if p == 3:
                        w.project(b - 1)
                    if p == 4:
                        w.add(b - 1)
                if not before_last:
                    if p == 4:
                        w.norm(b + 2)
                    if p == 5:
                        w.turn_x(b + 2)
                    if p == 6:
                        w.make_heads(b + 2)

        for b in range(2):
            for step in (w.norm, w.turn_x, w.split_x, w.make_heads, w.squares):
                step(b)
            if b == 0:
                w.head_norm(0, 0)
                w.stack(0, 0)
                w.stack_low(0, 0)
                w.ahead(0, 0, 0)
                w.score(0, 0, 0)
                w.ahead(0, 1, 0)
        batch(0, 0)
        with eng.Fori(0, (B - 4) // 2) as i:
            batch(2 * i + 1, 1)
            batch(2 * i + 2, 0)
        for b in range(B - 3, B):
            batch(b, b % 2)
        w.late(B - 1, NP - 1, 1)
        w.rows(B - 1, 3, 1)
        w.turn_y(B - 1, 1)
        for step in (w.split_y, w.project, w.add):
            step(B - 1)

    def either(eng, work):
        eng.wait_ge(gq_ready, 1)
        large = eng.value_load(is_large[0:1, 0:1], min_val=0, max_val=1)
        with eng.If(large > 0):
            schedule(eng, work(True))
        with eng.Else():
            schedule(eng, work(False))

    class Work:
        def __init__(self, maxima):
            self.maxima = maxima
        def norm(self, b): pass
        def turn_x(self, b): pass
        def split_x(self, b): pass
        def make_heads(self, b): pass
        def squares(self, b): pass
        def head_norm(self, b, z): pass
        def stack(self, b, z): pass
        def stack_low(self, b, z): pass
        def ahead(self, b, p, z): pass
        def now(self, b, p, z): pass
        def score(self, b, p, z): pass
        def late(self, b, p, z): pass
        def rows(self, b, g, z): pass
        def turn_y(self, b, z): pass
        def split_y(self, b): pass
        def project(self, b): pass
        def add(self, b): pass

    block = ctx.enter_context(nc.Block())

    @block.sync
    def _(sp):
        sp.dma_start(wt_stage[:], A["L0_attn_WT"].rearrange("(k p) n -> p k n", p=P)).then_inc(loaded, 16)
        sp.dma_start(w_stage[:], A["L0_attn_W"].rearrange("(k p) n -> p k n", p=P)).then_inc(loaded, 16)
        for g, name in ((g1, "L0_attn_g1"), (g2, "L0_attn_g2"), (g3, "L0_attn_g3")):
            sp.dma_start(g[:], A[name].rearrange("(o d) -> o d", o=1).broadcast_to([P, DH])).then_inc(loaded, 16)

    @block.tensor
    def _(pe):
        class PE(Work):
            def turn_x(self, b):
                pe.wait_ge(xn_ready, b + 1)
                at_least(pe, u_ready, b)
                for k in range(KB):
                    for s in range(S):
                        last = pe.transpose(tr[:, (k * S + s) * P:(k * S + s + 1) * P],
                                            xn[:, s, k * P:(k + 1) * P], m.ident[:])
                last.then_inc(xt_in_psum, 1)

            def make_heads(self, b):
                pe.wait_ge(xth, b + 1)
                pe.wait_ge(xtl, b + 1)
                xt, wt = (xt_hi, xt_lo), (wt_hi, wt_lo)
                for s in range(S):
                    last = split_product(
                        pe, tr[:, s * D:(s + 1) * D],
                        lambda a, k: xt[a][:, (k * S + s) * P:(k * S + s + 1) * P],
                        lambda a, k: wt[a][:, k, :], KB)
                last.then_inc(w_ready, 1)

            def ahead(self, b, p, z):
                n = NP * b + p
                if p == 0:
                    pe.wait_ge(kst_ready, b + 1)
                    pe.wait_ge(qst_ready, b + 1)
                at_least(pe, qkt_ready, n)
                for j, st in enumerate((qst, kst)):
                    for s in range(S):
                        rows = st[:, z, s * NH + 2 * p:s * NH + 2 * p + 2, :, :]
                        last = pe.transpose(qkp[:, (2 * j + s) * P:(2 * j + s + 1) * P],
                                            f32(rows.rearrange("p h r d -> p (h r d)")), m.ident[:])
                last.then_inc(qk_in_psum, 1)

            def score(self, b, p, z):
                n = NP * b + p
                pe.wait_ge(qkt_ready, n + 1)
                at_least(pe, exp_done, n - 1)
                for h in range(2):
                    for s in range(S):
                        last = pe.matmul(scores[:, p % 2, h, s, :],
                                         qkt[64 * h:64 * h + 3 * DH, p % 2, s * P:(s + 1) * P],
                                         qkt[64 * h:64 * h + 3 * DH, p % 2, 2 * P:4 * P], start=True, stop=True)
                last.then_inc(s_ready, 1)

            def late(self, b, p, z):
                n = NP * b + p
                pe.wait_ge(vr_ready, n + 1)
                if self.maxima:
                    for h in range(2):
                        for s in range(S):
                            for r in range(S):
                                last = pe.transpose(scores[:, p % 2, h, r, s * P:(s + 1) * P],
                                                    ebuf[:, p % 4, 2 * h + s, r * P:(r + 1) * P], m.ident[:])
                    last.then_inc(turned_in_psum, 1)
                    pe.wait_ge(turned_ready, n + 1)
                if p % 2 == 0:
                    at_least(pe, ytok_done, 4 * b + p // 2 - 1)
                sides = ((vv, turned[:]), (vs, ebuf[:, p % 4])) if self.maxima else ((vv, ebuf[:, p % 4]),)
                for s in range(S):
                    for h in range(2):
                        row = 32 * (2 * (p % 2) + h)
                        for i, (values, side) in enumerate(sides):
                            last = pe.matmul(av(p // 2)[row:row + 32, :],
                                             values[:, z, s * NH + 2 * p + h, :, :].rearrange("p r d -> p (r d)"),
                                             side[:, 2 * h + s, :], start=(s == 0 and i == 0),
                                             stop=(s == S - 1 and i == len(sides) - 1), skip_group_check=True)
                last.then_inc(av_done, 1)

            def rows(self, b, g, z):
                pe.wait_ge(outt_ready, 4 * b + g + 1)
                for s in range(S):
                    last = pe.transpose(yraw(g)[:, s * P:(s + 1) * P], outt[:, g % 2, s * P:(s + 1) * P], m.ident[:])
                last.then_inc(yraw_in_psum, 1)

            def turn_y(self, b, z):
                pe.wait_ge(ytok_done, 4 * b + 4)
                pe.wait_ge(u_ready, upto(b + 3, B))
                for k in range(KB):
                    for s in range(S):
                        last = pe.transpose(tr[:, (k * S + s) * P:(k * S + s + 1) * P],
                                            ytok[:, z, s, k * P:(k + 1) * P], m.ident[:])
                last.then_inc(yt_in_psum, 1)

            def project(self, b):
                pe.wait_ge(yth, b + 1)
                pe.wait_ge(ytl, b + 1)
                yt, w = (yt_hi, yt_lo), (w_hi, w_lo)
                for s in range(S):
                    last = split_product(
                        pe, tr[:, s * D:(s + 1) * D],
                        lambda a, k: yt[a][:, (k * S + s) * P:(k * S + s + 1) * P],
                        lambda a, k: w[a][:, k, :], KB)
                last.then_inc(proj_done, 1)

        pe.wait_ge(w_split, 1)
        either(pe, PE)

    @block.scalar
    def _(act):
        class Act(Work):
            def split_x(self, b):
                act.wait_ge(xt_in_psum, b + 1)
                act.activation(xt_hi[:], tr, ACT.Copy).then_inc(xth, 1)

            def squares(self, b):
                act.wait_ge(w_ready, b + 1)
                at_least(act, ms_done, b)
                act.activation(sq[:].rearrange("p h d -> p (h d)"), tr, ACT.Square).then_inc(sq_done, 1)

            def stack(self, b, z):
                at_least(act, qk_in_psum, NP * (b - 1))
                act.wait_ge(u_ready, b + 1)
                act.activation(kst[:, z, :, 0:3:2, :], u[:].unsqueeze(2).broadcast_to([P, S * NH, 2, DH]),
                               ACT.Copy).then_inc(kh_done, 1)
                act.wait_ge(q_done, b + 1)
                act.activation(qst[:, z, :, 0:2, :], q[:].unsqueeze(2).broadcast_to([P, S * NH, 2, DH]),
                               ACT.Copy).then_inc(qh_done, 1)

            def ahead(self, b, p, z):
                n = NP * b + p
                act.wait_ge(qk_in_psum, n + 1)
                at_least(act, s_ready, n - 1)
                act.activation(qkt[:, p % 2, :], qkp, ACT.Copy).then_inc(qkt_ready, 1)

            def score(self, b, p, z):
                n = NP * b + p
                act.wait_ge(s_ready, n + 1)
                at_least(act, av_done, n - 3)
                at_least(act, sum_done, n - 3)
                if self.maxima:
                    act.wait_ge(max_ready, n + 1)
                    for h in range(2):
                        for s in range(S):
                            last = act.activation(ebuf[:, p % 4, 2 * h + s, :], scores[:, p % 2, h, s, :], ACT.Exp,
                                                  bias=neg_max[:, p % 2, 2 * h + s:2 * h + s + 1])
                    last.then_inc(exp_done, 1)
                else:
                    act.activation(ebuf[:, p % 4, :, :], scores[:, p % 2, :, :, :].rearrange("p h s t -> p (h s) t"),
                                   ACT.Exp).then_inc(exp_done, 1)

            def late(self, b, p, z):
                if self.maxima:
                    act.wait_ge(turned_in_psum, NP * b + p + 1)
                    at_least(act, av_done, NP * b + p)
                    act.activation(turned[:], scores[:, p % 2, :, :, :].rearrange("p h s t -> p (h s) t"),
                                   ACT.Copy).then_inc(turned_ready, 1)
                if p % 2 == 1:
                    n = 4 * b + p // 2
                    act.wait_ge(av_done, 2 * n + 2)
                    at_least(act, yraw_in_psum, n - 1)
                    act.activation(outt[:, p // 2 % 2, :], av(p // 2), ACT.Copy).then_inc(outt_ready, 1)

            def split_y(self, b):
                act.wait_ge(yt_in_psum, b + 1)
                act.activation(yt_hi[:], tr, ACT.Copy).then_inc(yth, 1)

        act.preload_act_table(ACT.Exp)
        act.wait_ge(loaded, 80)
        act.activation(wt_hi[:], wt_stage[:], ACT.Copy)
        act.activation(w_hi[:], w_stage[:], ACT.Copy).then_inc(whi_done, 1)
        either(act, Act)

    @block.vector
    def _(dve):
        class Dve(Work):
            def norm(self, b):
                at_least(dve, xt_in_psum, b)
                for s in range(S):
                    at = bass.ds(S * b + s, 1)
                    last = dve.tensor_scalar(xn[:, s:s + 1, :], m.x_res[:, at, :], m.mv[:, at, 0],
                                             m.rstd[:, at], ALU.subtract, ALU.mult)
                last.then_inc(xn_ready, 1)

            def split_x(self, b):
                dve.wait_ge(xth, b + 1)
                dve.tensor_tensor(xt_lo[:], tr, f32(xt_hi[:]), ALU.subtract).then_inc(xtl, 1)

            def squares(self, b):
                dve.wait_ge(sq_done, b + 1)
                at_least(dve, mse_done, b)
                dve.tensor_reduce(ms[:], sq[:], AX_X, ALU.add).then_inc(ms_done, 1)
                dve.wait_ge(ms_done, b + 1)
                at_least(dve, rr_ready, b)
                dve.tensor_scalar(ms_eps[:], ms[:], 1.0 / DH, RMS_EPS, ALU.mult, ALU.add).then_inc(mse_done, 1)

            def head_norm(self, b, z):
                dve.wait_ge(rr_ready, b + 1)
                at_least(dve, qh_done, b)
                at_least(dve, qst_ready, b)
                wide = lambda g: g[:].unsqueeze(1).broadcast_to([P, S * NH, DH])
                dve.tensor_tensor(u[:], tr.rearrange("p (h d) -> p h d", d=DH),
                                  rr[:].unsqueeze(2).broadcast_to([P, S * NH, DH]), ALU.mult).then_inc(u_ready, 1)
                dve.wait_ge(u_ready, b + 1)
                dve.tensor_tensor(q[:], u[:], wide(gq), ALU.mult).then_inc(q_done, 1)
                at_least(dve, av_done, NP * (b - 1))
                dve.tensor_tensor(vv[:, z, :, 0, :], u[:], wide(g3), ALU.mult).then_inc(v_ready, 1)

            def stack_low(self, b, z):
                at_least(dve, qk_in_psum, NP * (b - 1))
                dve.wait_ge(kh_done, b + 1)
                dve.tensor_tensor(kst[:, z, :, 1, :], u[:], f32(kst[:, z, :, 0, :]), ALU.subtract).then_inc(kst_ready, 1)
                dve.wait_ge(qh_done, b + 1)
                dve.tensor_tensor(qst[:, z, :, 2, :], q[:], f32(qst[:, z, :, 0, :]), ALU.subtract).then_inc(qst_ready, 1)

            def score(self, b, p, z):
                if self.maxima:
                    n = NP * b + p
                    dve.wait_ge(s_ready, n + 1)
                    at_least(dve, exp_done, n - 1)
                    dve.tensor_reduce(row_max[:, p % 2, :], scores[:, p % 2, :, :, :].rearrange("p h s t -> p (h s) t"),
                                      AX_X, ALU.max).then_inc(max_found, 1)
                    dve.wait_ge(max_found, n + 1)
                    dve.tensor_scalar(neg_max[:, p % 2, :], row_max[:, p % 2, :], -1.0, None, ALU.mult).then_inc(max_ready, 1)

            def now(self, b, p, z):
                n = NP * b + p
                dve.wait_ge(exp_done, n + 1)
                dve.tensor_reduce(ssum[:, z, 4 * p:4 * p + 4], ebuf[:, p % 4, :, :], AX_X, ALU.add).then_inc(sum_done, 1)
                dve.wait_ge(sum_done, n + 1)
                dve.reciprocal(rs[:, z, 4 * p:4 * p + 4], ssum[:, z, 4 * p:4 * p + 4]).then_inc(rs_done, 1)
                dve.wait_ge(rs_done, n + 1)
                if p == 0:
                    dve.wait_ge(v_ready, b + 1)
                v1, v2 = (t[:, z, :, :, :].rearrange("p (s h) r d -> p s h r d", s=S)[:, :, 2 * p:2 * p + 2, :, :]
                          for t in (vv, vs if self.maxima else vv))
                r2 = rs[:, z, 4 * p:4 * p + 4].rearrange("p (h s) -> p s h", s=S)
                dve.tensor_tensor(v2[:, :, :, 1, :], v1[:, :, :, 0, :],
                                  r2.unsqueeze(3).broadcast_to([P, S, 2, DH]), ALU.mult).then_inc(vr_ready, 1)

            def rows(self, b, g, z):
                dve.wait_ge(yraw_in_psum, 4 * b + g + 1)
                at_least(dve, ytok_done, 4 * b + g)
                raw = yraw(g).rearrange("p (s h r d) -> p s h r d", s=S, h=4, r=2)
                r4 = rs[:, z, 4 * g * S:4 * (g + 1) * S].rearrange("p (h s) -> p s h", s=S)
                dve.tensor_tensor(ytmp[:], raw[:, :, :, 0, :], r4.unsqueeze(3).broadcast_to([P, S, 4, DH]),
                                  ALU.mult).then_inc(ytmp_done, 1)
                dve.wait_ge(ytmp_done, 4 * b + g + 1)
                dve.tensor_tensor(ytok[:, z, :, 4 * g * DH:4 * (g + 1) * DH].rearrange("p s (h d) -> p s h d", d=DH),
                                  raw[:, :, :, 1, :], ytmp[:], ALU.add).then_inc(ytok_done, 1)

            def split_y(self, b):
                dve.wait_ge(yth, b + 1)
                dve.tensor_tensor(yt_lo[:], tr, f32(yt_hi[:]), ALU.subtract).then_inc(ytl, 1)

            def add(self, b):
                dve.wait_ge(proj_done, b + 1)
                two = m.x_res[:, bass.ds(S * b, S), :]
                dve.tensor_tensor(two, two, tr.rearrange("p (s c) -> p s c", s=S), ALU.add).then_inc(x1_done, 1)
                dve.wait_ge(x1_done, b + 1)
                for s in range(S):
                    at = bass.ds(S * b + s, 1)
                    last = dve.bn_stats(m.bn6[:, at, :].rearrange("p a c -> p (a c)"),
                                        m.x_res[:, at, :].rearrange("p a c -> p (a c)"))
                last.then_inc(bn_done, 1)

        steps = [0]

        def then(ins):
            steps[0] += 1
            ins.then_inc(gq_step, 1)
            dve.wait_ge(gq_step, steps[0])

        dve.wait_ge(loaded, 80)
        then(dve.tensor_tensor(gq[:], g1[:], g2[:], ALU.mult))
        then(dve.tensor_scalar(gq[:], gq[:], float(DH) ** -0.5, None, ALU.mult))
        then(dve.tensor_scalar(neg_gq[:], gq[:], -1.0, None, ALU.mult))
        then(dve.tensor_tensor(abs_gq[:], gq[:], neg_gq[:], ALU.max))
        then(dve.tensor_reduce(most_gq[:], abs_gq[:], AX_X, ALU.max))
        then(dve.tensor_scalar(bound_large[:], most_gq[:], float(DH), SMALL_BOUND, ALU.mult, ALU.is_gt))
        dve.tensor_copy(is_large[:], bound_large[:]).then_inc(gq_ready, 1)
        dve.wait_ge(whi_done, 1)
        dve.tensor_tensor(wt_lo[:], wt_stage[:], f32(wt_hi[:]), ALU.subtract)
        dve.tensor_tensor(w_lo[:], w_stage[:], f32(w_hi[:]), ALU.subtract).then_inc(w_split, 1)
        dve.wait_ge(gaps_zero, 1)
        either(dve, Dve)
        dve.wait_ge(bn_done, B)
        aggregate(dve, m, aggr_done)
        dve.tensor_scalar(m.var_eps[:], m.mv[:, :, 1], LN_EPS, None, ALU.add).then_inc(eps_done, 1)

    @block.gpsimd
    def _(pool):
        class Pool(Work):
            def squares(self, b):
                pool.wait_ge(mse_done, b + 1)
                at_least(pool, u_ready, b)
                pool.tensor_tensor(rr[:], ms_eps[:], m.neg_half[:, 0:S * NH], ALU.pow).then_inc(rr_ready, 1)

        pool.memset(vv[:, :, :, 1, :], 0.0)
        pool.memset(vs[:], 0.0)
        pool.memset(f32(qst[:, :, :, 3, :]), 0.0)
        pool.memset(f32(kst[:, :, :, 3, :]), 0.0).then_inc(gaps_zero, 1)
        schedule(pool, Pool(False))
        pool.wait_ge(eps_done, 1)
        pool.tensor_tensor(m.rstd[:], m.var_eps[:], m.neg_half[:, 0:NT], ALU.pow).then_inc(rstd_done, 1)


class Mixture:
    def __init__(self, tag, experts, hidden, gated, shared, slope, lin_bias):
        self.tag, self.experts, self.hidden, self.shared = tag, experts, hidden, shared
        self.gated = gated
        self.slope = slope
        self.lin_bias = lin_bias
        self.groups = NT + experts - 1
        self.tiles = S * self.groups
        self.hb = hidden // P


def mixture_memory(nc, v, ctx):
    k = Names()
    sb = lambda name, shape, dt=F32: ctx.enter_context(nc.sbuf_tensor(f"{v.tag}_{name}", shape, dt))
    k.w13_hi, k.w13_lo = (sb(n, [P, v.experts, KB, 2 * v.hidden], F32R) for n in ("w13_hi", "w13_lo"))
    k.w2_hi, k.w2_lo = (sb(n, [P, v.experts, v.hb, D], F32R) for n in ("w2_hi", "w2_lo"))
    k.logits = sb("logits", [P, v.experts, NT])
    k.weight = sb("weight", [P, 2, NT])
    k.pos = sb("pos", [P, 2, NT], mybir.dt.int32)
    k.token_of = sb("token_of", [P, v.tiles], mybir.dt.int32)
    k.expert_of = sb("expert_of", [P, v.groups], mybir.dt.int32)
    if v.lin_bias:
        k.b1, k.b2 = sb("b1", [2, v.experts, 2 * v.hidden], F32R), sb("b2", [2, v.experts, D], F32R)
    k.xn_dram = nc.dram_tensor(f"{v.tag}_xn", [TOK, D], F32).ap()
    k.y_dram = nc.dram_tensor(f"{v.tag}_y", [v.tiles * P, D], F32).ap()
    return k


def router_phase(nc, m, A, v, k, ctx):
    E, HS = v.experts, 256
    HSB = HS // P
    sb = lambda name, shape, dt=F32: ctx.enter_context(nc.sbuf_tensor(f"{v.tag}r_{name}", shape, dt))
    sem = lambda name: nc.alloc_semaphore(f"{v.tag}r_{name}")
    xn = sb("xn", [P, 2, S, D])
    xt_hi, xt_lo = sb("xt_hi", [P, 2, KB, S * P], F32R), sb("xt_lo", [P, 2, KB, S * P], F32R)
    gate_stage = sb("gate_stage", [P, KB, E])
    gate_hi, gate_lo = sb("gate_hi", [P, KB, E], F32R), sb("gate_lo", [P, KB, E], F32R)
    gate_b = sb("gate_b", [P, E])
    w_shapes = ((KB, 2 * v.hidden), (v.hb, D))
    w_kinds = ((0,), (1,)) if 2 * E == B else ((0, 1), (0, 1))
    stages = {(kind, z): sb(f"stage{kind}{z}", [P, *w_shapes[kind]]) for z in range(2) for kind in w_kinds[z]}
    if v.shared:
        s13_hi, s13_lo = sb("s13_hi", [P, KB, 2 * HS], F32R), sb("s13_lo", [P, KB, 2 * HS], F32R)
        s13_stage, s2_stage = sb("s13_stage", [P, KB, 2 * HS]), sb("s2_stage", [P, HSB, D])
        s2_hi, s2_lo = sb("s2_hi", [P, HSB, D], F32R), sb("s2_lo", [P, HSB, D], F32R)
        th, s1, h = (sb(n, [P, 2, HSB * S * P]) for n in ("th", "s1", "h"))
        h_hi, h_lo = sb("h_hi", [P, 2, HSB, S * P], F32R), sb("h_lo", [P, 2, HSB, S * P], F32R)
    if v.lin_bias:
        bias_stage1, bias_stage2 = sb("bias1", [2, E, 2 * v.hidden]), sb("bias2", [2, E, D])

    (small_here, shared_here, xn_ready, stored0, stored1, xt_in_psum, xth, xtl, lg_in_psum, lg_done, up_done,
     th_done, s1_done, h_done, hh_done, hl_done, down_done, added, hi_done, lo_done, gate_done, bias_done) = (
        sem(n) for n in
        "small_here shared_here xn_ready stored0 stored1 xt_in_psum xth xtl lg_in_psum lg_done up_done "
        "th_done s1_done h_done hh_done hl_done down_done added hi_done lo_done gate_done bias_done".split())
    stage_here, w_hi_done, w_lo_done = ({key: sem(f"{n}{key[0]}{key[1]}") for key in stages}
                                        for n in ("stage_here", "w_hi_done", "w_lo_done"))
    stored = (stored0, stored1)
    if not v.shared:
        up_done = lg_in_psum
    w_dram = (A["w13T"].rearrange("e (k p) n -> p e k n", p=P), A["w2T"].rearrange("e (k p) n -> p e k n", p=P))
    w_parts = ((k.w13_hi, k.w13_lo), (k.w2_hi, k.w2_lo))
    expert_at = lambda c, half: bass.ds(half if 2 * E == B else c, 1)
    one = lambda ap: ap.rearrange("p o k n -> p (o k) n")

    C = B

    def schedule(eng, w):
        def slot(c, z, half):
            at = c if isinstance(c, int) else 1
            if v.shared and at > 0:
                w.second_h(c - 1, 1 - z)
            if at < C - 2:
                w.norm(c + 2, z, half + 1)
            if at < C - 1:
                w.turn(c + 1, 1 - z)
            w.products(c, z)
            if v.shared and at > 0:
                w.down(c - 1, 1 - z)
            w.weights(c, z, half)
        w.norm(0, 0, 0)
        w.norm(1, 1, 0)
        w.turn(0, 0)
        slot(0, 0, 0)
        slot(1, 1, 0)
        with eng.Fori(0, (C - 4) // 2) as i:
            slot(2 * i + 2, 0, i + 1)
            slot(2 * i + 3, 1, i + 1)
        for c in (C - 2, C - 1):
            slot(c, c % 2, c // 2)
        if v.shared:
            w.second_h(C - 1, 1)
            w.down(C - 1, 1)

    class Work:
        def norm(self, c, z, half): pass
        def turn(self, c, z): pass
        def products(self, c, z): pass
        def second_h(self, c, z): pass
        def down(self, c, z): pass
        def weights(self, c, z, half): pass

    block = ctx.enter_context(nc.Block())
    small = 16 * (1 + 3 * bool(v.lin_bias))

    @block.sync
    def _(sp):
        sp.dma_start(gate_stage[:], A["gateT"].rearrange("(k p) n -> p k n", p=P)).then_inc(small_here, 16)
        if v.lin_bias:
            sp.dma_start(gate_b[:], A["gate_b"].rearrange("(o d) -> o d", o=1).broadcast_to([P, E])).then_inc(small_here, 16)
            sp.dma_start(bias_stage1[:], A["b1"].rearrange("(o e) n -> o e n", o=1).broadcast_to([2, E, 2 * v.hidden])).then_inc(small_here, 16)
            sp.dma_start(bias_stage2[:], A["b2"].rearrange("(o e) n -> o e n", o=1).broadcast_to([2, E, D])).then_inc(small_here, 16)

        if v.shared:
            sp.dma_start(s13_stage[:], A["s13T"].rearrange("(k p) n -> p k n", p=P)).then_inc(shared_here, 16)
            sp.dma_start(s2_stage[:], A["s2T"].rearrange("(k p) n -> p k n", p=P)).then_inc(shared_here, 16)

        class Sp(Work):
            def norm(self, c, z, half):
                sp.wait_ge(xn_ready, c + 1)
                sp.dma_start(k.xn_dram.rearrange("(c s p) d -> c p s d", s=S, p=P)[bass.ds(c, 1)].rearrange("c p s d -> p (c s) d"),
                             xn[:, z]).then_inc(stored[z], 16)

            def weights(self, c, z, half, first=False):
                if isinstance(c, int) and c >= C - 2:
                    return
                for kind in w_kinds[z]:
                    if not first:
                        sp.wait_ge(w_lo_done[kind, z], half + 1)
                    sp.dma_start(stages[kind, z][:].unsqueeze(1), w_dram[kind][:, expert_at(c + 2, half + 1), :, :]).then_inc(stage_here[kind, z], 16)

        Sp().weights(-2, 0, -1, first=True)
        Sp().weights(-1, 1, -1, first=True)
        schedule(sp, Sp())
        for z in range(2):
            sp.wait_ge(stored[z], 16 * C // 2)

    @block.tensor
    def _(pe):
        class PE(Work):
            def turn(self, c, z):
                pe.wait_ge(xn_ready, c + 1)
                at_least(pe, xth, c)
                at_least(pe, xtl, c)
                for kb in range(KB):
                    for s in range(S):
                        last = pe.transpose(m.banks[:, 0, (kb * S + s) * P:(kb * S + s + 1) * P],
                                            xn[:, z, s, kb * P:(kb + 1) * P], m.ident[:])
                last.then_inc(xt_in_psum, 1)

            def products(self, c, z):
                pe.wait_ge(xth, c + 1)
                pe.wait_ge(xtl, c + 1)
                at_least(pe, lg_done, c)
                xt, gate = (xt_hi, xt_lo), (gate_hi, gate_lo)
                for s in range(S):
                    last = split_product(pe, m.banks[:, 1, s * E:(s + 1) * E],
                                         lambda a, kb: xt[a][:, z, kb, s * P:(s + 1) * P],
                                         lambda a, kb: gate[a][:, kb, :], KB)
                last.then_inc(lg_in_psum, 1)
                if v.shared:
                    at_least(pe, h_done, c - 1)
                    s13 = (s13_hi, s13_lo)
                    for j in range(2):
                        for hb in range(HSB):
                            col = j * HS + hb * P
                            last = split_product(pe, m.banks[:, 2 + 2 * z + j, hb * S * P:(hb + 1) * S * P],
                                                 lambda a, kb: s13[a][:, kb, col:col + P],
                                                 lambda a, kb: xt[a][:, z, kb, :], KB)
                    last.then_inc(up_done, 1)

            def down(self, c, z):
                pe.wait_ge(hh_done, c + 1)
                pe.wait_ge(hl_done, c + 1)
                at_least(pe, added, c)
                hp, s2 = (h_hi, h_lo), (s2_hi, s2_lo)
                for s in range(S):
                    last = split_product(pe, m.banks[:, 6 + z, s * D:(s + 1) * D],
                                         lambda a, kb: hp[a][:, z, kb, s * P:(s + 1) * P],
                                         lambda a, kb: s2[a][:, kb, :], HSB)
                last.then_inc(down_done, 1)

        pe.wait_ge(gate_done, 2)
        if v.shared:
            pe.wait_ge(lo_done, 1)
        schedule(pe, PE())

    @block.scalar
    def _(act):
        class Act(Work):
            def turn(self, c, z):
                act.wait_ge(xt_in_psum, c + 1)
                at_least(act, up_done, c - 1)
                act.activation(xt_hi[:, z].rearrange("p k t -> p (k t)"), m.banks[:, 0, :], ACT.Copy).then_inc(xth, 1)

            def products(self, c, z):
                if v.shared:
                    act.wait_ge(up_done, c + 1)
                    at_least(act, s1_done, c - 1)
                    act.activation(th[:, z], m.banks[:, 2 + 2 * z, :], ACT.Tanh, scale=v.slope / 2).then_inc(th_done, 1)

            def second_h(self, c, z):
                act.wait_ge(h_done, c + 1)
                at_least(act, down_done, c)
                act.activation(h_hi[:, z].rearrange("p k t -> p (k t)"), h[:, z], ACT.Copy).then_inc(hh_done, 1)

            def weights(self, c, z, half):
                for kind in w_kinds[z]:
                    act.wait_ge(stage_here[kind, z], 16 * (half + 1))
                    act.activation(one(w_parts[kind][0][:, expert_at(c, half), :, :]), stages[kind, z][:],
                                   ACT.Copy).then_inc(w_hi_done[kind, z], 1)

        act.preload_act_table(ACT.Exp)
        if v.shared:
            act.wait_ge(shared_here, 32)
            act.activation(s13_hi[:], s13_stage[:], ACT.Copy)
            act.activation(s2_hi[:], s2_stage[:], ACT.Copy).then_inc(hi_done, 1)
        schedule(act, Act())

    @block.vector
    def _(dve):
        class Dve(Work):
            def norm(self, c, z, half):
                at_least(dve, xt_in_psum, c - 1)
                if not (isinstance(c, int) and c < 2):
                    dve.wait_ge(stored[z], 16 * half)
                for s in range(S):
                    at = bass.ds(S * c + s, 1)
                    last = dve.tensor_scalar(xn[:, z, s:s + 1, :], m.x_res[:, at, :], m.mv[:, at, 0],
                                             m.rstd[:, at], ALU.subtract, ALU.mult)
                last.then_inc(xn_ready, 1)

            def turn(self, c, z):
                dve.wait_ge(xth, c + 1)
                at_least(dve, up_done, c - 1)
                dve.tensor_tensor(xt_lo[:, z].rearrange("p k t -> p (k t)"), m.banks[:, 0, :],
                                  f32(xt_hi[:, z]).rearrange("p k t -> p (k t)"), ALU.subtract).then_inc(xtl, 1)

            def products(self, c, z):
                dve.wait_ge(lg_in_psum, c + 1)
                out = k.logits[:, :, bass.ds(S * c, S)]
                lg = m.banks[:, 1, 0:S * E].rearrange("p (s e) -> p e s", s=S)
                if v.lin_bias:
                    ins = dve.tensor_tensor(out, lg, gate_b[:].unsqueeze(2).broadcast_to([P, E, S]), ALU.add)
                else:
                    ins = dve.tensor_copy(out, lg)
                ins.then_inc(lg_done, 1)
                if v.shared:
                    dve.wait_ge(th_done, c + 1)
                    at_least(dve, h_done, c - 1)
                    dve.scalar_tensor_tensor(out=s1[:, z], in0=th[:, z], scalar=1.0, in1=m.banks[:, 2 + 2 * z, :],
                                             op0=ALU.add, op1=ALU.mult).then_inc(s1_done, 1)
                    dve.wait_ge(s1_done, c + 1)
                    at_least(dve, hh_done, c - 1)
                    dve.scalar_tensor_tensor(out=h[:, z], in0=s1[:, z], scalar=0.5, in1=m.banks[:, 3 + 2 * z, :],
                                             op0=ALU.mult, op1=ALU.mult).then_inc(h_done, 1)

            def second_h(self, c, z):
                dve.wait_ge(hh_done, c + 1)
                at_least(dve, down_done, c)
                dve.tensor_tensor(h_lo[:, z].rearrange("p k t -> p (k t)"), h[:, z],
                                  f32(h_hi[:, z]).rearrange("p k t -> p (k t)"), ALU.subtract).then_inc(hl_done, 1)

            def down(self, c, z):
                dve.wait_ge(down_done, c + 1)
                two = m.x_res[:, bass.ds(S * c, S), :]
                dve.tensor_tensor(two, two, m.banks[:, 6 + z, :].rearrange("p (s c) -> p s c", s=S), ALU.add).then_inc(added, 1)

            def weights(self, c, z, half):
                for kind in w_kinds[z]:
                    dve.wait_ge(w_hi_done[kind, z], half + 1)
                    hi, lo = (one(part[:, expert_at(c, half), :, :]) for part in w_parts[kind])
                    dve.tensor_tensor(lo, stages[kind, z][:], f32(hi), ALU.subtract).then_inc(w_lo_done[kind, z], 1)

        dve.wait_ge(small_here, small)
        dve.tensor_copy(gate_hi[:], gate_stage[:]).then_inc(gate_done, 1)
        dve.wait_ge(gate_done, 1)
        dve.tensor_tensor(gate_lo[:], gate_stage[:], f32(gate_hi[:]), ALU.subtract).then_inc(gate_done, 1)
        if v.lin_bias:
            flat = lambda t: t[:].rearrange("p e n -> p (e n)")
            for st, out in ((bias_stage1, k.b1), (bias_stage2, k.b2)):
                last = dve.tensor_copy(out[:], st[:])
            last.then_inc(bias_done, 1)
            dve.wait_ge(bias_done, 1)
            for st, out in ((bias_stage1, k.b1), (bias_stage2, k.b2)):
                last = dve.scalar_tensor_tensor(out=flat(out), in0=f32(flat(out)), scalar=m.neg_row[0:2, 0:1],
                                                in1=flat(st), op0=ALU.mult, op1=ALU.add)
            last.then_inc(bias_done, 1)
        if v.shared:
            dve.wait_ge(hi_done, 1)
            dve.tensor_tensor(s13_lo[:], s13_stage[:], f32(s13_hi[:]), ALU.subtract)
            dve.tensor_tensor(s2_lo[:], s2_stage[:], f32(s2_hi[:]), ALU.subtract).then_inc(lo_done, 1)
        schedule(dve, Dve())


def rank_phase(nc, m, v, k, ctx):
    E, NTL, NG = v.experts, v.tiles, v.groups
    I32, F16 = mybir.dt.int32, mybir.dt.float16
    sb = lambda name, shape, dt=F32: ctx.enter_context(nc.sbuf_tensor(f"{v.tag}k_{name}", shape, dt))
    sem = lambda name: nc.alloc_semaphore(f"{v.tag}k_{name}")
    lg = k.logits
    mx, oh, eq, imin = sb("mx", [P, 2, NT]), sb("oh", [P, 2, E, NT]), sb("eq", [P, E, NT]), sb("imin", [P, NT])
    lg2, both, ex, diff, ex2 = (sb("lg2", [P, E, NT]), sb("both", [P, E, NT]), sb("ex", [P, E, NT]),
                                sb("diff", [P, NT]), sb("ex2", [P, NT]))
    total = sb("total", [P, NT])
    count, before, zeros = sb("count", [P, E, NT]), sb("before", [P, E, NT]), sb("zeros", [P, E * NT])
    upto_here = sb("upto_here", [P, E, NT])
    ne, full, group_end, base = sb("ne", [P, E]), sb("full", [P, E, NT]), sb("group_end", [P, E]), sb("base", [P, E])
    groups_of = sb("groups_of", [P, E])
    rank, picked, posf = sb("rank", [P, E, NT]), sb("picked", [P, E, NT]), sb("posf", [P, 2, NT])
    tile_i, row_i = sb("tile_i", [P, 2 * NT], I32), sb("row_i", [P, 2 * NT], I32)
    tile_f, row_f = sb("tile_f", [P, 2 * NT]), sb("row_f", [P, 2 * NT])
    tile_oh, tile_tok = sb("tile_oh", [P, 2 * NT, NTL]), sb("tile_tok", [P, 2 * NT, NTL], F16)
    row_oh = sb("row_oh", [P, 2 * NT, P], F16)
    passed, ef = sb("passed", [P, NG, E]), sb("ef", [P, NG])
    step, scalar_step, picks, ranked, rows_ready, listed, zeros_ready = (
        sem(n) for n in "step scalar_step picks ranked rows_ready listed zeros_ready".split())

    e_last = lambda ap: ap.rearrange("p e t -> p t e")
    over_e = lambda ap: ap.unsqueeze(1).broadcast_to([P, E, NT])
    over_t = lambda ap: ap.unsqueeze(2).broadcast_to([P, E, NT])
    block = ctx.enter_context(nc.Block())

    @block.gpsimd
    def _(pool):
        pool.memset(zeros[:], 0.0).then_inc(zeros_ready, 1)

    @block.scalar
    def _(act):
        act.wait_ge(picks, 1)
        act.activation(ex[:], eq[:], ACT.Exp).then_inc(scalar_step, 1)
        act.activation(ex2[:], diff[:], ACT.Exp).then_inc(scalar_step, 1)

    @block.tensor
    def _(pe):
        pe.wait_ge(ranked, 1)
        flat = both[:].rearrange("p e t -> p (e t)")
        pe.matmul(m.banks[:, 0, 0:E * NT], m.upper[:], flat, start=True, stop=True)
        pe.matmul(m.banks[:, 1, 0:E * NT], m.ones[:], flat, start=True, stop=True).then_inc(listed, 1)
        pe.wait_ge(rows_ready, 1)
        for j in range(2 * NT):
            last = pe.matmul(m.banks[:, 2, 0:NTL], row_oh[:, j, :], tile_tok[:, j, :],
                             start=(j == 0), stop=(j == 2 * NT - 1))
        last.then_inc(listed, 1)

    @block.vector
    def _(dve):
        done = [0]

        def then(ins):
            done[0] += 1
            ins.then_inc(step, 1)
            dve.wait_ge(step, done[0])

        source = lg
        for c in range(2):
            then(dve.tensor_reduce(mx[:, c, :], e_last(source[:]), AX_X, ALU.max))
            then(dve.tensor_tensor(eq[:], source[:], over_e(mx[:, c, :]), ALU.is_equal))
            then(dve.tensor_tensor(eq[:], eq[:], over_t(m.expert_less[v.tag][:]), ALU.mult))
            then(dve.tensor_reduce(imin[:], e_last(eq[:]), AX_X, ALU.min))
            then(dve.tensor_tensor(oh[:, c], eq[:], over_e(imin[:]), ALU.is_equal))
            if c == 0:
                then(dve.scalar_tensor_tensor(out=lg2[:].rearrange("p e t -> p (e t)"),
                                              in0=oh[:, 0].rearrange("p e t -> p (e t)"), scalar=-3e38,
                                              in1=lg[:].rearrange("p e t -> p (e t)"), op0=ALU.mult, op1=ALU.add))
                source = lg2
        then(dve.tensor_tensor(both[:], oh[:, 0], oh[:, 1], ALU.add))
        dve.tensor_tensor(diff[:], mx[:, 1, :], mx[:, 0, :], ALU.subtract).then_inc(ranked, 1)
        dve.wait_ge(ranked, 1)
        dve.tensor_tensor(eq[:], lg[:], over_e(mx[:, 0, :]), ALU.subtract).then_inc(picks, 1)
        dve.wait_ge(scalar_step, 2)
        if v.gated == "all":
            then(dve.tensor_reduce(total[:], e_last(ex[:]), AX_X, ALU.add))
        else:
            then(dve.tensor_scalar(total[:], ex2[:], 1.0, None, ALU.add))
        then(dve.reciprocal(k.weight[:, 0, :], total[:]))
        then(dve.tensor_tensor(k.weight[:, 1, :], ex2[:], k.weight[:, 0, :], ALU.mult))

        dve.wait_ge(listed, 1)
        dve.wait_ge(zeros_ready, 1)
        flat = lambda t: t[:].rearrange("p e t -> p (e t)")
        then(dve.tensor_copy(flat(count), m.banks[:, 1, 0:E * NT]))
        then(dve.tensor_tensor_scan(flat(upto_here), flat(count), zeros[:], 0.0, ALU.add, ALU.add))
        then(dve.tensor_tensor(before[:], upto_here[:], count[:], ALU.subtract))
        then(dve.tensor_tensor(ne[:], upto_here[:, :, NT - 1], before[:, :, 0], ALU.subtract))
        then(dve.tensor_tensor(full[:], over_t(ne[:]), over_e(m.group_starts[:]), ALU.is_gt))
        then(dve.tensor_reduce(groups_of[:], full[:], AX_X, ALU.add))
        then(dve.tensor_tensor_scan(group_end[:], groups_of[:], zeros[:, 0:E], 0.0, ALU.add, ALU.add))
        then(dve.tensor_tensor(base[:], group_end[:], groups_of[:], ALU.subtract))
        then(dve.scalar_tensor_tensor(out=base[:], in0=base[:], scalar=float(S * P), in1=before[:, :, 0],
                                      op0=ALU.mult, op1=ALU.subtract))
        then(dve.tensor_tensor(flat(rank), m.banks[:, 0, 0:E * NT], flat(before), ALU.add))
        then(dve.tensor_tensor(rank[:], rank[:], over_t(base[:]), ALU.add))
        for c in range(2):
            then(dve.tensor_tensor(picked[:], rank[:], oh[:, c], ALU.mult))
            then(dve.tensor_reduce(posf[:, c, :], e_last(picked[:]), AX_X, ALU.add))
        then(dve.tensor_copy(k.pos[:], posf[:]))
        pos = k.pos[:].rearrange("p c t -> p (c t)")
        dve.tensor_scalar(tile_i[:], pos, 7, None, ALU.arith_shift_right)
        then(dve.tensor_scalar(row_i[:], pos, P - 1, None, ALU.bitwise_and))
        dve.tensor_copy(tile_f[:], tile_i[:])
        then(dve.tensor_copy(row_f[:], row_i[:]))
        wide = lambda ap, n: ap.unsqueeze(2).broadcast_to([P, 2 * NT, n])
        dve.tensor_tensor(row_oh[:], wide(row_f[:], P), m.count_up[:].unsqueeze(1).broadcast_to([P, 2 * NT, P]), ALU.is_equal)
        then(dve.tensor_tensor(tile_oh[:], wide(tile_f[:], NTL),
                               m.count_up[:, 0:NTL].unsqueeze(1).broadcast_to([P, 2 * NT, NTL]), ALU.is_equal))
        dve.tensor_tensor(tile_tok[:], tile_oh[:], wide(m.token[:], NTL), ALU.mult).then_inc(rows_ready, 1)
        then(dve.tensor_tensor(passed[:], group_end[:].unsqueeze(1).broadcast_to([P, NG, E]),
                               m.count_up[:, 0:NG].unsqueeze(2).broadcast_to([P, NG, E]), ALU.is_le))
        then(dve.tensor_reduce(ef[:], passed[:], AX_X, ALU.add))
        then(dve.tensor_scalar(ef[:], ef[:], float(E - 1), None, ALU.min))
        then(dve.tensor_copy(k.expert_of[:], ef[:]))
        dve.wait_ge(listed, 2)
        then(dve.tensor_copy(k.token_of[:], m.banks[:, 2, 0:NTL]))


def expert_phase(nc, m, v, k, ctx):
    HB, NG, HJ = v.hb, v.groups, S * v.hidden
    sb = lambda name, shape, dt=F32: ctx.enter_context(nc.sbuf_tensor(f"{v.tag}x_{name}", shape, dt))
    sem = lambda name: nc.alloc_semaphore(f"{v.tag}x_{name}")
    index, taken = sb("index", [P, 2, S], mybir.dt.uint32), sb("taken", [P, 2])
    xg = sb("xg", [P, 2, S, D])
    xt_hi, xt_lo = sb("xt_hi", [P, S * KB * P], F32R), sb("xt_lo", [P, S * KB * P], F32R)
    th, s1, h = (sb(n, [P, HJ]) for n in ("th", "s1", "h"))
    ht_hi, ht_lo = sb("ht_hi", [P, HJ], F32R), sb("ht_lo", [P, HJ], F32R)
    yout = sb("yout", [P, 2, S, D])
    (gathered0, gathered1, index_done, xt_in_psum, xth, xtl, glu_done, lin_done, th_done, s1_done, h_done,
     ht_in_psum, hth, htl, down_done, y_done, stored0, stored1) = (
        sem(n) for n in
        "gathered0 gathered1 index_done xt_in_psum xth xtl glu_done lin_done th_done s1_done h_done "
        "ht_in_psum hth htl down_done y_done stored0 stored1".split())
    gathered, stored = (gathered0, gathered1), (stored0, stored1)
    U = HJ // 512
    turns = 4 // (2 * U)
    glu = lambda z: m.banks[:, 2 * U * (z % turns):2 * U * (z % turns) + U, :].rearrange("p b n -> p (b n)")
    lin = lambda z: m.banks[:, 2 * U * (z % turns) + U:2 * U * (z % turns) + 2 * U, :].rearrange("p b n -> p (b n)")
    h_turned = m.banks[:, 4:4 + U, :].rearrange("p b n -> p (b n)")

    def schedule(eng, w):
        def slot(g, z, half, left=NG):
            if left > 2:
                w.gather(g + 2, z, half + 1)
            if left > 1:
                w.turn_x(g + 1, 1 - z, half + z)
            if not (isinstance(g, int) and g == 0):
                w.down(g - 1, 1 - z, half - (1 - z))
            w.turn_h(g)
            if left > 1:
                w.up(g + 1, 1 - z)
        w.gather(0, 0, 0)
        w.gather(1, 1, 0)
        w.turn_x(0, 0, 0)
        w.up(0, 0)
        for g in range(3):
            slot(g, g % 2, g // 2)
        pairs = (NG - 5) // 2
        with eng.Fori(0, pairs) as i:
            slot(2 * i + 3, 1, i + 1)
            slot(2 * i + 4, 0, i + 2)
        for g in range(2 * pairs + 3, NG):
            slot(g, g % 2, g // 2, left=NG - g)
        w.down(NG - 1, (NG - 1) % 2, (NG - 1) // 2)

    class Work:
        def gather(self, g, z, half): pass
        def turn_x(self, g, z, half): pass
        def up(self, g, z): pass
        def turn_h(self, g): pass
        def down(self, g, z, half): pass

    block = ctx.enter_context(nc.Block())

    @block.gpsimd
    def _(pool):
        class Pool(Work):
            def gather(self, g, z, half):
                at_least(pool, xt_in_psum, g - 1)
                pool.tensor_copy(index[:, z, :], k.token_of[:, bass.ds(S * g, S)]).then_inc(index_done, 1)
                pool.wait_ge(index_done, g + 1)
                pool.tensor_tensor(taken[:, z:z + 1], m.neg_row[:], m.neg_row[:], ALU.add)
                for j in range(S):
                    pool.indirect_dma_start(xg[:, z, j, :], None, k.xn_dram,
                                            bass.IndirectOffsetOnAxis(ap=index[:, z, j:j + 1], axis=0)).then_inc(gathered[z], 16)
        schedule(pool, Pool())

    @block.sync
    def _(sp):
        class Sp(Work):
            def down(self, g, z, half):
                sp.wait_ge(y_done, g + 1)
                sp.dma_start(k.y_dram.rearrange("(t p) d -> p t d", p=P)[:, bass.ds(S * g, S), :],
                             yout[:, z, :, :]).then_inc(stored[z], 16)
        schedule(sp, Sp())
        sp.wait_ge(stored0, 16 * ((NG + 1) // 2))
        sp.wait_ge(stored1, 16 * (NG // 2))

    @block.tensor
    def _(pe):
        class PE(Work):
            def turn_x(self, g, z, half):
                pe.wait_ge(gathered[z], 16 * S * (half + 1))
                at_least(pe, xtl, g)
                for j in range(S):
                    for kb in range(KB):
                        last = pe.transpose(m.banks[:, 6, (j * KB + kb) * P:(j * KB + kb + 1) * P],
                                            xg[:, z, j, kb * P:(kb + 1) * P], m.ident[:])
                last.then_inc(xt_in_psum, 1)

            def up(self, g, z):
                pe.wait_ge(xth, g + 1)
                pe.wait_ge(xtl, g + 1)
                at_least(pe, h_done, g + 1 - turns)
                e = pe.value_load(k.expert_of[0:1, bass.ds(g, 1)], min_val=0, max_val=v.experts - 1)
                xt, w13 = (xt_hi, xt_lo), (k.w13_hi, k.w13_lo)
                for b, (half, done) in enumerate(((glu(z), glu_done), (lin(z), lin_done))):
                    cols = slice(b * v.hidden, (b + 1) * v.hidden)
                    steps = [(kb, c) for kb in range(KB) for c in range(2)]
                    for i, (kb, c) in enumerate(steps):
                        weights = w13[c][:, bass.ds(e, 1), kb, cols]
                        for j in range(S):
                            out = half[:, j * v.hidden:(j + 1) * v.hidden]
                            for a in range(2 - c):
                                last = pe.matmul(out, xt[a][:, (j * KB + kb) * P:(j * KB + kb + 1) * P], weights,
                                                 start=(i == 0 and a == 0 and (j == 0 or U == S)),
                                                 stop=(i == len(steps) - 1 and not v.lin_bias and (j == 1 or U == S)))
                    if v.lin_bias:
                        for j in range(S):
                            last = pe.matmul(half[:, j * v.hidden:(j + 1) * v.hidden], m.ones_r[0:2, :],
                                             k.b1[:, bass.ds(e, 1), cols], start=False, stop=(j == S - 1))
                    last.then_inc(done, 1)

            def turn_h(self, g):
                pe.wait_ge(h_done, g + 1)
                at_least(pe, htl, g)
                for j in range(S * HB):
                    last = pe.transpose(h_turned[:, j * P:(j + 1) * P], h[:, j * P:(j + 1) * P], m.ident[:])
                last.then_inc(ht_in_psum, 1)

            def down(self, g, z, half):
                pe.wait_ge(hth, g + 1)
                pe.wait_ge(htl, g + 1)
                at_least(pe, y_done, g)
                e = pe.value_load(k.expert_of[0:1, bass.ds(g, 1)], min_val=0, max_val=v.experts - 1)
                ht, w2 = (ht_hi, ht_lo), (k.w2_hi, k.w2_lo)
                steps = [(hb, c) for hb in range(HB) for c in range(2)]
                for j in range(S):
                    out = m.banks[:, 7, j * D:(j + 1) * D]
                    for i, (hb, c) in enumerate(steps):
                        for a in range(2 - c):
                            last = pe.matmul(out, ht[a][:, (j * HB + hb) * P:(j * HB + hb + 1) * P],
                                             w2[c][:, bass.ds(e, 1), hb, :],
                                             start=(i == 0 and a == 0), stop=(i == len(steps) - 1 and not v.lin_bias))
                    if v.lin_bias:
                        last = pe.matmul(out, m.ones_r[0:2, :], k.b2[:, bass.ds(e, 1), :], start=False, stop=True)
                last.then_inc(down_done, 1)

        schedule(pe, PE())

    @block.scalar
    def _(act):
        class Act(Work):
            def turn_x(self, g, z, half):
                act.wait_ge(xt_in_psum, g + 1)
                at_least(act, lin_done, g)
                act.activation(xt_hi[:], m.banks[:, 6, :], ACT.Copy).then_inc(xth, 1)

            def up(self, g, z):
                act.wait_ge(glu_done, g + 1)
                at_least(act, s1_done, g)
                act.activation(th[:], glu(z), ACT.Tanh, scale=v.slope / 2).then_inc(th_done, 1)

            def turn_h(self, g):
                act.wait_ge(ht_in_psum, g + 1)
                at_least(act, down_done, g)
                act.activation(ht_hi[:], h_turned, ACT.Copy, scale=0.5).then_inc(hth, 1)

            def down(self, g, z, half):
                act.wait_ge(down_done, g + 1)
                if not (isinstance(g, int) and g < 2):
                    act.wait_ge(stored[z], 16 * half)
                act.activation(yout[:, z, :, :].rearrange("p j d -> p (j d)"), m.banks[:, 7, :], ACT.Copy).then_inc(y_done, 1)

        act.preload_act_table(ACT.Tanh)
        schedule(act, Act())

    @block.vector
    def _(dve):
        class Dve(Work):
            def turn_x(self, g, z, half):
                dve.wait_ge(xth, g + 1)
                at_least(dve, lin_done, g)
                dve.tensor_tensor(xt_lo[:], m.banks[:, 6, :], f32(xt_hi[:]), ALU.subtract).then_inc(xtl, 1)

            def up(self, g, z):
                dve.wait_ge(th_done, g + 1)
                at_least(dve, h_done, g)
                dve.scalar_tensor_tensor(out=s1[:], in0=th[:], scalar=1.0, in1=glu(z), op0=ALU.add,
                                         op1=ALU.mult).then_inc(s1_done, 1)
                dve.wait_ge(s1_done, g + 1)
                dve.wait_ge(lin_done, g + 1)
                at_least(dve, ht_in_psum, g)
                dve.scalar_tensor_tensor(out=h[:], in0=lin(z), scalar=float(v.lin_bias), in1=s1[:], op0=ALU.add,
                                         op1=ALU.mult).then_inc(h_done, 1)

            def turn_h(self, g):
                dve.wait_ge(hth, g + 1)
                at_least(dve, down_done, g)
                dve.scalar_tensor_tensor(out=ht_lo[:], in0=h_turned, scalar=0.5, in1=f32(ht_hi[:]), op0=ALU.mult,
                                         op1=ALU.subtract).then_inc(htl, 1)

        schedule(dve, Dve())


def combine_phase(nc, m, A, v, k, ctx, out=None):
    sb = lambda name, shape, dt=F32: ctx.enter_context(nc.sbuf_tensor(f"{v.tag}c_{name}", shape, dt))
    sem = lambda name: nc.alloc_semaphore(f"{v.tag}c_{name}")
    U32 = mybir.dt.uint32
    index, taken = sb("index", [P, 2, 2], U32), sb("taken", [P, 2])
    y = sb("y", [P, 2, 2, D])
    gathered = [[sem(f"gathered{z}{c}") for c in range(2)] for z in range(2)]
    index_done, one_added, both_added, stored, bn_done, aggr_done, eps_done, rstd_done = (
        sem(n) for n in "index_done one_added both_added stored bn_done aggr_done eps_done rstd_done".split())
    block = ctx.enter_context(nc.Block())

    @block.gpsimd
    def _(pool):
        def tile(t, z, half):
            at_least(pool, both_added, t - 1)
            for c in range(2):
                pool.tensor_copy(index[:, z, c:c + 1], k.pos[:, c, bass.ds(t, 1)]).then_inc(index_done, 1)
            pool.wait_ge(index_done, 2 * t + 2)
            pool.tensor_tensor(taken[:, z:z + 1], m.neg_row[:], m.neg_row[:], ALU.add)
            for c in range(2):
                pool.indirect_dma_start(y[:, z, c, :], None, k.y_dram,
                                        bass.IndirectOffsetOnAxis(ap=index[:, z, c:c + 1], axis=0)).then_inc(gathered[z][c], 16)
        tile(0, 0, 0)
        with pool.Fori(0, (NT - 2) // 2) as i:
            tile(2 * i + 1, 1, i)
            tile(2 * i + 2, 0, i + 1)
        tile(NT - 1, 1, NT // 2 - 1)
        if out is None:
            pool.wait_ge(eps_done, 1)
            pool.tensor_tensor(m.rstd[:], m.var_eps[:], m.neg_half[:, 0:NT], ALU.pow).then_inc(rstd_done, 1)

    @block.vector
    def _(dve):
        with dve.Fori(0, NT // 2) as i:
            for z in range(2):
                t = 2 * i + z
                at = bass.ds(t, 1)
                x_t = m.x_res[:, at, :].rearrange("p a d -> p (a d)")
                dve.wait_ge(gathered[z][0], 16 * i + 16)
                dve.scalar_tensor_tensor(out=x_t, in0=y[:, z, 0, :], scalar=k.weight[:, 0, at], in1=x_t,
                                         op0=ALU.mult, op1=ALU.add).then_inc(one_added, 1)
                dve.wait_ge(one_added, t + 1)
                dve.wait_ge(gathered[z][1], 16 * i + 16)
                dve.scalar_tensor_tensor(out=x_t, in0=y[:, z, 1, :], scalar=k.weight[:, 1, at], in1=x_t,
                                         op0=ALU.mult, op1=ALU.add).then_inc(both_added, 1)
                if out is None:
                    dve.wait_ge(both_added, t + 1)
                    dve.bn_stats(m.bn6[:, at, :].rearrange("p a c -> p (a c)"), x_t).then_inc(bn_done, 1)
        if out is None:
            dve.wait_ge(bn_done, NT)
            aggregate(dve, m, aggr_done)
            dve.tensor_scalar(m.var_eps[:], m.mv[:, :, 1], LN_EPS, None, ALU.add).then_inc(eps_done, 1)

    @block.sync
    def _(sp):
        if out is not None:
            with sp.Fori(0, NT) as t:
                sp.wait_ge(both_added, t + 1)
                sp.dma_start(out.rearrange("(t p) d -> p t d", p=P)[:, bass.ds(t, 1), :],
                             m.x_res[:, bass.ds(t, 1), :]).then_inc(stored, 16)
            sp.wait_ge(stored, 16 * NT)


def rwkv_phase(nc, m, A, ctx):
    EB = KB
    sb = lambda name, shape, dt=F32: ctx.enter_context(nc.sbuf_tensor("r_" + name, shape, dt))
    sem = lambda name: nc.alloc_semaphore("r_" + name)
    w_stage, w_mixed = sb("w_stage", [P, 4, KB, D]), sb("w_mixed", [P, 3, 2, KB, D])
    w_hi, w_lo = sb("w_hi", [P, 3, 2, KB, D], F32R), sb("w_lo", [P, 3, 2, KB, D], F32R)
    wo_hi, wo_lo = sb("wo_hi", [P, KB, D], F32R), sb("wo_lo", [P, KB, D], F32R)
    tm, tm_less = sb("tm", [P, 3, KB]), sb("tm_less", [P, 3, KB])
    decay, first, gain, shift = (sb(n, [P, EB]) for n in ("decay", "first", "gain", "shift"))
    grown = sb("grown", [P, EB])
    mean_of = sb("mean_of", [P, P])
    xn = sb("xn", [P, S, D])
    xt_hi, xt_lo = sb("xt_hi", [P, 2, KB, T + 1], F32R), sb("xt_lo", [P, 2, KB, T + 1], F32R)
    ks, vs, th = (sb(n, [P, 2, EB, T]) for n in ("k", "v", "th"))
    top, aa, bb = (sb(n, [P, EB, T + 1]) for n in ("top", "aa", "bb"))
    less, ex = sb("less", [P, 4, EB, T]), sb("ex", [P, 4, EB, T])
    dif, f2v, e2v, e1a, num, den, rden, wkv, c, sq, lnv, rw = (
        sb(n, [P, EB, T]) for n in ("dif", "f2v", "e2v", "e1a", "num", "den", "rden", "wkv", "c", "sq", "lnv", "rw"))
    ve, rstd = sb("ve", [P, S]), sb("rstd", [P, S])
    rw_hi, rw_lo = sb("rw_hi", [P, EB, T], F32R), sb("rw_lo", [P, EB, T], F32R)
    names = ("loaded exp_decay half mixed whi wlo edges xn_ready xt_in_psum xth xtl kvr_done evac top_done dif_done "
             "less_done exp_done f2v_done e2v_done aa_done bb_done e1a_done num_done e1b_done den_done rden_done wkv_done "
             "mean_done c_done sq_done var_done ve_done rstd_done t_done ln_done rw_done rwh rwl out_done x_done "
             "bn_done aggr_done eps_done next_rstd prep spread")
    done = {n: sem(n) for n in names.split()}
    NEVER = -1e38

    def schedule(eng, w):
        def slot(b, z, first=False, last=False):
            if not last:
                w.turn(b + 1, 1 - z)
            if not first:
                w.centre(b - 1)
            w.scores(b, z)
            if not last:
                w.second_x(b + 1, 1 - z)
            if not first:
                w.vary(b - 1)
            if not last:
                w.products(b + 1, 1 - z, (0, 1))
            w.weigh(b, z)
            if not first:
                w.epsilon(b - 1)
                w.spread(b - 1)
            if not last:
                w.products(b + 1, 1 - z, (2,))
            w.divide(b)
            if not first:
                w.norm(b - 1, 1 - z)
            w.ratio(b)
            if not isinstance(b, int) or b >= 2:
                w.add(b - 2)
            if not first:
                w.second_rw(b - 1)
            w.mean(b)
            if not first:
                w.out(b - 1)
        w.turn(0, 0)
        w.second_x(0, 0)
        w.products(0, 0, (0, 1, 2))
        slot(0, 0, first=True)
        slot(1, 1)
        with eng.Fori(0, (B - 4) // 2) as i:
            slot(2 * i + 2, 0)
            slot(2 * i + 3, 1)
        slot(B - 2, 0)
        slot(B - 1, 1, last=True)
        w.add(B - 2)
        w.centre(B - 1)
        w.vary(B - 1)
        w.epsilon(B - 1)
        w.spread(B - 1)
        w.norm(B - 1, 1)
        w.second_rw(B - 1)
        w.out(B - 1)
        w.add(B - 1)

    class Work:
        def add(self, b): pass
        def second_x(self, b, z): pass
        def second_rw(self, b): pass
        def ratio(self, b): pass
        def epsilon(self, b): pass
        def spread(self, b): pass
        def divide(self, b): pass
        def scores(self, b, z): pass
        def centre(self, b): pass
        def turn(self, b, z): pass
        def vary(self, b): pass
        def weigh(self, b, z): pass
        def norm(self, b, z): pass
        def products(self, b, z, kinds): pass
        def mean(self, b): pass
        def out(self, b): pass

    flat = lambda t: t.rearrange("p e t -> p (e t)")
    block = ctx.enter_context(nc.Block())

    @block.sync
    def _(sp):
        for i, n in enumerate("kvro"):
            sp.dma_start(w_stage[:, i], A[f"W{n}T"].rearrange("(k p) n -> p k n", p=P)).then_inc(done["loaded"], 16)
        for i, n in enumerate("kvr"):
            sp.dma_start(tm[:, i, :], A[f"tm_{n}"].rearrange("(k p) -> p k", p=P),
                         allow_slow_non_contiguous=True).then_inc(done["loaded"], 16)
        for t, n in ((decay, "time_decay"), (first, "time_first"), (gain, "ln_g"), (shift, "ln_b")):
            sp.dma_start(t[:], A[n].rearrange("(k p) -> p k", p=P), allow_slow_non_contiguous=True).then_inc(done["loaded"], 16)

    @block.tensor
    def _(pe):
        class PE(Work):
            def turn(self, b, z):
                pe.wait_ge(done["xn_ready"], b + 1)
                at_least(pe, done["xth"], b)
                at_least(pe, done["xtl"], b)
                for kb in range(KB):
                    for s in range(S):
                        last = pe.transpose(m.banks[:, 0, (kb * S + s) * P:(kb * S + s + 1) * P],
                                            xn[:, s, kb * P:(kb + 1) * P], m.ident[:])
                last.then_inc(done["xt_in_psum"], 1)

            def products(self, b, z, kinds):
                pe.wait_ge(done["xth"], b + 1)
                pe.wait_ge(done["xtl"], b + 1)
                at_least(pe, done["evac"], 3 * b)
                xt, w = (xt_hi, xt_lo), (w_hi, w_lo)
                for kind in kinds:
                    for eb in range(EB):
                        last = split_product(
                            pe, m.banks[:, 1 + kind, eb * T:(eb + 1) * T],
                            lambda a, j: w[a][:, kind, j // KB, j % KB, eb * P:(eb + 1) * P],
                            lambda a, j: xt[a][:, z, j % KB, 1 - j // KB:T + 1 - j // KB], 2 * KB)
                    last.then_inc(done["kvr_done"], 1)

            def mean(self, b):
                pe.wait_ge(done["wkv_done"], b + 1)
                at_least(pe, done["c_done"], b)
                for eb in range(EB):
                    last = pe.matmul(m.banks[:, 4, 0:T], mean_of[:], wkv[:, eb, :], start=(eb == 0), stop=(eb == EB - 1))
                last.then_inc(done["mean_done"], 1)

            def vary(self, b):
                pe.wait_ge(done["sq_done"], b + 1)
                at_least(pe, done["ve_done"], b)
                for s in range(S):
                    for eb in range(EB):
                        last = pe.matmul(m.banks[:, 5, s:s + 1], sq[:, eb, s * P:(s + 1) * P], mean_of[:, 0:1],
                                         start=(eb == 0), stop=(eb == EB - 1))
                last.then_inc(done["var_done"], 1)

            def spread(self, b):
                pe.wait_ge(done["rstd_done"], b + 1)
                at_least(pe, done["t_done"], b)
                for s in range(S):
                    last = pe.matmul(m.banks[:, 7, s * P:(s + 1) * P], rstd[:, s:s + 1].broadcast_to([P, P]), m.ident[:],
                                     start=True, stop=True)
                last.then_inc(done["spread"], 1)

            def out(self, b):
                pe.wait_ge(done["rwh"], b + 1)
                pe.wait_ge(done["rwl"], b + 1)
                at_least(pe, done["x_done"], b)
                r, w = (rw_hi, rw_lo), (wo_hi, wo_lo)
                for s in range(S):
                    last = split_product(pe, m.banks[:, 6, s * D:(s + 1) * D],
                                         lambda a, kb: r[a][:, kb, s * P:(s + 1) * P],
                                         lambda a, kb: w[a][:, kb, :], EB)
                last.then_inc(done["out_done"], 1)

        pe.wait_ge(done["wlo"], 2)
        schedule(pe, PE())

    @block.scalar
    def _(act):
        class Act(Work):
            def turn(self, b, z):
                act.wait_ge(done["xt_in_psum"], b + 1)
                at_least(act, done["kvr_done"], 3 * (b - 1))
                act.activation(xt_hi[:, z, :, 1:T + 1], m.banks[:, 0, :].rearrange("p (k t) -> p k t", k=KB),
                               ACT.Copy).then_inc(done["xth"], 1)

            def products(self, b, z, kinds):
                at_least(act, done["wkv_done"], b - 1)
                at_least(act, done["rw_done"], b - 1)
                for kind in kinds:
                    to, func, scale = ((ks, ACT.Copy, 1.0), (vs, ACT.Copy, 1.0), (th, ACT.Tanh, 0.5))[kind]
                    act.wait_ge(done["kvr_done"], 3 * b + kind + 1)
                    act.activation(flat(to[:, z]), m.banks[:, 1 + kind, :], func, scale=scale).then_inc(done["evac"], 1)

            def scores(self, b, z):
                act.wait_ge(done["less_done"], b + 1)
                at_least(act, done["wkv_done"], b)
                act.activation(ex[:], less[:], ACT.Exp).then_inc(done["exp_done"], 1)

            def centre(self, b):
                act.wait_ge(done["c_done"], b + 1)
                at_least(act, done["var_done"], b)
                act.activation(sq[:], c[:], ACT.Square).then_inc(done["sq_done"], 1)

            def norm(self, b, z):
                act.wait_ge(done["rw_done"], b + 1)
                at_least(act, done["out_done"], b)
                act.activation(rw_hi[:], rw[:], ACT.Copy).then_inc(done["rwh"], 1)

        act.preload_act_table(ACT.Exp)
        act.wait_ge(done["loaded"], 16 * 11)
        act.activation(grown[:], decay[:], ACT.Exp).then_inc(done["exp_decay"], 1)
        act.wait_ge(done["mixed"], 6)
        act.activation(w_hi[:], w_mixed[:], ACT.Copy)
        act.activation(wo_hi[:], w_stage[:, 3], ACT.Copy).then_inc(done["whi"], 1)
        schedule(act, Act())

    @block.vector
    def _(dve):
        class Dve(Work):
            def turn(self, b, z):
                at_least(dve, done["xt_in_psum"], b)
                for s in range(S):
                    at = bass.ds(S * b + s, 1)
                    last = dve.tensor_scalar(xn[:, s:s + 1, :], m.x_res[:, at, :], m.mv[:, at, 0],
                                             m.rstd[:, at], ALU.subtract, ALU.mult)
                last.then_inc(done["xn_ready"], 1)

            def second_x(self, b, z):
                dve.wait_ge(done["xth"], b + 1)
                at_least(dve, done["kvr_done"], 3 * (b - 1))
                dve.tensor_tensor(xt_lo[:, z, :, 1:T + 1], m.banks[:, 0, :].rearrange("p (k t) -> p k t", k=KB),
                                  f32(xt_hi[:, z, :, 1:T + 1]), ALU.subtract).then_inc(done["xtl"], 1)

            def scores(self, b, z):
                dve.wait_ge(done["evac"], 3 * b + 3)
                at_least(dve, done["less_done"], b)
                for eb in range(EB):
                    last = dve.tensor_tensor_scan(top[:, eb, 1:T + 1], grown[:, eb:eb + 1].broadcast_to([P, T]),
                                                  ks[:, z, eb, :], NEVER, ALU.add, ALU.max)
                last.then_inc(done["top_done"], 1)
                dve.wait_ge(done["top_done"], b + 1)
                for eb in range(EB):
                    last = dve.scalar_tensor_tensor(out=dif[:, eb, :], in0=ks[:, z, eb, :], scalar=first[:, eb:eb + 1],
                                                    in1=top[:, eb, 0:T], op0=ALU.add, op1=ALU.subtract)
                last.then_inc(done["dif_done"], 1)
                at_least(dve, done["exp_done"], b)
                dve.tensor_tensor(less[:, 2], top[:, :, 0:T], top[:, :, 1:T + 1], ALU.subtract)
                dve.tensor_tensor(less[:, 3], ks[:, z], top[:, :, 1:T + 1], ALU.subtract)
                dve.wait_ge(done["dif_done"], b + 1)
                dve.tensor_scalar(less[:, 0], dif[:], 0.0, None, ALU.min)
                dve.tensor_scalar(less[:, 1], dif[:], -1.0, 0.0, ALU.mult, ALU.min).then_inc(done["less_done"], 1)

            def weigh(self, b, z):
                def then(ins, name):
                    ins.then_inc(done[name], 1)
                    dve.wait_ge(done[name], b + 1)

                dve.wait_ge(done["exp_done"], b + 1)
                then(dve.tensor_tensor(f2v[:], ex[:, 3], vs[:, z], ALU.mult), "f2v_done")
                for eb in range(EB):
                    last = dve.tensor_tensor_scan(aa[:, eb, 1:T + 1], ex[:, 2, eb, :], f2v[:, eb, :], 0.0, ALU.mult, ALU.add)
                last.then_inc(done["aa_done"], 1)
                for eb in range(EB):
                    last = dve.tensor_tensor_scan(bb[:, eb, 1:T + 1], ex[:, 2, eb, :], ex[:, 3, eb, :], 0.0, ALU.mult, ALU.add)
                last.then_inc(done["bb_done"], 1)

            def divide(self, b):
                def then(ins, name):
                    ins.then_inc(done[name], 1)
                    dve.wait_ge(done[name], b + 1)

                dve.wait_ge(done["bb_done"], b + 1)
                then(dve.tensor_tensor(den[:], ex[:, 1], bb[:, :, 0:T], ALU.mult), "e1b_done")
                then(dve.tensor_tensor(den[:], den[:], ex[:, 0], ALU.add), "den_done")
                then(dve.reciprocal(rden[:], den[:]), "rden_done")

            def ratio(self, b):
                dve.wait_ge(done["num_done"], b + 1)
                at_least(dve, done["mean_done"], b)
                dve.tensor_tensor(wkv[:], num[:], rden[:], ALU.mult).then_inc(done["wkv_done"], 1)

            def centre(self, b):
                dve.wait_ge(done["mean_done"], b + 1)
                at_least(dve, done["sq_done"], b)
                dve.tensor_tensor(c[:], wkv[:], m.banks[:, 4, 0:T].unsqueeze(1).broadcast_to([P, EB, T]),
                                  ALU.subtract).then_inc(done["c_done"], 1)

            def epsilon(self, b):
                dve.wait_ge(done["var_done"], b + 1)
                at_least(dve, done["rstd_done"], b)
                dve.tensor_scalar(ve[:], m.banks[:, 5, 0:S], LN_EPS, None, ALU.add).then_inc(done["ve_done"], 1)

            def norm(self, b, z):
                dve.wait_ge(done["spread"], b + 1)
                dve.tensor_tensor(lnv[:], c[:], m.banks[:, 7, 0:T].unsqueeze(1).broadcast_to([P, EB, T]), ALU.mult).then_inc(done["t_done"], 1)
                dve.wait_ge(done["t_done"], b + 1)
                for eb in range(EB):
                    last = dve.tensor_scalar(lnv[:, eb, :], lnv[:, eb, :], gain[:, eb:eb + 1], shift[:, eb:eb + 1],
                                             ALU.mult, ALU.add)
                last.then_inc(done["ln_done"], 1)
                dve.wait_ge(done["ln_done"], b + 1)
                at_least(dve, done["rwh"], b)
                dve.scalar_tensor_tensor(out=flat(rw[:]), in0=flat(th[:, z]), scalar=1.0, in1=flat(lnv[:]),
                                         op0=ALU.add, op1=ALU.mult).then_inc(done["rw_done"], 1)

            def second_rw(self, b):
                dve.wait_ge(done["rwh"], b + 1)
                at_least(dve, done["out_done"], b)
                dve.tensor_tensor(rw_lo[:], rw[:], f32(rw_hi[:]), ALU.subtract).then_inc(done["rwl"], 1)

            def add(self, b):
                dve.wait_ge(done["out_done"], b + 1)
                two = m.x_res[:, bass.ds(S * b, S), :]
                dve.tensor_tensor(two, two, m.banks[:, 6, :].rearrange("p (s c) -> p s c", s=S), ALU.add).then_inc(done["x_done"], 1)
                dve.wait_ge(done["x_done"], b + 1)
                for s in range(S):
                    at = bass.ds(S * b + s, 1)
                    last = dve.bn_stats(m.bn6[:, at, :].rearrange("p a c -> p (a c)"),
                                        m.x_res[:, at, :].rearrange("p a c -> p (a c)"))
                last.then_inc(done["bn_done"], 1)

        dve.wait_ge(done["loaded"], 16 * 11)
        dve.tensor_scalar(tm_less[:], tm[:], -1.0, 1.0, ALU.mult, ALU.add).then_inc(done["prep"], 1)
        dve.tensor_scalar(gain[:], gain[:], 0.5, None, ALU.mult)
        dve.tensor_scalar(shift[:], shift[:], 0.5, None, ALU.mult).then_inc(done["prep"], 1)
        dve.wait_ge(done["exp_decay"], 1)
        dve.wait_ge(done["prep"], 2)
        dve.tensor_scalar(grown[:], grown[:], -1.0, None, ALU.mult).then_inc(done["prep"], 1)
        for kind in range(3):
            for kb in range(KB):
                dve.tensor_scalar(w_mixed[:, kind, 0, kb, :], w_stage[:, kind, kb, :], tm[:, kind, kb:kb + 1], None, ALU.mult)
                dve.tensor_scalar(w_mixed[:, kind, 1, kb, :], w_stage[:, kind, kb, :], tm_less[:, kind, kb:kb + 1], None,
                                  ALU.mult).then_inc(done["mixed"], 1)
        dve.wait_ge(done["whi"], 1)
        dve.tensor_tensor(w_lo[:], w_mixed[:], f32(w_hi[:]), ALU.subtract).then_inc(done["wlo"], 1)
        dve.tensor_tensor(wo_lo[:], w_stage[:, 3], f32(wo_hi[:]), ALU.subtract).then_inc(done["wlo"], 1)
        dve.wait_ge(done["edges"], 1)
        schedule(dve, Dve())
        dve.wait_ge(done["bn_done"], B)
        aggregate(dve, m, done["aggr_done"])
        dve.tensor_scalar(m.var_eps[:], m.mv[:, :, 1], LN_EPS, None, ALU.add).then_inc(done["eps_done"], 1)

    @block.gpsimd
    def _(pool):
        class Pool(Work):
            def vary(self, b):
                pool.wait_ge(done["ve_done"], b + 1)
                at_least(pool, done["spread"], b)
                pool.tensor_tensor(rstd[:], ve[:], m.neg_half[:, 0:S], ALU.pow).then_inc(done["rstd_done"], 1)

            def weigh(self, b, z):
                pool.wait_ge(done["exp_done"], b + 1)
                pool.wait_ge(done["evac"], 3 * b + 3)
                pool.tensor_tensor(e2v[:], ex[:, 0], vs[:, z], ALU.mult).then_inc(done["e2v_done"], 1)
                pool.wait_ge(done["aa_done"], b + 1)
                pool.tensor_tensor(e1a[:], ex[:, 1], aa[:, :, 0:T], ALU.mult).then_inc(done["e1a_done"], 1)
                pool.wait_ge(done["e1a_done"], b + 1)
                pool.wait_ge(done["e2v_done"], b + 1)
                at_least(pool, done["wkv_done"], b)
                pool.tensor_tensor(num[:], e1a[:], e2v[:], ALU.add).then_inc(done["num_done"], 1)

        for part in (xt_hi, xt_lo):
            pool.memset(f32(part[:, :, :, 0]), 0.0)
        pool.memset(top[:, :, 0], NEVER)
        pool.memset(aa[:, :, 0], 0.0)
        pool.memset(mean_of[:], 1.0 / D)
        pool.memset(bb[:, :, 0], 0.0).then_inc(done["edges"], 1)
        pool.wait_ge(done["edges"], 1)
        schedule(pool, Pool())
        pool.wait_ge(done["eps_done"], 1)
        pool.tensor_tensor(m.rstd[:], m.var_eps[:], m.neg_half[:, 0:NT], ALU.pow).then_inc(done["next_rstd"], 1)


def build_program(nc, A, out):
    with ExitStack() as ctx:
        m = shared_memory(nc, ctx)
        with phase(nc) as scope:
            setup_phase(nc, m, A, scope)
        with phase(nc) as scope:
            attention_phase(nc, m, A, scope)
        mixture_layer(nc, m, {name[3:]: ap for name, ap in A.items() if name.startswith("f0_")},
                      Mixture("f0", 4, 512, "all", True, 1.0, 0))
        with phase(nc) as scope:
            rwkv_phase(nc, m, A, scope)
        mixture_layer(nc, m, {name[3:]: ap for name, ap in A.items() if name.startswith("f1_")},
                      Mixture("f1", 8, 256, "two", False, 1.702, 1), out)


@contextmanager
def phase(nc):
    before = nc.snapshot_sems()
    with ExitStack() as scope:
        yield scope
    nc.clear_and_free_semaphores(nc.allocated_since(before))
    nc.all_engine_barrier()


def mixture_layer(nc, m, A, v, out=None):
    with ExitStack() as layer:
        k = mixture_memory(nc, v, layer)
        with phase(nc) as scope:
            router_phase(nc, m, A, v, k, scope)
        with phase(nc) as scope:
            rank_phase(nc, m, v, k, scope)
        with phase(nc) as scope:
            expert_phase(nc, m, v, k, scope)
        with phase(nc) as scope:
            combine_phase(nc, m, A, v, k, scope, out)


def laid_out(inputs):
    i = {name: np.asarray(a) for name, a in inputs.items()}
    turned = lambda a: np.swapaxes(a, -1, -2)
    halves = lambda a: np.concatenate([a[:, 0::2], a[:, 1::2]], axis=1)
    a = {
        "L0_attn_x": i["L0_attn_x"].reshape(TOK, D),
        "L0_attn_W": i["L0_attn_W"], "L0_attn_WT": turned(i["L0_attn_W"]),
        "L0_attn_g1": i["L0_attn_g1"], "L0_attn_g2": i["L0_attn_g2"], "L0_attn_g3": i["L0_attn_g3"],
        "f0_gateT": turned(i["L0_ffn_gate_w"]),
        "f0_w13T": turned(np.concatenate([i["L0_ffn_w1"], i["L0_ffn_w3"]], axis=1)),
        "f0_w2T": turned(i["L0_ffn_w2"]),
        "f0_s13T": turned(np.concatenate([i["L0_ffn_sw1"], i["L0_ffn_sw3"]], axis=0)),
        "f0_s2T": turned(i["L0_ffn_sw2"]),
        "f1_gateT": turned(i["L1_ffn_gate_w"]), "f1_gate_b": i["L1_ffn_gate_b"],
        "f1_w13T": turned(halves(i["L1_ffn_w1"])), "f1_w2T": turned(i["L1_ffn_w2"]),
        "f1_b1": halves(i["L1_ffn_b1"]), "f1_b2": i["L1_ffn_b2"],
    }
    for n in "kvro":
        a[f"W{n}T"] = turned(i[f"L1_attn_W{n}"])
    for n in ("tm_k", "tm_v", "tm_r", "time_decay", "time_first", "ln_g", "ln_b"):
        a[n] = i[f"L1_attn_{n}"].reshape(D)
    return {name: np.ascontiguousarray(v) for name, v in a.items()}


def kernel(**inputs):
    import concourse.bacc as bacc
    from concourse.bass_utils import run_bass_kernel_spmd

    arrays = {f"in_{name}": a for name, a in laid_out(inputs).items()}
    nc = bacc.Bacc("TRN2", target_bir_lowering=False, num_devices=1)
    A = {name[3:]: nc.dram_tensor(name, a.shape, mybir.dt.from_np(a.dtype), kind="ExternalInput").ap()
         for name, a in arrays.items()}
    out = nc.dram_tensor("out_x", (TOK, D), F32, kind="ExternalOutput").ap()
    build_program(nc, A, out)
    result = run_bass_kernel_spmd(nc, [arrays], core_ids=[0])
    return result.results[0]["out_x"].reshape(B, T, D)
```
